# Optimizing a Trainium2 kernel written in Bass

```python
import numpy as np
import jax
import jax.numpy as jnp

def _softmax(x, axis=-1):
    return jax.nn.softmax(x, axis=axis)

def _gelu(x):
    return jax.nn.gelu(x, approximate=True)

def _silu(x):
    return jax.nn.silu(x)

def _sigmoid(x):
    return jax.nn.sigmoid(x)

def _layernorm(x, axis=-1, eps=1e-05):
    m = jnp.mean(x, axis=axis, keepdims=True)
    v = jnp.var(x, axis=axis, keepdims=True)
    return (x - m) / jnp.sqrt(v + eps)

def _scatter_add(tgt, idx, src, axis=0):
    return tgt.at[idx].add(src)

def _segment_sum(src, seg, n):
    return jax.ops.segment_sum(src, seg, n)
kernel_name = 'mk_gnn_ffn_d1_gnn_r8_61d928'

def setup_inputs(seed: int=0):
    np.random.seed(seed)
    _w = jnp.asarray

    def _rec_inputs():
        import jax
        import jax.numpy as jnp
        _gk = jax.random.key(seed)
        x = -0.0003713 + 1 * jax.random.normal(jax.random.fold_in(_gk, 1), (6250, 256), jnp.float32)
        src = jax.random.randint(jax.random.fold_in(_gk, 2), (200000,), 0, 6250, jnp.int32)
        dst = jax.random.randint(jax.random.fold_in(_gk, 3), (200000,), 0, 6250, jnp.int32)
        _o = jnp.argsort(dst, stable=True)
        src = src[_o]
        dst = dst[_o]
        return (x, src, dst)
    x, src, dst = _rec_inputs()

    def _L0_gnn_setup():
        import jax, jax.numpy as jnp
        import numpy as np
        N_NODES = 6250
        N_EDGES = 200000
        IN_FEATS = 256
        HIDDEN = 512
        OUT_FEATS = 256
        EPS = 0.0
        key = jax.random.key(seed)
        ks = jax.random.split(key, 6)
        x = jax.random.normal(ks[0], (N_NODES, IN_FEATS), dtype=jnp.float32)
        edge_row = jax.random.randint(ks[1], (N_EDGES,), 0, N_NODES, dtype=jnp.int32)
        edge_col = jax.random.randint(ks[2], (N_EDGES,), 0, N_NODES, dtype=jnp.int32)
        W1 = jax.random.uniform(ks[3], (IN_FEATS, HIDDEN), dtype=jnp.float32, minval=-1.0 / np.sqrt(IN_FEATS), maxval=1.0 / np.sqrt(IN_FEATS))
        b1 = jnp.zeros((HIDDEN,), dtype=jnp.float32)
        W2 = jax.random.uniform(ks[4], (HIDDEN, OUT_FEATS), dtype=jnp.float32, minval=-1.0 / np.sqrt(HIDDEN), maxval=1.0 / np.sqrt(HIDDEN))
        b2 = jnp.zeros((OUT_FEATS,), dtype=jnp.float32)
        return {'x': x, 'edge_row': edge_row, 'edge_col': edge_col, 'W1': W1, 'b1': b1, 'W2': W2, 'b2': b2}
    _L0_gnn_all = _L0_gnn_setup()
    _L0_gnn_in = {k: v for k, v in _L0_gnn_all.items() if k in ('W1', 'b1', 'W2', 'b2')}
    del _L0_gnn_all

    def _L0_ffn_setup():
        import jax, jax.numpy as jnp
        import numpy as np
        B, S, H, F, E, K = (8, 512, 256, 512, 16, 2)
        EPS = 1e-05
        key = jax.random.key(seed)
        ks = jax.random.split(key, 9)
        sc = 0.02
        return {'x': jax.random.normal(ks[0], (B, S, H), dtype=jnp.float32), 'gate_w': jax.random.normal(ks[1], (H, E), dtype=jnp.float32) * sc, 'gate_b': jnp.zeros((E,), dtype=jnp.float32), 'w1': jax.random.normal(ks[2], (E, H, F), dtype=jnp.float32) * sc, 'b1': jnp.zeros((E, F), dtype=jnp.float32), 'w2': jax.random.normal(ks[3], (E, F, H), dtype=jnp.float32) * sc, 'b2': jnp.zeros((E, H), dtype=jnp.float32), 'gamma': jnp.ones((H,), dtype=jnp.float32), 'beta': jnp.zeros((H,), dtype=jnp.float32)}
    _L0_ffn_all = _L0_ffn_setup()
    _L0_ffn_in = {k: v for k, v in _L0_ffn_all.items() if k in ('gate_w', 'gate_b', 'w1', 'b1', 'w2', 'b2', 'gamma', 'beta')}
    del _L0_ffn_all
    return {'x': x, 'src': src, 'dst': dst, 'L0_gnn_W1': _L0_gnn_in['W1'], 'L0_gnn_b1': _L0_gnn_in['b1'], 'L0_gnn_W2': _L0_gnn_in['W2'], 'L0_gnn_b2': _L0_gnn_in['b2'], 'L0_ffn_gate_w': _L0_ffn_in['gate_w'], 'L0_ffn_gate_b': _L0_ffn_in['gate_b'], 'L0_ffn_w1': _L0_ffn_in['w1'], 'L0_ffn_b1': _L0_ffn_in['b1'], 'L0_ffn_w2': _L0_ffn_in['w2'], 'L0_ffn_b2': _L0_ffn_in['b2'], 'L0_ffn_gamma': _L0_ffn_in['gamma'], 'L0_ffn_beta': _L0_ffn_in['beta']}

def reference(x, src, dst, L0_gnn_W1, L0_gnn_b1, L0_gnn_W2, L0_gnn_b2, L0_ffn_gate_w, L0_ffn_gate_b, L0_ffn_w1, L0_ffn_b1, L0_ffn_w2, L0_ffn_b2, L0_ffn_gamma, L0_ffn_beta):
    import jax
    import jax.numpy as jnp

    def _L0_gnn_ref(x, edge_row, edge_col, W1, b1, W2, b2):
        import jax, jax.numpy as jnp
        import numpy as np
        N_NODES = 6250
        N_EDGES = 200000
        IN_FEATS = 256
        HIDDEN = 512
        OUT_FEATS = 256
        EPS = 0.0
        agg = jax.ops.segment_sum(x[edge_col], edge_row, num_segments=N_NODES)
        h = agg + (1.0 + EPS) * x
        h = h @ W1 + b1
        out = h @ W2 + b2
        return out

    def _L0_ffn_ref(x, gate_w, gate_b, w1, b1, w2, b2, gamma, beta):
        import jax, jax.numpy as jnp
        import numpy as np
        B, S, H, F, E, K = (8, 512, 256, 512, 16, 2)
        EPS = 1e-05
        gate_logits = x @ gate_w + gate_b
        topk_vals, topk_idx = jax.lax.top_k(gate_logits, K)
        topk_w = jax.nn.softmax(topk_vals, axis=-1)
        h = jax.nn.relu(jnp.einsum('bsh,ehf->bsef', x, w1) + b1)
        expert_out = jnp.einsum('bsef,efh->bseh', h, w2) + b2
        sel = jnp.take_along_axis(expert_out, topk_idx[:, :, :, None], axis=2)
        moe = jnp.sum(topk_w[..., None] * sel, axis=2)
        y = x + moe
        mu = jnp.mean(y, axis=-1, keepdims=True)
        var = jnp.var(y, axis=-1, keepdims=True)
        return (y - mu) / jnp.sqrt(var + EPS) * gamma + beta
    x = x + _L0_gnn_ref(_layernorm(x, axis=-1), src, dst, L0_gnn_W1, L0_gnn_b1, L0_gnn_W2, L0_gnn_b2)
    x = x + _L0_ffn_ref(_layernorm(x, axis=-1)[None], L0_ffn_gate_w, L0_ffn_gate_b, L0_ffn_w1, L0_ffn_b1, L0_ffn_w2, L0_ffn_b2, L0_ffn_gamma, L0_ffn_beta)[0]
    return x

_drawn_inputs = setup_inputs


def setup_inputs(seed=0):
    import zlib

    import numpy as np

    out = dict(_drawn_inputs(seed))
    spreads = {'L0_gnn_b1': (0.0, 0.283),
     'L0_gnn_b2': (0.0, 0.1),
     'L0_ffn_gate_b': (0.0, 0.364),
     'L0_ffn_b1': (0.0, 0.8),
     'L0_ffn_b2': (0.0, 0.343),
     'L0_ffn_gamma': (1.0, 0.2),
     'L0_ffn_beta': (0.0, 0.1)}
    factors = {'L0_ffn_w1': 2.882}
    for name, (base, spread) in spreads.items():
        noise = np.random.default_rng([zlib.crc32(name.encode()), seed]).standard_normal(out[name].shape)
        drawn = base * np.exp(spread * noise) if base else spread * noise
        out[name] = jnp.asarray(drawn.astype(out[name].dtype))
    for name, factor in factors.items():
        out[name] = (out[name] * factor).astype(out[name].dtype)
    return out
```

```python
import concourse.bass as bass
from concourse import mybir
from contextlib import ExitStack


def prog(nc, x, src, dst, W1, b1, W2, b2, gate_w, gate_b, ew1, eb1, ew2, eb2, gamma, beta, out, list_d, off_d, slots_d, eo_d):
    fp32, fp16, i32 = mybir.dt.float32, mybir.dt.float16, mybir.dt.int32
    ALU, ACT, AX = mybir.AluOpType, mybir.ActivationFunctionType, mybir.AxisListType
    DS = bass.ds

    N, F = x.shape
    E = src.shape[0]
    HID = W1.shape[1]
    NP, NT = 125, 50
    BT = 4
    BN = BT * NP
    NS = -(-NT // BT)
    NB = NS * NT
    EC = E // NP
    C = 2048
    LEVELS = 7
    BASE = 128
    SENTINEL = (NB + 50 + BASE) << 16
    K = 3
    WIN = 128 * K
    LAST_START = 128 * C - WIN
    HH, HL = 21, 32
    HP = 400
    PIECES = EC // HP
    UP = 2.0 ** 11
    GU = 10
    OR = 5
    AR = 2
    HJ = 4
    EPS = 1e-5
    X, EH = ew1.shape[0], ew1.shape[2]
    KT = 2 * NT
    NCH = (KT * NP + X * 127) // 128
    HA = EH // 128
    GR = 5
    FH = F // 128

    kept, kept2 = [], []

    ctx = ExitStack()
    with ctx:
        def sb(name, shape, dt):
            return ctx.enter_context(nc.sbuf_tensor(name, shape, dt))

        def sem(name):
            return ctx.enter_context(nc.semaphore(name))

        x_sb = sb("x_sb", [NP, NT, F], fp32)
        xnT = sb("xnT", [128, FH, NS * BN], fp32)
        halves = sb("halves", [128, 2, NT * F], fp16)
        xh = halves[0:NP, 0, :].rearrange("p (t f) -> p t f", t=NT)
        xl = halves[0:NP, 1, :].rearrange("p (t f) -> p t f", t=NT)
        scratch = halves[0:NP, :, :].rearrange("p a n -> p (a n)").bitcast(i32)
        edges = [scratch[:, i * EC:(i + 1) * EC] for i in range(8)]
        srcs, dsts, ta, tb, tc, td, te, tf = edges
        hots = [m[0:NP, :, :].rearrange("p a n -> p (a n)").bitcast(fp16)[:, 0:(HH + HL) * HP]
                for m in (xnT, halves)]
        hot_hi = [h[:, 0:HH * HP].rearrange("p (g v j) -> p g v j", v=HH, j=HJ) for h in hots]
        hot_lo = [h[:, HH * HP:].rearrange("p (v j) -> p v j", j=HP) for h in hots]
        keys = [sb(f"keys{i}", [128, C], fp32) for i in range(2)]
        listed = sb("listed", [128, C, 2], fp32)
        digits = listed[0:NP, :, :].rearrange("p c w -> p (c w)").bitcast(fp16)
        hi16, lo16 = digits[:, 0:EC], digits[:, EC:2 * EC]
        upper = listed[:, 0:C // 4, :].rearrange("p c w -> p (c w)")
        ident = sb("ident", [128, 128], fp32)
        rown = sb("rown", [128, 1], i32)
        bit = sb("bit", [128, 1], i32)
        sign = sb("sign", [128, LEVELS + 1], fp32)
        toggle = sb("toggle", [128, LEVELS + 1], fp32)
        before = sb("before", [128, 128], fp32)
        cube = sb("cube", [HJ * HH, HH, HJ], fp32)
        same = sb("same", [HJ * HH, HJ], fp32)
        fold = sb("fold", [HJ * HH, HH], fp32)
        crossed = sb("crossed", [HJ * HH, HJ, HL], fp32)
        diag = sb("diag", [HJ * HH, HL], fp32)
        stats = sb("stats", [NP, NT, 6], fp32)
        mean = sb("mean", [NP, NT], fp32)
        var = sb("var", [NP, NT], fp32)
        rstd = sb("rstd", [NP, NT], fp32)
        shift = sb("shift", [NP, NT], fp32)
        eps = sb("eps", [128, 1], fp32)
        rows = sb("rows", [128, 2, F], fp32)
        xs = rows[0:NP, :, :]
        hst = rows[:, :, 0:FH * NP].rearrange("p u (a n) -> p u a n", a=FH)
        ohs = (listed[:, :, :].rearrange("p c w -> p (c w)").bitcast(fp16)[:, 0:OR * K * BN]
               .rearrange("p (o k n) -> p o k n", o=OR, k=K))
        small = sb("small", [128, OR * K * 64], fp32)
        ohd = small[:, :].bitcast(fp16).rearrange("p (o k n) -> p o k n", o=OR, k=K)
        zeros = small[:, 0:F]
        atn = sb("atn", [NP, AR, BN], fp16)
        win = sb("win", [128, GU, K, 2], fp32)
        rel = sb("rel", [128, 2, K], fp32)
        firsts = sb("firsts", [128, NB], fp32)
        places = sb("places", [128, BN], fp16)
        wf = sb("wf", [128, FH, F], fp32)
        w1s = keys[0][:, 0:FH * HID].rearrange("p (a n) -> p a n", a=FH)
        w2s = keys[1][:, 0:FH * HID].rearrange("p (a n) -> p a n", a=HID // 128)
        w1T = keys[0][:, FH * HID:2 * FH * HID].rearrange("p (a n) -> p a n", a=HID // 128)
        b1c = sb("b1c", [128, HID // 128], fp32)
        brow = sb("brow", [1, F], fp32)
        b2r = sb("b2r", [1, F], fp32)
        ones = sb("ones", [1, 128], fp32)
        cnt = sb("cnt", [HH, HL], fp32)
        incl = sb("incl", [HH, HL], fp32)
        offf = sb("offf", [HH, HL], fp32)
        offi = sb("offi", [HH, HL], i32)
        most = sb("most", [HH, 1], fp32)
        rnd = sb("rnd", [1, 8], i32)
        offrow = sb("offrow", [1, HH * HL], i32)

        yn = halves[0:NP, :, :].rearrange("p a n -> p (a n)").bitcast(fp32).rearrange("p (t f) -> p t f", t=NT)
        area = xnT[:, :, :].rearrange("p a n -> p (a n)")
        at = [0]

        def carve(n, rows=128):
            at[0] += n
            return area[0:rows, at[0] - n:at[0]]

        wt1 = carve(2 * 1024).rearrange("p (u a n) -> p u a n", u=2, a=FH)
        wt2 = carve(2 * 1024).rearrange("p (u a n) -> p u a n", u=2, a=HA)
        wb2 = carve(2 * F).rearrange("p (u n) -> p u n", u=2)
        xr = carve(2 * F).rearrange("p (u n) -> p u n", u=2)
        xT = carve(2 * F).rearrange("p (u a n) -> p u a n", u=2, a=FH)
        hT = carve(2 * EH).rearrange("p (u a n) -> p u a n", u=2, a=HA)
        eo = carve(2 * F).rearrange("p (u n) -> p u n", u=2)
        got = carve(GR * 2 * F, NP).rearrange("p (g k n) -> p g k n", g=GR, k=2)
        logits = carve(NT * X, NP).rearrange("p (t e) -> p t e", e=X)
        masked = carve(NT * X, NP).rearrange("p (t e) -> p t e", e=X)
        chosen16 = carve(KT * X // 2, NP).bitcast(fp16)
        b1T = carve(X * HA)
        b1r = carve(128, X * HA)
        chosen = keys[0][0:NP, 0:KT * X].rearrange("p (e k) -> p e k", e=X)
        total = keys[1][0:NP, 0:KT * X].rearrange("p (e k) -> p e k", e=X)
        lst = listed[0:NP, :, :].rearrange("p c w -> p (c w)")
        upto = lst[:, 0:KT * X].rearrange("p (e k) -> p e k", e=X)
        place = lst[:, 2048:2048 + KT * X].rearrange("p (e k) -> p e k", e=X)
        gw = sb("gw", [128, FH, X], fp32)
        gb = sb("gb", [NP, X], fp32)
        eix = sb("eix", [NP, X], fp32)
        eix64 = sb("eix64", [NP, X], fp32)
        used = [0]

        def take(*shape, dt=fp32):
            n = shape[0] if len(shape) == 1 else shape[0] * shape[1]
            used[0] += n
            flat = small[0:NP, used[0] - n:used[0]]
            flat = flat if dt is fp32 else flat.bitcast(dt)
            return flat if len(shape) == 1 else flat.rearrange("p (a b) -> p a b", a=shape[0])

        before16 = sb("before16", [NP, NP], fp16)
        ones16 = sb("ones16", [NP, NP], fp16)
        best = take(2, NT)
        which = take(2, NT)
        share = take(2, NT)
        nexp = take(X, dt=i32)
        padded = take(X)
        padend = take(X)
        adjust = take(X)
        posf = take(KT)
        posi = take(KT, dt=i32)
        erow = take(NCH, dt=i32)[0:1, :]
        erowf = take(NCH)[0:1, :]
        gam = carve(F, NP)
        bet = carve(F, NP)
        ynT = hst
        reach = listed[0:1, :, :].rearrange("p c w -> p (c w)")[:, 0:NCH * X].rearrange("p (j e) -> p j e", e=X)
        started = got[0:1, :, :, :].rearrange("p g k n -> p (g k n)")[:, 0:NCH * X].rearrange("p (j e) -> p j e", e=X)

        ps = ctx.enter_context(nc.psum_tensor("ps", [128, 8, 512], fp32))
        psT = ps[:, 0:4, :].rearrange("p a n -> p (a n)")
        psR = ps[:, 4:8, :].rearrange("p a n -> p (a n)")
        psH = ps[0:HJ * HH, 7, 0:HJ * HL]
        psC = ps[0:HH, 4, 0:HL]
        psO = ps[0:HH, 6, 0:1]
        psM = ps[0:1, 5, 0:HH]

        s_src, s_dst = sem("s_src"), sem("s_dst")
        s_const = sem("s_const")
        s_chain = sem("s_chain")
        s_hot = sem("s_hot")
        s_hist = sem("s_hist")
        s_cnt, s_base, s_mx, s_mxT, s_rounds = sem("s_cnt"), sem("s_base"), sem("s_mx"), sem("s_mxT"), sem("s_rounds")
        s_offi, s_offd, s_offrow = sem("s_offi"), sem("s_offd"), sem("s_offrow")
        s_rows, s_signed, s_T, s_Tdone, s_R = sem("s_rows"), sem("s_signed"), sem("s_T"), sem("s_Tdone"), sem("s_R")
        s_Tup, s_Rup = sem("s_Tup"), sem("s_Rup")
        s_listed, s_list, s_out = sem("s_listed"), sem("s_list"), sem("s_out")
        s_x, s_diag, s_folded = sem("s_x"), sem("s_diag"), sem("s_folded")
        s_var, s_std, s_ln = sem("s_var"), sem("s_std"), sem("s_ln")
        s_xs, s_hi, s_lo, s_lnT, s_lnE = sem("s_xs"), sem("s_hi"), sem("s_lo"), sem("s_lnT"), sem("s_lnE")
        s_win = [sem(f"s_win{u}") for u in range(GU)]
        s_winfree, s_rel, s_oh, s_built, s_at, s_main, s_agg = (
            sem(n) for n in ("s_winfree", "s_rel", "s_oh", "s_built", "s_at", "s_main", "s_agg"))
        s_started = sem("s_started")
        s_round, s_offnew, s_tabs = sem("s_round"), sem("s_offnew"), sem("s_tabs")
        s_w, s_w1T, s_w1Te, s_wf, s_wfe = sem("s_w"), sem("s_w1T"), sem("s_w1Te"), sem("s_wf"), sem("s_wfe")
        s_hst, s_lin, s_x1 = sem("s_hst"), sem("s_lin"), sem("s_x1")
        s_zero, s_z, s_gw, s_gam, s_con2 = sem("s_zero"), sem("s_z"), sem("s_gw"), sem("s_gam"), sem("s_con2")
        s_var2, s_std2, s_ln2, s_yn, s_ynT, s_ynE, s_lg = (
            sem(n) for n in ("s_var2", "s_std2", "s_ln2", "s_yn", "s_ynT", "s_ynE", "s_lg"))
        s_gap, s_exp, s_chosen, s_rank, s_pos, s_scat = (
            sem(n) for n in ("s_gap", "s_exp", "s_chosen", "s_rank", "s_pos", "s_scat"))
        s_erowi = sem("s_erowi")
        s_b1r, s_b1T, s_b1e, s_erow = sem("s_b1r"), sem("s_b1T"), sem("s_b1e"), sem("s_erow")
        s_wt = [sem(f"s_wt{u}") for u in range(2)]
        s_ct, s_xT, s_l1, s_h, s_ffn, s_eo = (sem(n) for n in ("s_ct", "s_xT", "s_l1", "s_h", "s_ffn", "s_eo"))
        s_store = [sem(f"s_store{u}") for u in range(2)]
        s_got = [sem(f"s_got{u}") for u in range(GR)]
        s_used, s_y, s_v3, s_std3, s_sh3, s_norm, s_fin, s_xb = (
            sem(n) for n in ("s_used", "s_y", "s_v3", "s_std3", "s_sh3", "s_norm", "s_fin", "s_xb"))
        block = ctx.enter_context(nc.Block())

        @block.gpsimd
        def _(pool):
            nc.gpsimd.memset(ident[:, :], 0.0).then_inc(s_const, 1)
            nc.gpsimd.memset(zeros[:, :], 0.0).then_inc(s_z, 1)
            nc.gpsimd.memset(before[:, :], 1.0).then_inc(s_const, 1)
            pool.wait_ge(s_const, 2)
            nc.gpsimd.affine_select(out=ident[:, :], in_=ident[:, :], compare_op=ALU.not_equal, fill=1.0,
                                    base=0, pattern=[[-1, 128]], channel_multiplier=1).then_inc(s_const, 1)
            nc.gpsimd.affine_select(out=before[:, :], in_=before[:, :], compare_op=ALU.is_gt, fill=0.0,
                                    base=0, pattern=[[1, 128]], channel_multiplier=-1).then_inc(s_const, 1)
            nc.gpsimd.iota(rown[:, :], pattern=[[0, 1]], base=0, channel_multiplier=1).then_inc(s_const, 1)
            nc.gpsimd.memset(cube[:, :, :], 0.0).then_inc(s_const, 1)
            nc.gpsimd.memset(eps[:, :], EPS).then_inc(s_const, 1)
            nc.gpsimd.memset(ones[:, :], 1.0).then_inc(s_const, 1)
            pool.wait_ge(s_const, 8)
            nc.gpsimd.affine_select(out=cube[:, :, :], in_=cube[:, :, :], compare_op=ALU.not_equal, fill=1.0,
                                    base=0, pattern=[[-HJ, HH], [-1, HJ]], channel_multiplier=1).then_inc(s_const, 1)
            nc.gpsimd.iota(places[:, :], pattern=[[1, BN]], base=0, channel_multiplier=0,
                           allow_small_or_imprecise_dtypes=True).then_inc(s_const, 1)
            nc.gpsimd.iota(firsts[:, :], pattern=[[512, NB]], base=512 * BASE, channel_multiplier=0,
                           allow_small_or_imprecise_dtypes=True).then_inc(s_const, 1)

            def low_half(t, u):
                pool.wait_ge(s_hi, t + 1)
                nc.gpsimd.tensor_tensor(xl[:, DS(t, 1), :].rearrange("p a f -> p (a f)"), xs[:, u, :],
                                        xh[:, DS(t, 1), :].rearrange("p a f -> p (a f)"), ALU.subtract).then_inc(s_lo, 1)

            with pool.Fori(0, NT - 1, 2) as t:
                for u in range(2):
                    low_half(t + u, u)

            nc.gpsimd.iota(eix[:, :], pattern=[[1, X]], base=0, channel_multiplier=0,
                           allow_small_or_imprecise_dtypes=True).then_inc(s_con2, 1)
            nc.gpsimd.iota(eix64[:, :], pattern=[[1, X]], base=64, channel_multiplier=0,
                           allow_small_or_imprecise_dtypes=True).then_inc(s_con2, 1)
            nc.gpsimd.tensor_copy(before16[:, :], before[0:NP, 0:NP]).then_inc(s_con2, 1)
            nc.gpsimd.memset(ones16[:, :], 1.0).then_inc(s_con2, 1)

            pool.wait_ge(s_rank, 1)
            nc.gpsimd.iota(started, pattern=[[128, NCH], [0, X]], base=0, channel_multiplier=0,
                           allow_small_or_imprecise_dtypes=True).then_inc(s_erowi, 1)

            pool.wait_ge(s_pos, 1)
            pool.wait_ge(s_zero, 16)
            for c in range(KT):
                nc.gpsimd.indirect_dma_start(
                    out=slots_d, out_offset=bass.IndirectOffsetOnAxis(ap=posi[:, c:c + 1], axis=0),
                    in_=yn[:, c % NT, :], in_offset=None).then_inc(s_scat, 16)

            pool.wait_ge(s_gam, 32)
            with pool.Fori(0, NT) as t:
                nc.gpsimd.tensor_tensor(x_sb[:, DS(t, 1), :].rearrange("p a f -> p (a f)"),
                                        x_sb[:, DS(t, 1), :].rearrange("p a f -> p (a f)"), bet[:, :], ALU.add
                                        ).then_inc(s_xb, 1)

            def store(j, u):
                pool.wait_ge(s_eo, j + 1 + 2)
                pool.dma_start(eo_d[DS(j * 128, 128), :], eo[:, u, :]).then_inc(s_store[u], 16)

            with pool.Fori(0, NCH - 2, 2) as j:
                for u in range(2):
                    store(j + u, u)
            store(NCH - 1, 0)
            pool.wait_ge(s_store[0], 16 * (NCH // 2 + 1))
            pool.wait_ge(s_store[1], 16 * (NCH // 2))
            for t in range(NT):
                if t >= GR:
                    pool.wait_ge(s_used, t - GR + 1)
                for k in range(2):
                    nc.gpsimd.indirect_dma_start(
                        out=got[:, t % GR, k, :], out_offset=None, in_=eo_d,
                        in_offset=bass.IndirectOffsetOnAxis(ap=posi[:, k * NT + t:k * NT + t + 1], axis=0)
                        ).then_inc(s_got[t % GR], 16)

        @block.sync
        def _(sp):
            sp.dma_start(dsts, dst.rearrange("(p j) -> p j", p=NP)).then_inc(s_dst, 16)
            sp.dma_start(srcs, src.rearrange("(p j) -> p j", p=NP)).then_inc(s_src, 16)
            sp.dma_start(x_sb[:, :, :], x.rearrange("(p t) f -> p t f", t=NT)).then_inc(s_x, 16)
            sp.dma_start(gw[:, :, :], gate_w.rearrange("(a p) e -> p a e", p=128)).then_inc(s_gw, 16)
            sp.dma_start(gb[:, :], gate_b.rearrange("(a n) -> a n", a=1).to_broadcast([NP, X])).then_inc(s_gw, 16)
            sp.wait_ge(s_z, 1)
            sp.dma_start(slots_d.rearrange("(j p) f -> p j f", p=128),
                         zeros[:, :].rearrange("p (a f) -> p a f", a=1).to_broadcast([128, NCH, F])).then_inc(s_zero, 16)
            sp.wait_ge(s_offi, 1)
            sp.dma_start(off_d.rearrange("(h l) -> h l", h=HH), offi[:, :]).then_inc(s_offd, 16)
            sp.wait_ge(s_offd, 16)
            sp.dma_start(offrow[:, :], off_d.rearrange("(a n) -> a n", a=1)).then_inc(s_offrow, 16)
            sp.wait_ge(s_offrow, 16)
            sp.wait_ge(s_listed, 2)
            sp.dma_start(list_d.rearrange("(p c) w -> p (c w)", p=128), listed[:, :, :].rearrange("p c w -> p (c w)")).then_inc(s_list, 16)
            sp.wait_ge(s_list, 16)
            sp.dma_start(w1s, W1.rearrange("(a p) n -> p a n", p=128)).then_inc(s_w, 16)
            sp.dma_start(w2s, W2.rearrange("(a p) n -> p a n", p=128)).then_inc(s_w, 16)
            with nc.allow_non_contiguous_dma(reason="512 numbers, once"):
                sp.dma_start(b1c[:, :], b1.rearrange("(a p) -> p a", p=128)).then_inc(s_w, 16)
            sp.dma_start(b2r[:, :], b2.rearrange("(a n) -> a n", a=1)).then_inc(s_w, 16)
            sp.wait_ge(s_rounds, 1)
            rounds = sp.value_load(rnd[0:1, 4:5], min_val=1, max_val=521)
            with sp.Fori(0, rounds) as r:
                sp.wait_ge(s_offnew, r + 1)
                sp.sem_inc(s_started, 1)
                with sp.Fori(0, NS * NT // GU) as g:
                    _, starts = nc.values_load_multi_w_load_instructions(
                        offrow[0:1, DS(g * GU, GU)], engines=[mybir.EngineType.SP], min_val=0, max_val=LAST_START)
                    for u in range(GU):
                        sp.wait_ge(s_winfree, (r * (NS * NT // GU) + g) * GU + u + 1)
                        sp.dma_start(win[:, u, :, :].rearrange("p k w -> p (k w)"),
                                     list_d[DS(starts[u], WIN), :].rearrange("(p k) w -> p (k w)", p=128)
                                     ).then_inc(s_win[u], 16)
                sp.drain().then_inc(s_round, 1)
            sp.wait_ge(s_hst, NT)
            sp.dma_start(gam[:, :], gamma.rearrange("(a n) -> a n", a=1).to_broadcast([NP, F])).then_inc(s_gam, 16)
            sp.dma_start(bet[:, :], beta.rearrange("(a n) -> a n", a=1).to_broadcast([NP, F])).then_inc(s_gam, 16)
            sp.dma_start(b1r, eb1.rearrange("e (a n) -> (e a) n", a=HA)).then_inc(s_b1r, 16)
            sp.wait_ge(s_erow, 1)
            sp.wait_ge(s_scat, 16 * KT)

            def load(j, u):
                e = sp.value_load(erow[0:1, DS(j, 1)], min_val=0, max_val=X - 1)
                sp.wait_ge(s_ffn, j + 1)
                sp.sem_inc(s_started, 1)
                sp.wait_ge(s_eo, j + 1)
                sp.sem_inc(s_started, 1)
                sp.dma_start(xr[:, u, :], slots_d[DS(j * 128, 128), :]).then_inc(s_wt[u], 16)
                sp.dma_start(wt1[:, u, :, :], ew1[DS(e, 1), :, :].rearrange("e (a p) n -> p (e a) n", p=128)).then_inc(s_wt[u], 16)
                sp.dma_start(wt2[:, u, :, :], ew2[DS(e, 1), :, :].rearrange("e (a p) n -> p (e a) n", p=128)).then_inc(s_wt[u], 16)
                sp.dma_start(wb2[:, u, :], eb2[DS(e, 1), :].to_broadcast([128, F])).then_inc(s_wt[u], 16)

            with sp.Fori(0, NCH - 2, 2) as j:
                for u in range(2):
                    load(j + u, u)
            load(NCH - 1, 0)
            with sp.Fori(0, NT // GR) as g:
                sp.wait_ge(s_fin, g + 1)
                sp.dma_start(out.rearrange("(p t) f -> p t f", t=NT)[:, DS(g * GR, GR), :],
                             yn[:, DS(g * GR, GR), :]).then_inc(s_out, 16)
            sp.wait_ge(s_out, 16 * (NT // GR))

        @block.vector
        def _(dve):
            V = nc.vector
            chain = [0]

            def link(ins):
                chain[0] += 1
                ins.then_inc(s_chain, 1)
                dve.wait_ge(s_chain, chain[0])

            def after(ins):
                chain[0] += 1
                ins.then_inc(s_chain, 1)

            def join():
                dve.wait_ge(s_chain, chain[0])

            V.memset(keys[0][:, :].bitcast(i32), SENTINEL).then_inc(s_chain, 1)
            chain[0] += 1
            dve.wait_ge(s_const, 11)
            for lv in range(LEVELS + 1):
                link(V.tensor_scalar(bit[:, :], rown[:, :], lv, 1, ALU.logical_shift_right, ALU.bitwise_and))
                link(V.tensor_scalar(sign[:, lv:lv + 1], bit[:, :], -2.0, 1.0, ALU.mult, ALU.add))
            link(V.tensor_tensor(toggle[:, 1:], sign[:, 0:LEVELS], sign[:, 1:], ALU.mult))

            def split(whole, quotient, rest, t1):
                link(V.tensor_scalar(t1, whole, 1, None, ALU.logical_shift_right))
                link(V.tensor_scalar(quotient, t1, 1311, None, ALU.mult))
                link(V.tensor_scalar(quotient, quotient, 15, None, ALU.logical_shift_right))
                link(V.scalar_tensor_tensor(rest, quotient, -NT, whole, ALU.mult, ALU.add))

            dve.wait_ge(s_dst, 16)
            split(dsts, ta, tb, tf)
            dve.wait_ge(s_src, 16)
            split(srcs, tc, td, tf)
            link(V.tensor_scalar(te, td, 3, None, ALU.bitwise_and))
            link(V.scalar_tensor_tensor(tc, te, NP, tc, ALU.mult, ALU.add))
            link(V.tensor_scalar(td, td, 2, None, ALU.logical_shift_right))
            link(V.scalar_tensor_tensor(td, td, NT, tb, ALU.mult, ALU.add))
            link(V.scalar_tensor_tensor(tc, tc, 128, ta, ALU.mult, ALU.add))
            after(V.tensor_scalar(ta, td, 5, None, ALU.logical_shift_right))
            after(V.tensor_scalar(tb, td, 31, None, ALU.bitwise_and))
            link(V.tensor_scalar(td, td, BASE, None, ALU.add))
            after(V.tensor_copy(hi16[:, :], ta))
            after(V.tensor_copy(lo16[:, :], tb))
            link(V.scalar_tensor_tensor(keys[0][0:NP, 0:EC].bitcast(i32), td, 16, tc,
                                        ALU.logical_shift_left, ALU.bitwise_or))
            link(V.tensor_scalar(keys[0][:, :], keys[0][:, :], sign[:, 0:1], None, ALU.mult))

            for q in range(PIECES):
                if q >= 2:
                    dve.wait_ge(s_hist, q - 1)
                for v in range(HH):
                    V.tensor_scalar(hot_hi[q % 2][:, :, v, :], hi16[:, q * HP:(q + 1) * HP].rearrange("p (g j) -> p g j", j=HJ),
                                    float(v), None, ALU.is_equal)
                for v in range(HL):
                    last = V.tensor_scalar(hot_lo[q % 2][:, v, :], lo16[:, q * HP:(q + 1) * HP], float(v), None, ALU.is_equal)
                last.then_inc(s_hot, 1)

            dve.wait_ge(s_x, 16)
            with dve.Fori(0, NT) as t:
                V.bn_stats(stats[:, DS(t, 1), :].rearrange("p a s -> p (a s)"),
                           x_sb[:, DS(t, 1), :].rearrange("p a f -> p (a f)")).then_inc(s_ln, 1)
            dve.wait_ge(s_ln, NT)
            link(V.tensor_tensor(mean[:, :], stats[:, :, 1], stats[:, :, 4], ALU.add))
            link(V.tensor_tensor(var[:, :], stats[:, :, 1], stats[:, :, 4], ALU.subtract))
            link(V.tensor_tensor(var[:, :], var[:, :], var[:, :], ALU.mult))
            link(V.tensor_tensor(shift[:, :], stats[:, :, 2], stats[:, :, 5], ALU.add))
            link(V.tensor_scalar(var[:, :], var[:, :], F / 4, None, ALU.mult))
            link(V.tensor_tensor(var[:, :], var[:, :], shift[:, :], ALU.add))
            V.tensor_scalar(mean[:, :], mean[:, :], 0.5, None, ALU.mult).then_inc(s_var, 1)
            dve.wait_ge(s_std, 1)
            link(V.reciprocal(rstd[:, :], var[:, :]))
            link(V.tensor_scalar(rstd[:, :], rstd[:, :], UP, None, ALU.mult))
            link(V.tensor_tensor(shift[:, :], mean[:, :], rstd[:, :], ALU.mult))
            V.tensor_scalar(shift[:, :], shift[:, :], -1.0, None, ALU.mult).then_inc(s_ln, 1)

            dve.wait_ge(s_hist, PIECES)
            after(V.tensor_reduce(same[:, :], cube[:, :, :].rearrange("p v j -> p j v"), AX.X, ALU.add))
            link(V.tensor_reduce(fold[:, :], cube[:, :, :], AX.X, ALU.add))
            link(V.tensor_tensor(crossed[:, :, :], psH.rearrange("p (j l) -> p j l", j=HJ),
                                 same[:, :].rearrange("p (j a) -> p j a", a=1).to_broadcast([HJ * HH, HJ, HL]), ALU.mult))
            link(V.tensor_reduce(diag[:, :], crossed[:, :, :].rearrange("p j l -> p l j"), AX.X, ALU.add))
            V.tensor_copy(bit[0:1, :], rown[0:1, :]).then_inc(s_diag, 1)
            dve.wait_ge(s_folded, 1)
            link(V.tensor_copy(cnt[:, :], psC))
            after(V.tensor_reduce(most[:, :], cnt[:, :], AX.X, ALU.max))
            link(V.tensor_tensor_scan(incl[:, :], cnt[:, :], cnt[:, :], 0.0, ALU.add, ALU.bypass))
            V.tensor_copy(bit[0:1, :], rown[0:1, :]).then_inc(s_cnt, 1)
            dve.wait_ge(s_base, 1)
            link(V.tensor_tensor(offf[:, :], incl[:, :], cnt[:, :], ALU.subtract))
            V.tensor_scalar(offi[:, :], offf[:, :], psO, None, ALU.add).then_inc(s_offi, 1)
            link(V.tensor_reduce(rnd[:, 0:1], psM, AX.X, ALU.max))
            link(V.tensor_scalar(rnd[:, 1:2], rnd[:, 0:1], WIN - 1, None, ALU.add))
            link(V.tensor_scalar(rnd[:, 2:3], rnd[:, 1:2], 7, None, ALU.logical_shift_right))
            link(V.tensor_scalar(rnd[:, 3:4], rnd[:, 2:3], 683, None, ALU.mult))
            V.tensor_scalar(rnd[:, 4:5], rnd[:, 3:4], 11, None, ALU.logical_shift_right).then_inc(s_rounds, 1)

            state = [0]

            def exchange(source, sz, k, both, other=None):
                join()
                target = keys[1 - state[0]]
                if both:
                    i, o = (a.rearrange("p (m d q w k) -> p m d q w k", d=2, q=sz // (2 * k), w=2, k=k)
                            for a in (source, target[:, :]))
                    for d in range(2):
                        a, b = i[:, :, d, :, 0, :], i[:, :, d, :, 1, :]
                        after(V.tensor_tensor(o[:, :, d, :, 0, :], a, b, ALU.max if d else ALU.min))
                        after(V.tensor_tensor(o[:, :, d, :, 1, :], a, b, ALU.min if d else ALU.max))
                else:
                    i, o = (a.rearrange("p (q w k) -> p q w k", w=2, k=k) for a in (source, target[:, :]))
                    a, b = i[:, :, 0, :], i[:, :, 1, :]
                    if other is not None:
                        b = other.rearrange("p (q k) -> p q k", k=k)
                    after(V.tensor_tensor(o[:, :, 0, :], a, b, ALU.min))
                    after(V.tensor_tensor(o[:, :, 1, :], a, b, ALU.max))
                state[0] = 1 - state[0]

            def now():
                return keys[state[0]][:, :]

            sz = 2
            while sz <= C:
                k = sz // 2
                while k:
                    exchange(now(), sz, k, sz < C)
                    k //= 2
                sz *= 2
            for lv in range(1, LEVELS + 1):
                join()
                V.tensor_copy(bit[0:1, :], rown[0:1, :]).then_inc(s_rows, 1)
                kept.append(state[0])
                dve.wait_ge(s_T, 4 * lv)
                dve.wait_ge(s_Tup, 4 * lv)
                source = psT
                k = 2 ** (lv - 1)
                while k:
                    exchange(source, 2 * k, k, False, upper if source is psT else None)
                    source = now()
                    k //= 2
                join()
                V.tensor_copy(bit[0:1, :], rown[0:1, :]).then_inc(s_Tdone, 1)
                kept2.append(state[0])
                dve.wait_ge(s_R, 4 * lv)
                dve.wait_ge(s_Rup, 2 * lv)
                source = psR
                k = C // 2
                while k:
                    exchange(source, 2 * k, k, False, upper if source is psR else None)
                    source = now()
                    k //= 2
            join()
            a, b = keys[state[0]], keys[1 - state[0]]
            link(V.tensor_scalar(b[:, :].bitcast(i32), a[:, :].bitcast(i32), 7, None, ALU.logical_shift_right))
            V.tensor_copy(listed[:, :, 0], b[:, :].bitcast(i32)).then_inc(s_listed, 1)
            link(V.tensor_scalar(a[:, :].bitcast(i32), a[:, :].bitcast(i32), 127, None, ALU.bitwise_and))
            V.tensor_copy(listed[:, :, 1], a[:, :].bitcast(i32)).then_inc(s_listed, 1)
            dve.wait_ge(s_lnE, NT)
            link(V.memset(xnT[:, :, N:], 0.0))

            dve.wait_ge(s_offrow, 16)
            V.tensor_scalar(offrow[:, :], offrow[:, :], LAST_START, None, ALU.min).then_inc(s_offnew, 1)
            dve.wait_ge(s_rounds, 1)
            rounds = dve.value_load(rnd[0:1, 4:5], min_val=1, max_val=521)

            dve.sem_inc(s_winfree, GU)
            dve.wait_ge(s_list, 16)
            dve.wait_ge(s_zero, 16)
            with dve.Fori(0, rounds) as r:
                with dve.Fori(0, NS) as S:
                    with dve.Fori(0, NT // GU) as G:
                        b0 = (S * (NT // GU) + G) * GU
                        n0 = r * NB + b0
                        for u in range(GU):
                            dve.wait_ge(s_win[u], (r * (NB // GU) + S * (NT // GU) + G) * 16 + 16)
                            V.tensor_tensor(rel[:, u % 2, :], win[:, u, :, 0],
                                            firsts[:, DS(b0 + u, 1)].to_broadcast([128, K]), ALU.subtract).then_inc(s_rel, 1)
                            dve.wait_ge(s_built, n0 + u + 1)
                            for k in range(K):
                                V.tensor_scalar(ohd[:, u % OR, k, :], places[:, 0:128], win[:, u, k, 1:2], None, ALU.is_equal)
                            dve.wait_ge(s_rel, n0 + u + 1)
                            for k in range(K):
                                last = V.tensor_scalar(ohs[:, u % OR, k, :], places[:, :], rel[:, u % 2, k:k + 1], None, ALU.is_equal)
                            last.then_inc(s_oh, 1)
                            V.tensor_copy(bit[0:1, :], rown[0:1, :]).then_inc(s_winfree, 1)
                    dve.wait_ge(s_main, r * NB + S * NT + NT + AR)
                    V.scalar_tensor_tensor(xnT[:, :, DS(S * BN, BN)], ps[:, 2:4, 0:BN], 1.0 / UP,
                                           xnT[:, :, DS(S * BN, BN)], ALU.mult, ALU.add).then_inc(s_agg, 1)
                dve.wait_ge(s_round, r + 1)
                V.tensor_scalar(offrow[:, :], offrow[:, :], WIN, LAST_START, ALU.add, ALU.min).then_inc(s_offnew, 1)

            dve.wait_ge(s_w1T, 1)
            for a in range(HID // 128):
                last = V.tensor_copy(w1T[:, a, :], ps[:, 4 + a // 2, (a % 2) * 256:(a % 2) * 256 + 256])
            last.then_inc(s_w1Te, 1)
            dve.wait_ge(s_wf, 1)
            V.tensor_copy(wf[:, :, :], ps[:, 6, :].rearrange("p (a f) -> p a f", a=FH))
            V.tensor_tensor(brow[:, :], ps[0:1, 7, 0:F], b2r[:, :], ALU.add).then_inc(s_wfe, 1)
            with dve.Fori(0, NT - 1, 2) as t:
                for u in range(2):
                    dve.wait_ge(s_lin, t + u + 1)
                    V.tensor_tensor(x_sb[:, DS(t + u, 1), :].rearrange("p a f -> p (a f)"), ps[0:NP, u, 0:F],
                                    x_sb[:, DS(t + u, 1), :].rearrange("p a f -> p (a f)"), ALU.add).then_inc(s_x1, 1)

            dve.wait_ge(s_x1, NT)
            with dve.Fori(0, NT) as t:
                V.bn_stats(stats[:, DS(t, 1), :].rearrange("p a s -> p (a s)"),
                           x_sb[:, DS(t, 1), :].rearrange("p a f -> p (a f)")).then_inc(s_ln2, 1)
            dve.wait_ge(s_ln2, NT)
            link(V.tensor_tensor(mean[:, :], stats[:, :, 1], stats[:, :, 4], ALU.add))
            link(V.tensor_tensor(var[:, :], stats[:, :, 1], stats[:, :, 4], ALU.subtract))
            link(V.tensor_tensor(var[:, :], var[:, :], var[:, :], ALU.mult))
            link(V.tensor_tensor(shift[:, :], stats[:, :, 2], stats[:, :, 5], ALU.add))
            link(V.tensor_scalar(var[:, :], var[:, :], F / 4, None, ALU.mult))
            link(V.tensor_tensor(var[:, :], var[:, :], shift[:, :], ALU.add))
            V.tensor_scalar(mean[:, :], mean[:, :], 0.5, None, ALU.mult).then_inc(s_var2, 1)
            dve.wait_ge(s_std2, 1)
            link(V.reciprocal(rstd[:, :], var[:, :]))
            link(V.tensor_tensor(shift[:, :], mean[:, :], rstd[:, :], ALU.mult))
            V.tensor_scalar(shift[:, :], shift[:, :], -1.0, None, ALU.mult).then_inc(s_ln2, 1)

            def evacuate(t, u, first=False):
                dve.wait_ge(s_ynT, t + 1)
                if not first:
                    dve.wait_ge(s_lg, t - 1)
                V.tensor_copy(ynT[:, u, :, :], ps[:, u, 0:FH * NP].rearrange("p (a n) -> p a n", a=FH)).then_inc(s_ynE, 1)

            for t in range(2):
                evacuate(t, t, True)
            with dve.Fori(2, NT - 1, 2) as t:
                for u in range(2):
                    evacuate(t + u, u)

            dve.wait_ge(s_lg, NT)
            dve.wait_ge(s_con2, 4)
            dve.wait_ge(s_gw, 32)

            def over_tiles(a, n):
                return a.rearrange("p (t e) -> p t e", t=1).to_broadcast([NP, n, X])

            def over_experts(a):
                return a.rearrange("p (t e) -> p t e", e=1).to_broadcast([NP, NT, X])

            after(V.tensor_tensor(logits[:, 0:32, :], ps[0:NP, 2, :].rearrange("p (t e) -> p t e", e=X), over_tiles(gb[:, :], 32), ALU.add))
            link(V.tensor_tensor(logits[:, 32:, :], ps[0:NP, 3, 0:(NT - 32) * X].rearrange("p (t e) -> p t e", e=X), over_tiles(gb[:, :], NT - 32), ALU.add))
            values = logits
            for k in range(2):
                one = chosen[:, :, k * NT:(k + 1) * NT].rearrange("p e t -> p t e")
                link(V.tensor_reduce(best[:, k, :], values, AX.X, ALU.max))
                link(V.tensor_tensor(one, values, over_experts(best[:, k, :]), ALU.is_equal))
                link(V.scalar_tensor_tensor(one, one, -64.0, over_tiles(eix64[:, :], NT), ALU.mult, ALU.add))
                link(V.tensor_reduce(which[:, k, :], one, AX.X, ALU.min))
                link(V.tensor_tensor(one, over_tiles(eix[:, :], NT), over_experts(which[:, k, :]), ALU.is_equal))
                if k == 0:
                    link(V.scalar_tensor_tensor(masked, one, -3.0e38, logits, ALU.mult, ALU.add))
                    values = masked
            V.tensor_tensor(share[:, 1, :], best[:, 1, :], best[:, 0, :], ALU.subtract).then_inc(s_gap, 1)
            V.tensor_copy(chosen16, chosen.rearrange("p e k -> p (e k)")).then_inc(s_chosen, 1)
            dve.wait_ge(s_exp, 1)
            link(V.tensor_scalar(share[:, 0, :], share[:, 1, :], 1.0, None, ALU.add))
            link(V.reciprocal(share[:, 0, :], share[:, 0, :]))
            link(V.tensor_tensor(share[:, 1, :], share[:, 1, :], share[:, 0, :], ALU.mult))

            dve.wait_ge(s_rank, 1)
            link(V.tensor_copy(total.rearrange("p e k -> p (e k)").rearrange("p (b n) -> p b n", b=4), ps[0:NP, 4:8, 0:400]))
            flat = (total.rearrange("p e k -> p (e k)"), upto.rearrange("p e k -> p (e k)"))
            link(V.tensor_tensor_scan(flat[1], flat[0], flat[0], 0.0, ALU.add, ALU.bypass))
            link(V.tensor_tensor(total, upto, total, ALU.subtract))
            link(V.tensor_tensor(padded[:, :], upto[:, :, KT - 1], total[:, :, 0], ALU.subtract))
            link(V.tensor_scalar(nexp[:, :], padded[:, :], 127.0, None, ALU.add))
            link(V.tensor_scalar(nexp[:, :], nexp[:, :], 7, 7, ALU.logical_shift_right, ALU.logical_shift_left))
            link(V.tensor_copy(padded[:, :], nexp[:, :]))
            link(V.tensor_tensor_scan(padend[:, :], padded[:, :], padded[:, :], 0.0, ALU.add, ALU.bypass))
            link(V.tensor_tensor(adjust[:, :], padend[:, :], padded[:, :], ALU.subtract))
            link(V.tensor_tensor(adjust[:, :], adjust[:, :], total[:, :, 0], ALU.subtract))
            link(V.tensor_tensor(place.rearrange("p e k -> p (e k)").rearrange("p (b n) -> p b n", b=4), ps[0:NP, 0:4, 0:400],
                                 total.rearrange("p e k -> p (e k)").rearrange("p (b n) -> p b n", b=4), ALU.add))
            link(V.tensor_tensor(place, place, adjust[:, :].rearrange("p (e k) -> p e k", k=1).to_broadcast([NP, X, KT]), ALU.add))
            link(V.tensor_tensor(place, place, chosen, ALU.mult))
            link(V.tensor_reduce(posf[:, :], place.rearrange("p e k -> p k e"), AX.X, ALU.add))
            V.tensor_copy(posi[:, :], posf[:, :]).then_inc(s_pos, 1)
            dve.wait_ge(s_erowi, 1)
            link(V.tensor_tensor(reach, started, padend[0:1, :].rearrange("p (j e) -> p j e", j=1).to_broadcast([1, NCH, X]), ALU.is_ge))
            link(V.tensor_reduce(erowf[:, :], reach, AX.X, ALU.add))
            dve.wait_ge(s_b1T, 1)
            link(V.tensor_copy(b1T, ps[:, 7, 448:448 + X * HA]))
            V.tensor_scalar(erow[:, :], erowf[:, :], X - 1, None, ALU.min).then_inc(s_erow, 1)

            dve.sem_inc(s_l1, 2 * HA)
            dve.sem_inc(s_eo, 2)

            def rows_T(j, u):
                dve.wait_ge(s_ct, j + 1)
                dve.wait_ge(s_l1, (j + 1) * HA)
                V.tensor_copy(xT[:, u, :, :], ps[:, u, 0:F].rearrange("p (a n) -> p a n", a=FH)).then_inc(s_xT, 1)

            def result(j, u, pair):
                dve.wait_ge(s_ffn, j + 1 + 2)
                if pair is not None:
                    dve.wait_ge(s_store[u], pair * 16)
                V.tensor_tensor(eo[:, u, :], ps[:, 4 + u, 0:F], wb2[:, u, :], ALU.add).then_inc(s_eo, 1)

            rows_T(0, 0)
            rows_T(1, 1)
            result(0, 0, None)
            rows_T(2, 0)
            result(1, 1, None)
            with dve.Fori(1, NCH // 2) as g:
                rows_T(g * 2 + 1, 1)
                result(g * 2, 0, g)
                rows_T(g * 2 + 2, 0)
                result(g * 2 + 1, 1, g)
            result(NCH - 1, 0, NCH // 2)

            dve.wait_ge(s_xb, NT)
            dve.wait_ge(s_gam, 32)
            def rows(t):
                return yn[:, DS(t, 1), :].rearrange("p a f -> p (a f)")

            with dve.Fori(0, NT // GR) as g:
                for u in range(GR):
                    dve.wait_ge(s_got[u], g * 32 + 32)
                    V.scalar_tensor_tensor(rows(g * GR + u), got[:, u, 0, :], share[:, 0, DS(g * GR + u, 1)], rows(g * GR + u),
                                           ALU.mult, ALU.add).then_inc(s_y, 1)
                for u in range(GR):
                    dve.wait_ge(s_y, g * 2 * GR + u + 1)
                    V.scalar_tensor_tensor(rows(g * GR + u), got[:, u, 1, :], share[:, 1, DS(g * GR + u, 1)], rows(g * GR + u),
                                           ALU.mult, ALU.add).then_inc(s_y, 1)
                dve.wait_ge(s_y, g * 2 * GR + 2 * GR)
                dve.sem_inc(s_started, 1)
                for u in range(GR):
                    V.bn_stats(stats[:, u, :], rows(g * GR + u)).then_inc(s_used, 1)
                n = [0]

                def step(ins):
                    n[0] += 1
                    ins.then_inc(s_v3, 1)
                    dve.wait_ge(s_v3, g * 10 + n[0])

                dve.wait_ge(s_used, g * GR + GR)
                step(V.tensor_tensor(mean[:, 0:GR], stats[:, 0:GR, 1], stats[:, 0:GR, 4], ALU.add))
                step(V.tensor_tensor(var[:, 0:GR], stats[:, 0:GR, 1], stats[:, 0:GR, 4], ALU.subtract))
                step(V.tensor_tensor(var[:, 0:GR], var[:, 0:GR], var[:, 0:GR], ALU.mult))
                step(V.tensor_tensor(shift[:, 0:GR], stats[:, 0:GR, 2], stats[:, 0:GR, 5], ALU.add))
                step(V.tensor_scalar(var[:, 0:GR], var[:, 0:GR], F / 4, None, ALU.mult))
                step(V.tensor_tensor(var[:, 0:GR], var[:, 0:GR], shift[:, 0:GR], ALU.add))
                step(V.tensor_scalar(mean[:, 0:GR], mean[:, 0:GR], -0.5, None, ALU.mult))
                dve.wait_ge(s_std3, g + 1)
                step(V.reciprocal(rstd[:, 0:GR], var[:, 0:GR]))
                step(V.tensor_tensor(shift[:, 0:GR], mean[:, 0:GR], rstd[:, 0:GR], ALU.mult))
                V.tensor_copy(bit[0:1, :], rown[0:1, :]).then_inc(s_v3, 1)
                dve.wait_ge(s_norm, g * GR + GR)
                five = yn[:, DS(g * GR, GR), :]
                V.tensor_tensor(five, five, gam[:, :].rearrange("p (t f) -> p t f", t=1).to_broadcast([NP, GR, F]),
                                ALU.mult).then_inc(s_sh3, 1)
                dve.wait_ge(s_sh3, g + 1)
                V.tensor_tensor(five, five, x_sb[:, DS(g * GR, GR), :], ALU.add).then_inc(s_fin, 1)

        @block.scalar
        def _(act):
            A = nc.scalar
            act.wait_ge(s_var, 1)
            act.wait_ge(s_const, 11)
            A.activation(var[:, :], var[:, :], ACT.Sqrt, bias=eps[0:NP, :], scale=1.0 / F).then_inc(s_std, 1)
            act.wait_ge(s_ln, NT + 1)
            act.wait_ge(s_hist, PIECES)

            def normalise(t, u, first=False):
                if not first:
                    act.wait_ge(s_lnT, t - 1)
                    act.wait_ge(s_lo, t - 1)
                A.activation(xs[:, u, :], x_sb[:, DS(t, 1), :].rearrange("p a f -> p (a f)"), ACT.Identity,
                             bias=shift[:, DS(t, 1)], scale=rstd[:, DS(t, 1)]).then_inc(s_xs, 1)
                act.wait_ge(s_xs, t + 1)
                A.activation(xh[:, DS(t, 1), :].rearrange("p a f -> p (a f)"), xs[:, u, :], ACT.Copy).then_inc(s_hi, 1)
                act.wait_ge(s_lnT, t + 1)
                A.activation(xnT[:, :, DS(t * NP, NP)], ps[:, u, 0:FH * NP].rearrange("p (a n) -> p a n", a=FH),
                             ACT.Copy, scale=1.0 / UP).then_inc(s_lnE, 1)

            for t in range(2):
                normalise(t, t, True)
            with act.Fori(2, NT - 1, 2) as t:
                for u in range(2):
                    normalise(t + u, u)
            for lv in range(1, LEVELS + 1):
                act.wait_ge(s_rows, lv)
                a, b = keys[kept[lv - 1]], keys[1 - kept[lv - 1]]
                for q in range(4):
                    nc.scalar.activation(b[:, q * 512:(q + 1) * 512], a[:, q * 512:(q + 1) * 512], ACT.Copy,
                                         scale=toggle[:, lv:lv + 1]).then_inc(s_signed, 1)
                k = 2 ** (lv - 1)
                for q in range(4):
                    act.wait_ge(s_T, 4 * (lv - 1) + q + 1)
                    nc.scalar.activation(upper[:, q * 256:(q + 1) * 256].rearrange("p (a k) -> p a k", k=k),
                                         ps[:, q, :].rearrange("p (a w k) -> p a w k", w=2, k=k)[:, :, 1, :],
                                         ACT.Copy).then_inc(s_Tup, 1)
                for q in range(2):
                    act.wait_ge(s_R, 4 * (lv - 1) + q + 3)
                    nc.scalar.activation(upper[:, q * 512:(q + 1) * 512], ps[:, 6 + q, :], ACT.Copy).then_inc(s_Rup, 1)

            act.wait_ge(s_rounds, 1)
            rounds = act.value_load(rnd[0:1, 4:5], min_val=1, max_val=521)
            act.sem_inc(s_at, AR)
            with act.Fori(0, rounds) as r:
                with act.Fori(0, NB // GU) as g:
                    n0 = (r * (NB // GU) + g) * GU
                    for u in range(GU):
                        act.wait_ge(s_built, n0 + u + 1 + OR)
                        act.wait_ge(s_main, n0 + u + 1)
                        A.activation(atn[:, u % AR, :], ps[0:NP, u % AR, 0:BN], ACT.Copy).then_inc(s_at, 1)
            act.wait_ge(s_agg, rounds * NS + 1)

            def stage(t, u, first=False):
                if not first:
                    act.wait_ge(s_lin, t - 1)
                A.activation(hst[:, u, :, :], xnT[:, :, DS(t * NP, NP)], ACT.Copy).then_inc(s_hst, 1)

            for t in range(2):
                stage(t, t, True)
            with act.Fori(2, NT - 1, 2) as t:
                for u in range(2):
                    stage(t + u, u)

            act.wait_ge(s_var2, 1)
            A.activation(var[:, :], var[:, :], ACT.Sqrt, bias=eps[0:NP, :], scale=1.0 / F).then_inc(s_std2, 1)
            act.wait_ge(s_ln2, NT + 1)
            with act.Fori(0, NT) as t:
                A.activation(yn[:, DS(t, 1), :].rearrange("p a f -> p (a f)"), x_sb[:, DS(t, 1), :].rearrange("p a f -> p (a f)"),
                             ACT.Identity, bias=shift[:, DS(t, 1)], scale=rstd[:, DS(t, 1)]).then_inc(s_yn, 1)
            act.wait_ge(s_gap, 1)
            A.activation(share[:, 1, :], share[:, 1, :], ACT.Exp).then_inc(s_exp, 1)
            act.wait_ge(s_erow, 1)

            def hidden(j, u):
                e = act.value_load(erow[0:1, DS(j, 1)], min_val=0, max_val=X - 1)
                act.wait_ge(s_ffn, j + 1)
                for a in range(HA):
                    if a % 2 == 0:
                        act.wait_ge(s_l1, j * HA + a + 2 + 2 * HA)
                    A.activation(hT[:, u, a, :], ps[:, 2 + 4 * u + a // 2, (a % 2) * 128:(a % 2 + 1) * 128], ACT.Relu,
                                 bias=b1T[:, DS(e * HA + a, 1)]).then_inc(s_h, 1)

            with act.Fori(0, NCH - 2, 2) as j:
                for u in range(2):
                    hidden(j + u, u)
            hidden(NCH - 1, 0)

            with act.Fori(0, NT // GR) as g:
                act.wait_ge(s_v3, g * 10 + 7)
                A.activation(var[:, 0:GR], var[:, 0:GR], ACT.Sqrt, bias=eps[0:NP, :], scale=1.0 / F).then_inc(s_std3, 1)
                act.wait_ge(s_v3, g * 10 + 9)
                for u in range(GR):
                    A.activation(yn[:, DS(g * GR + u, 1), :].rearrange("p a f -> p (a f)"), yn[:, DS(g * GR + u, 1), :].rearrange("p a f -> p (a f)"),
                                 ACT.Identity, bias=shift[:, u:u + 1], scale=rstd[:, u:u + 1]).then_inc(s_norm, 1)

        @block.tensor
        def _(pe):
            T = nc.tensor
            HG = 10

            def count(q, g, start, stop):
                return T.matmul(psH.rearrange("p (j l) -> p j l", j=HJ),
                                hot_hi[q % 2][:, DS(g, 1), :, :].rearrange("p g v j -> p (g v j)"),
                                hot_lo[q % 2][:, :, DS(g * HJ, HJ)].rearrange("p v j -> p j v"), start=start, stop=stop)

            steps = HP // HJ
            for q in range(PIECES):
                pe.wait_ge(s_hot, q + 1)
                head = HG if q == 0 else 0
                for j in range(head):
                    count(q, j, j == 0, False)
                with pe.Fori(head, steps - 2 * HG + 1, HG) as j0:
                    for j in range(HG):
                        count(q, j0 + j, False, False)
                for j in range(steps - HG, steps):
                    last = count(q, j, False, q == PIECES - 1 and j == steps - 1)
                last.then_inc(s_hist, 1)
            pe.wait_ge(s_const, 11)
            pe.wait_ge(s_diag, 1)
            T.matmul(psC, fold[:, :], diag[:, :], start=True, stop=True).then_inc(s_folded, 1)
            pe.wait_ge(s_cnt, 1)
            T.matmul(psO, before[0:HH, 0:HH], incl[:, HL - 1:HL], start=True, stop=True)
            T.transpose(psM, most[:, :], ident[0:HH, 0:HH]).then_inc(s_base, 1)

            def turn(t, u, first=False):
                pe.wait_ge(s_xs, t + 1)
                if not first:
                    pe.wait_ge(s_lnE, t - 1)
                for a in range(FH):
                    last = T.transpose(ps[:, u, a * NP:(a + 1) * NP], xs[:, u, a * 128:(a + 1) * 128], ident[0:NP, 0:NP])
                last.then_inc(s_lnT, 1)

            for t in range(2):
                turn(t, t, True)
            with pe.Fori(2, NT - 1, 2) as t:
                for u in range(2):
                    turn(t + u, u)
            pe.wait_ge(s_lnE, NT)
            for lv in range(1, LEVELS + 1):
                b = keys[1 - kept[lv - 1]]
                for q in range(16):
                    if q % 4 == 0:
                        pe.wait_ge(s_signed, 4 * (lv - 1) + q // 4 + 1)
                    t = T.transpose(psT[:, q * 128:(q + 1) * 128], b[:, q * 128:(q + 1) * 128], ident[:, :])
                    if q % 4 == 3:
                        t.then_inc(s_T, 1)
                b = keys[kept2[lv - 1]]
                pe.wait_ge(s_Tdone, lv)
                for q in range(16):
                    t = T.transpose(psR[:, q * 128:(q + 1) * 128], b[:, q * 128:(q + 1) * 128], ident[:, :])
                    if q % 4 == 3:
                        t.then_inc(s_R, 1)
            pe.wait_ge(s_Tdone, LEVELS)


            pe.wait_ge(s_lo, NT)
            pe.wait_ge(s_listed, 2)
            pe.wait_ge(s_rounds, 1)
            rounds = pe.value_load(rnd[0:1, 4:5], min_val=1, max_val=521)
            pe.sem_inc(s_built, OR)
            pe.sem_inc(s_main, AR)
            pe.sem_inc(s_agg, 1)

            def build(n, u):
                pe.wait_ge(s_oh, n + 1)
                pe.wait_ge(s_at, n + 1)
                for k in range(K):
                    last = T.matmul(ps[0:NP, u % AR, 0:BN], ohd[:, u % OR, k, 0:NP], ohs[:, u % OR, k, :],
                                    start=k == 0, stop=k == K - 1)
                last.then_inc(s_built, 1)

            def add(n, D, u, start, stop):
                pe.wait_ge(s_at, n + 1 + AR)
                for a in range(FH):
                    for h, half in enumerate((xh, xl)):
                        last = T.matmul(ps[:, 2 + a, 0:BN],
                                        half[:, DS(D, 1), a * 128:(a + 1) * 128].rearrange("p a f -> p (a f)"),
                                        atn[:, u % AR, :], start=start and h == 0, stop=stop and h == 1)
                last.then_inc(s_main, 1)

            with pe.Fori(0, rounds) as r:
                with pe.Fori(0, NS) as S:
                    n = r * NB + S * NT
                    build(n, 0)
                    for u in range(1, GU):
                        build(n + u, u)
                        if u == 1:
                            pe.wait_ge(s_agg, r * NS + S + 1)
                        add(n + u - 1, u - 1, u - 1, u == 1, False)
                    with pe.Fori(GU, NT - GU + 1, GU) as D:
                        for u in range(GU):
                            build(n + D + u, u)
                            add(n + D + (u - 1), D + (u - 1), (u - 1) % GU, False, False)
                    add(n + NT - 1, NT - 1, (NT - 1) % GU, False, True)

            pe.wait_ge(s_w, 64)
            for a in range(HID // 128):
                for f in range(FH):
                    last = T.transpose(ps[:, 4 + a // 2, (a % 2) * 256 + f * 128:(a % 2) * 256 + (f + 1) * 128],
                                       w1s[:, f, a * 128:(a + 1) * 128], ident[:, :])
            last.then_inc(s_w1T, 1)
            pe.wait_ge(s_w1Te, 1)
            for f in range(FH):
                for a in range(HID // 128):
                    T.matmul(ps[:, 6, f * F:(f + 1) * F], w1T[:, a, f * 128:(f + 1) * 128], w2s[:, a, :],
                             start=a == 0, stop=a == HID // 128 - 1)
            for a in range(HID // 128):
                last = T.matmul(ps[0:1, 7, 0:F], b1c[:, a:a + 1], w2s[:, a, :], start=a == 0, stop=a == HID // 128 - 1)
            last.then_inc(s_wf, 1)
            pe.wait_ge(s_wfe, 1)
            pe.wait_ge(s_agg, rounds * NS + 1)

            def linear(t, u, first=False):
                pe.wait_ge(s_hst, t + 1)
                if not first:
                    pe.wait_ge(s_x1, t - 1)
                for a in range(FH):
                    T.matmul(ps[0:NP, u, 0:F], hst[:, u, a, :], wf[:, a, :], start=a == 0, stop=False)
                T.matmul(ps[0:NP, u, 0:F], ones[0:1, 0:NP], brow[:, :], start=False, stop=True).then_inc(s_lin, 1)

            for t in range(2):
                linear(t, t, True)
            with pe.Fori(2, NT - 1, 2) as t:
                for u in range(2):
                    linear(t + u, u)

            def gate_T(t, u):
                pe.wait_ge(s_yn, t + 1)
                for a in range(FH):
                    last = T.transpose(ps[:, u, a * NP:(a + 1) * NP],
                                       yn[:, DS(t, 1), a * 128:(a + 1) * 128].rearrange("p a f -> p (a f)"), ident[0:NP, 0:NP])
                last.then_inc(s_ynT, 1)

            def gate(t, u):
                pe.wait_ge(s_ynE, t + 1)
                for a in range(FH):
                    last = T.matmul(ps[0:NP, 2 + t // 32, (t % 32) * X:(t % 32 + 1) * X], ynT[:, u, a, :], gw[:, a, :],
                                    start=a == 0, stop=a == FH - 1)
                last.then_inc(s_lg, 1)

            pe.wait_ge(s_x1, NT)
            pe.wait_ge(s_gw, 32)
            gate_T(0, 0)
            for t in range(1, NT):
                gate_T(t, t % 2)
                gate(t - 1, (t - 1) % 2)
            gate(NT - 1, (NT - 1) % 2)

            pe.wait_ge(s_con2, 4)
            pe.wait_ge(s_chosen, 1)
            for b in range(4):
                T.matmul(ps[0:NP, b, 0:400], before16[:, :], chosen16[:, b * 400:(b + 1) * 400], start=True, stop=True)
                last = T.matmul(ps[0:NP, 4 + b, 0:400], ones16[:, :], chosen16[:, b * 400:(b + 1) * 400], start=True, stop=True)
            last.then_inc(s_rank, 1)
            pe.wait_ge(s_b1r, 16)
            pe.wait_ge(s_pos, 1)
            T.transpose(ps[:, 7, 448:448 + X * HA], b1r, ident[0:X * HA, 0:X * HA]).then_inc(s_b1T, 1)

            pe.wait_ge(s_erow, 1)
            pe.sem_inc(s_ffn, 2)

            def chunk_T(j, u, pair):
                pe.wait_ge(s_wt[u], pair * 64 + 64)
                for a in range(FH):
                    last = T.transpose(ps[:, u, a * 128:(a + 1) * 128], xr[:, u, a * 128:(a + 1) * 128], ident[:, :])
                last.then_inc(s_ct, 1)

            def up(j, u):
                pe.wait_ge(s_xT, j + 1)
                for m in range(HA):
                    for a in range(FH):
                        last = T.matmul(ps[:, 2 + 4 * u + m // 2, (m % 2) * 128:(m % 2 + 1) * 128], wt1[:, u, a, m * 128:(m + 1) * 128], xT[:, u, a, :],
                                        start=a == 0, stop=a == FH - 1)
                    last.then_inc(s_l1, 1)

            def down(j, u):
                pe.wait_ge(s_eo, j + 1)
                for m in range(HA):
                    pe.wait_ge(s_h, j * HA + m + 1)
                    last = T.matmul(ps[:, 4 + u, 0:F], hT[:, u, m, :], wt2[:, u, m, :], start=m == 0, stop=m == HA - 1)
                last.then_inc(s_ffn, 1)

            chunk_T(0, 0, 0)
            up(0, 0)
            with pe.Fori(0, NCH // 2) as g:
                chunk_T(g * 2 + 1, 1, g)
                down(g * 2, 0)
                up(g * 2 + 1, 1)
                chunk_T(g * 2 + 2, 0, g + 1)
                down(g * 2 + 1, 1)
                up(g * 2 + 2, 0)
            down(NCH - 1, 0)


_INS = ['x', 'src', 'dst', 'L0_gnn_W1', 'L0_gnn_b1', 'L0_gnn_W2', 'L0_gnn_b2', 'L0_ffn_gate_w', 'L0_ffn_gate_b',
        'L0_ffn_w1', 'L0_ffn_b1', 'L0_ffn_w2', 'L0_ffn_b2', 'L0_ffn_gamma', 'L0_ffn_beta']
_OUTS = [((6250, 256), 'float32')]


def kernel(**inputs):
    import numpy as _np
    import concourse.bacc as _bacc
    from concourse import mybir as _mybir
    from concourse.bass_utils import run_bass_kernel_spmd as _run
    nc = _bacc.Bacc("TRN2", target_bir_lowering=False, num_devices=1)
    arrays, args, outs = {}, [], []
    for name in _INS:
        a = _np.ascontiguousarray(inputs[name])
        arrays[f"in_{name}_dram"] = a
        args.append(nc.dram_tensor(f"in_{name}_dram", a.shape, _mybir.dt.from_np(a.dtype), kind="ExternalInput").ap())
    for i, (shape, dtype) in enumerate(_OUTS):
        dt = _mybir.dt.from_np(_np.dtype(dtype))
        outs.append(nc.dram_tensor(f"out_{i}_dram", shape, dt, kind="ExternalOutput").ap())
    list_d = nc.dram_tensor("list_d", (262144, 2), _mybir.dt.float32, kind="Internal").ap()
    off_d = nc.dram_tensor("off_d", (672,), _mybir.dt.int32, kind="Internal").ap()
    slots_d = nc.dram_tensor("slots_d", (113 * 128, 256), _mybir.dt.float32, kind="Internal").ap()
    eo_d = nc.dram_tensor("eo_d", (113 * 128, 256), _mybir.dt.float32, kind="Internal").ap()
    prog(nc, *args, outs[0], list_d, off_d, slots_d, eo_d)
    r = _run(nc, [arrays], core_ids=[0])
    return r.results[0]["out_0_dram"]
```

```python
import concourse.bass as bass
from concourse import mybir
from contextlib import ExitStack


def prog(nc, x, src, dst, W1, b1, W2, b2, gate_w, gate_b, ew1, eb1, ew2, eb2, gamma, beta, out, list_d, off_d, slots_d, eo_d, xb_d, yn_d):
    fp32, fp16, i32 = mybir.dt.float32, mybir.dt.float16, mybir.dt.int32
    ALU, ACT, AX = mybir.AluOpType, mybir.ActivationFunctionType, mybir.AxisListType
    DS = bass.ds

    N, F = x.shape
    E = src.shape[0]
    HID = W1.shape[1]
    NP, NT = 125, 50
    BT = 4
    BN = BT * NP
    NS = -(-NT // BT)
    NB = NS * NT
    EC = E // NP
    C = 2048
    LEVELS = 7
    BASE = 128
    SENTINEL = (NB + 50 + BASE) << 16
    K = 3
    WIN = 128 * K
    LAST_START = 128 * C - WIN
    HH, HL = 21, 32
    HP = 400
    PIECES = EC // HP
    UP = 2.0 ** 11
    GU = 10
    OR = 5
    AR = 2
    HJ = 4
    EPS = 1e-5
    X, EH = ew1.shape[0], ew1.shape[2]
    KT = 2 * NT
    NCH = (KT * NP + X * 127) // 128
    HA = EH // 128
    GR = 5
    FH = F // 128
    LR = 4

    kept, kept2 = [], []

    ctx = ExitStack()
    with ctx:
        def sb(name, shape, dt):
            return ctx.enter_context(nc.sbuf_tensor(name, shape, dt))

        def sem(name):
            return ctx.enter_context(nc.semaphore(name))

        XN, XS = FH * NS * BN, NT * F
        arena = sb("arena", [128, XN + 2 * XS], fp32)
        xnT = arena[:, 0:XN].rearrange("p (a n) -> p a n", a=FH)
        x_sb = arena[0:NP, XN:XN + XS].rearrange("p (t f) -> p t f", t=NT)
        halves = arena[:, XN + XS:].bitcast(fp16).rearrange("p (a n) -> p a n", a=2)
        xh = halves[0:NP, 0, :].rearrange("p (t f) -> p t f", t=NT)
        xl = halves[0:NP, 1, :].rearrange("p (t f) -> p t f", t=NT)
        scratch = halves[0:NP, :, :].rearrange("p a n -> p (a n)").bitcast(i32)
        edges = [scratch[:, i * EC:(i + 1) * EC] for i in range(8)]
        srcs, dsts, ta, tb, tc, td, te, tf = edges
        hots = [m[0:NP, :, :].rearrange("p a n -> p (a n)").bitcast(fp16)[:, 0:(HH + HL) * HP]
                for m in (xnT, halves)]
        hot_hi = [h[:, 0:HH * HP].rearrange("p (g v j) -> p g v j", v=HH, j=HJ) for h in hots]
        hot_lo = [h[:, HH * HP:].rearrange("p (v j) -> p v j", j=HP) for h in hots]
        keys = [sb(f"keys{i}", [128, C], fp32) for i in range(2)]
        listed = sb("listed", [128, C, 2], fp32)
        digits = listed[0:NP, :, :].rearrange("p c w -> p (c w)").bitcast(fp16)
        hi16, lo16 = digits[:, 0:EC], digits[:, EC:2 * EC]
        upper = listed[:, 0:C // 4, :].rearrange("p c w -> p (c w)")
        ident = sb("ident", [128, 128], fp32)
        rown = sb("rown", [128, 1], i32)
        bit = sb("bit", [128, 1], i32)
        sign = sb("sign", [128, LEVELS + 1], fp32)
        toggle = sb("toggle", [128, LEVELS + 1], fp32)
        before = sb("before", [128, 128], fp32)
        cube = sb("cube", [HJ * HH, HH, HJ], fp32)
        same = sb("same", [HJ * HH, HJ], fp32)
        fold = sb("fold", [HJ * HH, HH], fp32)
        crossed = sb("crossed", [HJ * HH, HJ, HL], fp32)
        diag = sb("diag", [HJ * HH, HL], fp32)
        stats = sb("stats", [NP, NT, 6], fp32)
        mean = sb("mean", [NP, NT], fp32)
        var = sb("var", [NP, NT], fp32)
        rstd = sb("rstd", [NP, NT], fp32)
        shift = sb("shift", [NP, NT], fp32)
        eps = sb("eps", [128, 1], fp32)
        squares = sb("squares", [128, 4 * X + 1], fp32)
        bound = sb("bound", [128, 4], fp32)
        expo = sb("expo", [128, 4], i32)
        up2 = sb("up2", [128, 4], fp32)
        down2 = sb("down2", [128, 4], fp32)
        back = sb("back", [128, 2], fp32)
        rows = sb("rows", [128, 2, F], fp32)
        xs = rows[0:NP, :, :]
        hst = rows[:, :, 0:FH * NP].rearrange("p u (a n) -> p u a n", a=FH)
        ohs = (listed[:, :, :].rearrange("p c w -> p (c w)").bitcast(fp16)[:, 0:OR * K * BN]
               .rearrange("p (o k n) -> p o k n", o=OR, k=K))
        small = sb("small", [128, OR * K * 64], fp32)
        ohd = small[:, :].bitcast(fp16).rearrange("p (o k n) -> p o k n", o=OR, k=K)
        zeros = small[:, 0:F]
        sqs = [small[:, 0:HID], rows[:, :, :].rearrange("p u n -> p (u n)")]
        atn = sb("atn", [NP, AR, BN], fp16)
        win = sb("win", [128, GU, K, 2], fp32)
        rel = sb("rel", [128, 2, K], fp32)
        firsts = sb("firsts", [128, NB], fp32)
        places = sb("places", [128, BN], fp16)
        wf = sb("wf", [128, FH, F], fp32)
        w1s = keys[0][:, 0:FH * HID].rearrange("p (a n) -> p a n", a=FH)
        w2s = keys[1][:, 0:FH * HID].rearrange("p (a n) -> p a n", a=HID // 128)
        w1T = keys[0][:, FH * HID:2 * FH * HID].rearrange("p (a n) -> p a n", a=HID // 128)
        b1c = sb("b1c", [128, HID // 128], fp32)
        brow = sb("brow", [1, F], fp32)
        b2r = sb("b2r", [1, F], fp32)
        ones = sb("ones", [1, 128], fp32)
        cnt = sb("cnt", [HH, HL], fp32)
        incl = sb("incl", [HH, HL], fp32)
        offf = sb("offf", [HH, HL], fp32)
        offi = sb("offi", [HH, HL], i32)
        most = sb("most", [HH, 1], fp32)
        rnd = sb("rnd", [1, 8], i32)
        offrow = sb("offrow", [1, HH * HL], i32)

        yn = halves[0:NP, :, :].rearrange("p a n -> p (a n)").bitcast(fp32).rearrange("p (t f) -> p t f", t=NT)
        area = xnT[:, :, :].rearrange("p a n -> p (a n)")
        at = [0]

        def carve(n, rows=128):
            at[0] += n
            return area[0:rows, at[0] - n:at[0]]

        wb2 = carve(LR * F).rearrange("p (u n) -> p u n", u=LR)
        xr = carve(LR * F).rearrange("p (u n) -> p u n", u=LR)
        xT = carve(2 * F).bitcast(fp16).rearrange("p (u h a n) -> p u h a n", u=2, h=2, a=FH)
        hs = carve(2 * EH).rearrange("p (u n) -> p u n", u=2)
        hT = carve(2 * EH).bitcast(fp16).rearrange("p (u h n) -> p u h n", u=2, h=2)
        eo = carve(2 * F).rearrange("p (u n) -> p u n", u=2)
        logits = area[0:NP, 0:NT * X].rearrange("p (t e) -> p t e", e=X)
        masked = area[0:NP, 800:800 + NT * X].rearrange("p (t e) -> p t e", e=X)
        chosen16 = area[0:NP, 1600:1600 + KT * X // 2].bitcast(fp16)
        ones128 = area[:, 2400:2528]
        WN = FH * EH + HA * F
        wts = arena[:, XN + 2 * XS - X * WN:].bitcast(fp16).rearrange("p (e h n) -> p e h n", e=X, h=2)
        staged = [k[:, 0:WN] for k in keys]
        b1T = carve(X * HA)
        assert at[0] + 128 + 2 * F <= XN + 2 * XS - X * WN
        b1r = carve(128, X * HA)
        chosen = keys[0][0:NP, 0:KT * X].rearrange("p (e k) -> p e k", e=X)
        total = keys[1][0:NP, 0:KT * X].rearrange("p (e k) -> p e k", e=X)
        lst = listed[0:NP, :, :].rearrange("p c w -> p (c w)")
        upto = lst[:, 0:KT * X].rearrange("p (e k) -> p e k", e=X)
        place = lst[:, 2048:2048 + KT * X].rearrange("p (e k) -> p e k", e=X)
        gw = sb("gw", [128, FH, X], fp32)
        gb = sb("gb", [NP, X], fp32)
        eix = sb("eix", [NP, X], fp32)
        eix64 = sb("eix64", [NP, X], fp32)
        used = [0]

        def take(*shape, dt=fp32):
            n = shape[0] if len(shape) == 1 else shape[0] * shape[1]
            used[0] += n
            flat = small[0:NP, used[0] - n:used[0]]
            flat = flat if dt is fp32 else flat.bitcast(dt)
            return flat if len(shape) == 1 else flat.rearrange("p (a b) -> p a b", a=shape[0])

        before16 = sb("before16", [NP, NP], fp16)
        ones16 = sb("ones16", [NP, NP], fp16)
        best = take(2, NT)
        which = take(2, NT)
        share = take(2, NT)
        nexp = take(X, dt=i32)
        padded = take(X)
        padend = take(X)
        adjust = take(X)
        posf = take(KT)
        posi = take(KT, dt=i32)
        erow = take(NCH, dt=i32)[0:1, :]
        erowf = take(NCH)[0:1, :]
        gam = carve(F, NP)
        bet = carve(F, NP)
        ynT = hst
        reach = listed[0:1, :, :].rearrange("p c w -> p (c w)")[:, 0:NCH * X].rearrange("p (j e) -> p j e", e=X)
        got = lst[:, 0:GR * 2 * F].rearrange("p (g k n) -> p g k n", g=GR, k=2)
        started = keys[1][0:1, 0:NCH * X].rearrange("p (j e) -> p j e", e=X)

        ps = ctx.enter_context(nc.psum_tensor("ps", [128, 8, 512], fp32))
        psT = ps[:, 0:4, :].rearrange("p a n -> p (a n)")
        psR = ps[:, 4:8, :].rearrange("p a n -> p (a n)")
        psH = ps[0:HJ * HH, 7, 0:HJ * HL]
        psC = ps[0:HH, 4, 0:HL]
        psO = ps[0:HH, 6, 0:1]
        psM = ps[0:1, 5, 0:HH]

        s_src, s_dst = sem("s_src"), sem("s_dst")
        s_const = sem("s_const")
        s_chain = sem("s_chain")
        s_hot = sem("s_hot")
        s_hist = sem("s_hist")
        s_cnt, s_base, s_mx, s_mxT, s_rounds = sem("s_cnt"), sem("s_base"), sem("s_mx"), sem("s_mxT"), sem("s_rounds")
        s_offi, s_offd, s_offrow = sem("s_offi"), sem("s_offd"), sem("s_offrow")
        s_rows, s_signed, s_T, s_Tdone, s_R = sem("s_rows"), sem("s_signed"), sem("s_T"), sem("s_Tdone"), sem("s_R")
        s_Tup, s_Rup = sem("s_Tup"), sem("s_Rup")
        s_listed, s_list, s_out = sem("s_listed"), sem("s_list"), sem("s_out")
        s_x, s_diag, s_folded = sem("s_x"), sem("s_diag"), sem("s_folded")
        s_var, s_std, s_ln = sem("s_var"), sem("s_std"), sem("s_ln")
        s_xs, s_hi, s_lo, s_lnT, s_lnE = sem("s_xs"), sem("s_hi"), sem("s_lo"), sem("s_lnT"), sem("s_lnE")
        s_win = [sem(f"s_win{u}") for u in range(GU)]
        s_winfree, s_rel, s_oh, s_built, s_at, s_main, s_agg = (
            sem(n) for n in ("s_winfree", "s_rel", "s_oh", "s_built", "s_at", "s_main", "s_agg"))
        s_started = sem("s_started")
        s_round, s_offnew, s_tabs = sem("s_round"), sem("s_offnew"), sem("s_tabs")
        s_w, s_w1T, s_w1Te, s_wf, s_wfe = sem("s_w"), sem("s_w1T"), sem("s_w1Te"), sem("s_wf"), sem("s_wfe")
        s_hst, s_lin, s_x1 = sem("s_hst"), sem("s_lin"), sem("s_x1")
        s_zero, s_z, s_gw, s_gam, s_con2 = sem("s_zero"), sem("s_z"), sem("s_gw"), sem("s_gam"), sem("s_con2")
        s_var2, s_std2, s_ln2, s_yn, s_ynT, s_ynE, s_lg = (
            sem(n) for n in ("s_var2", "s_std2", "s_ln2", "s_yn", "s_ynT", "s_ynE", "s_lg"))
        s_gap, s_exp, s_chosen, s_rank, s_pos, s_scat = (
            sem(n) for n in ("s_gap", "s_exp", "s_chosen", "s_rank", "s_pos", "s_scat"))
        s_erowi = sem("s_erowi")
        s_b1r, s_b1T, s_b1e, s_erow = sem("s_b1r"), sem("s_b1T"), sem("s_b1e"), sem("s_erow")
        s_xld = [sem(f"s_xld{u}") for u in range(LR)]
        s_ct, s_xh, s_xl, s_l1, s_hs, s_hh, s_hl, s_ffn, s_eo = (
            sem(n) for n in ("s_ct", "s_xh", "s_xl", "s_l1", "s_hs", "s_hh", "s_hl", "s_ffn", "s_eo"))
        s_sqld = [sem(f"s_sqld{u}") for u in range(2)]
        s_sq, s_sum, s_bound, s_root, s_scales = (sem(n) for n in ("s_sq", "s_sum", "s_bound", "s_root", "s_scales"))
        s_stg = [sem(f"s_stg{u}") for u in range(2)]
        s_whi, s_wlo, s_parked, s_back = sem("s_whi"), sem("s_wlo"), sem("s_parked"), sem("s_back")
        s_store = [sem(f"s_store{u}") for u in range(2)]
        s_got = [sem(f"s_got{u}") for u in range(GR)]
        s_used, s_y, s_v3, s_std3, s_sh3, s_norm, s_fin, s_xb = (
            sem(n) for n in ("s_used", "s_y", "s_v3", "s_std3", "s_sh3", "s_norm", "s_fin", "s_xb"))
        block = ctx.enter_context(nc.Block())

        @block.gpsimd
        def _(pool):
            nc.gpsimd.memset(ident[:, :], 0.0).then_inc(s_const, 1)
            nc.gpsimd.memset(zeros[:, :], 0.0).then_inc(s_z, 1)
            nc.gpsimd.memset(before[:, :], 1.0).then_inc(s_const, 1)
            pool.wait_ge(s_const, 2)
            nc.gpsimd.affine_select(out=ident[:, :], in_=ident[:, :], compare_op=ALU.not_equal, fill=1.0,
                                    base=0, pattern=[[-1, 128]], channel_multiplier=1).then_inc(s_const, 1)
            nc.gpsimd.affine_select(out=before[:, :], in_=before[:, :], compare_op=ALU.is_gt, fill=0.0,
                                    base=0, pattern=[[1, 128]], channel_multiplier=-1).then_inc(s_const, 1)
            nc.gpsimd.iota(rown[:, :], pattern=[[0, 1]], base=0, channel_multiplier=1).then_inc(s_const, 1)
            nc.gpsimd.memset(cube[:, :, :], 0.0).then_inc(s_const, 1)
            nc.gpsimd.memset(eps[:, :], EPS).then_inc(s_const, 1)
            nc.gpsimd.memset(ones[:, :], 1.0).then_inc(s_const, 1)
            pool.wait_ge(s_const, 8)
            nc.gpsimd.affine_select(out=cube[:, :, :], in_=cube[:, :, :], compare_op=ALU.not_equal, fill=1.0,
                                    base=0, pattern=[[-HJ, HH], [-1, HJ]], channel_multiplier=1).then_inc(s_const, 1)
            nc.gpsimd.iota(places[:, :], pattern=[[1, BN]], base=0, channel_multiplier=0,
                           allow_small_or_imprecise_dtypes=True).then_inc(s_const, 1)
            nc.gpsimd.iota(firsts[:, :], pattern=[[512, NB]], base=512 * BASE, channel_multiplier=0,
                           allow_small_or_imprecise_dtypes=True).then_inc(s_const, 1)

            def low_half(t, u):
                pool.wait_ge(s_hi, t + 1)
                nc.gpsimd.tensor_tensor(xl[:, DS(t, 1), :].rearrange("p a f -> p (a f)"), xs[:, u, :],
                                        xh[:, DS(t, 1), :].rearrange("p a f -> p (a f)"), ALU.subtract).then_inc(s_lo, 1)

            with pool.Fori(0, NT - 1, 2) as t:
                for u in range(2):
                    low_half(t + u, u)

            nc.gpsimd.iota(eix[:, :], pattern=[[1, X]], base=0, channel_multiplier=0,
                           allow_small_or_imprecise_dtypes=True).then_inc(s_con2, 1)
            nc.gpsimd.iota(eix64[:, :], pattern=[[1, X]], base=64, channel_multiplier=0,
                           allow_small_or_imprecise_dtypes=True).then_inc(s_con2, 1)
            nc.gpsimd.tensor_copy(before16[:, :], before[0:NP, 0:NP]).then_inc(s_con2, 1)
            nc.gpsimd.memset(ones16[:, :], 1.0).then_inc(s_con2, 1)

            pool.wait_ge(s_gam, 32)
            pool.wait_ge(s_yn, NT)
            with pool.Fori(0, NT) as t:
                nc.gpsimd.tensor_tensor(x_sb[:, DS(t, 1), :].rearrange("p a f -> p (a f)"),
                                        x_sb[:, DS(t, 1), :].rearrange("p a f -> p (a f)"), bet[:, :], ALU.add
                                        ).then_inc(s_xb, 1)

            pool.wait_ge(s_pos, 1)
            nc.gpsimd.iota(started, pattern=[[128, NCH], [0, X]], base=0, channel_multiplier=0,
                           allow_small_or_imprecise_dtypes=True).then_inc(s_erowi, 1)

            pool.wait_ge(s_zero, 16)
            for c in range(KT):
                nc.gpsimd.indirect_dma_start(
                    out=slots_d, out_offset=bass.IndirectOffsetOnAxis(ap=posi[:, c:c + 1], axis=0),
                    in_=yn[:, c % NT, :], in_offset=None).then_inc(s_scat, 16)

            def store(j, u):
                pool.wait_ge(s_eo, j + 1 + LR)
                pool.dma_start(eo_d[DS(j * 128, 128), :], eo[:, u, :]).then_inc(s_store[u], 16)

            with pool.Fori(0, NCH - 2, 2) as j:
                for u in range(2):
                    store(j + u, u)
            store(NCH - 1, 0)
            pool.wait_ge(s_store[0], 16 * (NCH // 2 + 1))
            pool.wait_ge(s_store[1], 16 * (NCH // 2))
            for t in range(NT):
                if t >= GR:
                    pool.wait_ge(s_used, t - GR + 1)
                for k in range(2):
                    nc.gpsimd.indirect_dma_start(
                        out=got[:, t % GR, k, :], out_offset=None, in_=eo_d,
                        in_offset=bass.IndirectOffsetOnAxis(ap=posi[:, k * NT + t:k * NT + t + 1], axis=0)
                        ).then_inc(s_got[t % GR], 16)

        @block.sync
        def _(sp):
            sp.dma_start(dsts, dst.rearrange("(p j) -> p j", p=NP)).then_inc(s_dst, 16)
            sp.dma_start(srcs, src.rearrange("(p j) -> p j", p=NP)).then_inc(s_src, 16)
            sp.dma_start(x_sb[:, :, :], x.rearrange("(p t) f -> p t f", t=NT)).then_inc(s_x, 16)
            sp.dma_start(gw[:, :, :], gate_w.rearrange("(a p) e -> p a e", p=128)).then_inc(s_gw, 16)
            sp.dma_start(gb[:, :], gate_b.rearrange("(a n) -> a n", a=1).to_broadcast([NP, X])).then_inc(s_gw, 16)
            sp.wait_ge(s_z, 1)
            sp.dma_start(slots_d.rearrange("(j p) f -> p j f", p=128),
                         zeros[:, :].rearrange("p (a f) -> p a f", a=1).to_broadcast([128, NCH, F])).then_inc(s_zero, 16)
            sp.wait_ge(s_offi, 1)
            sp.dma_start(off_d.rearrange("(h l) -> h l", h=HH), offi[:, :]).then_inc(s_offd, 16)
            sp.wait_ge(s_offd, 16)
            sp.dma_start(offrow[:, :], off_d.rearrange("(a n) -> a n", a=1)).then_inc(s_offrow, 16)
            sp.wait_ge(s_offrow, 16)

            def weigh(w, e, lo):
                for a in range(2):
                    sp.wait_ge(s_sq, 2 * (lo + e) + a + 1)
                    sp.dma_start(sqs[a], w[DS(e, 1), a * w.shape[1] // 2:(a + 1) * w.shape[1] // 2, :].rearrange(
                        "e (p c) n -> p (e c n)", p=128)).then_inc(s_sqld[a], 16)

            sp.wait_ge(s_zero, 16)
            sp.wait_ge(s_lnT, NT)
            sp.wait_ge(s_lo, NT)
            with sp.Fori(0, X) as e:
                weigh(ew1, e, 0)
            with sp.Fori(0, X) as e:
                weigh(ew2, e, X)
            sp.wait_ge(s_sq, 4 * X + 1)
            sp.dma_start(sqs[0][:, 0:X * HA], eb1.rearrange("e (c n) -> (e c) n", c=128 // X)
                         ).then_inc(s_sqld[0], 16)
            sp.wait_ge(s_listed, 2)
            sp.dma_start(list_d.rearrange("(p c) w -> p (c w)", p=128), listed[:, :, :].rearrange("p c w -> p (c w)")).then_inc(s_list, 16)
            sp.wait_ge(s_list, 16)
            sp.dma_start(w1s, W1.rearrange("(a p) n -> p a n", p=128)).then_inc(s_w, 16)
            sp.dma_start(w2s, W2.rearrange("(a p) n -> p a n", p=128)).then_inc(s_w, 16)
            with nc.allow_non_contiguous_dma(reason="512 numbers, once"):
                sp.dma_start(b1c[:, :], b1.rearrange("(a p) -> p a", p=128)).then_inc(s_w, 16)
            sp.dma_start(b2r[:, :], b2.rearrange("(a n) -> a n", a=1)).then_inc(s_w, 16)
            sp.wait_ge(s_rounds, 1)
            rounds = sp.value_load(rnd[0:1, 4:5], min_val=1, max_val=521)
            with sp.Fori(0, rounds) as r:
                sp.wait_ge(s_offnew, r + 1)
                sp.sem_inc(s_started, 1)
                with sp.Fori(0, NS * NT // GU) as g:
                    _, starts = nc.values_load_multi_w_load_instructions(
                        offrow[0:1, DS(g * GU, GU)], engines=[mybir.EngineType.SP], min_val=0, max_val=LAST_START)
                    for u in range(GU):
                        sp.wait_ge(s_winfree, (r * (NS * NT // GU) + g) * GU + u + 1)
                        sp.dma_start(win[:, u, :, :].rearrange("p k w -> p (k w)"),
                                     list_d[DS(starts[u], WIN), :].rearrange("(p k) w -> p (k w)", p=128)
                                     ).then_inc(s_win[u], 16)
                sp.drain().then_inc(s_round, 1)
            sp.wait_ge(s_hst, NT)
            sp.dma_start(gam[:, :], gamma.rearrange("(a n) -> a n", a=1).to_broadcast([NP, F])).then_inc(s_gam, 16)
            sp.dma_start(bet[:, :], beta.rearrange("(a n) -> a n", a=1).to_broadcast([NP, F])).then_inc(s_gam, 16)
            sp.dma_start(b1r, eb1.rearrange("e (a n) -> (e a) n", a=HA)).then_inc(s_b1r, 16)
            sp.wait_ge(s_erow, 1)
            sp.wait_ge(s_scales, 1)
            sp.wait_ge(s_yn, NT)
            sp.dma_start(yn_d.rearrange("(p t) f -> p t f", t=NT), yn).then_inc(s_parked, 16)
            sp.wait_ge(s_xb, NT)
            sp.dma_start(xb_d.rearrange("(p t) f -> p t f", t=NT), x_sb).then_inc(s_parked, 16)
            sp.wait_ge(s_parked, 32)

            def stage_weights(e, u):
                sp.wait_ge(s_wlo, e + 1)
                sp.dma_start(staged[u][:, 0:FH * EH].rearrange("p (a n) -> p a n", a=FH),
                             ew1[DS(e, 1), :, :].rearrange("e (a p) n -> p (e a) n", p=128)).then_inc(s_stg[u], 16)
                sp.dma_start(staged[u][:, FH * EH:].rearrange("p (a n) -> p a n", a=HA),
                             ew2[DS(e, 1), :, :].rearrange("e (a p) n -> p (e a) n", p=128)).then_inc(s_stg[u], 16)

            with sp.Fori(0, X // 2 - 1, 2) as e:
                for u in range(2):
                    stage_weights(e + u, u)
            sp.wait_ge(s_scat, 16 * KT)
            with sp.Fori(X // 2, X - 1, 2) as e:
                for u in range(2):
                    stage_weights(e + u, u)

            def load(j, u):
                e = sp.value_load(erow[0:1, DS(j, 1)], min_val=0, max_val=X - 1)
                sp.wait_ge(s_eo, j + 1)
                sp.sem_inc(s_started, 1)
                sp.dma_start(xr[:, u, :], slots_d[DS(j * 128, 128), :]).then_inc(s_xld[u], 16)
                sp.dma_start(wb2[:, u, :], eb2[DS(e, 1), :].to_broadcast([128, F])).then_inc(s_xld[u], 16)

            with sp.Fori(0, NCH - LR, LR) as j:
                for u in range(LR):
                    load(j + u, u)
            load(NCH - 1, 0)
            sp.wait_ge(s_ffn, NCH + 2)
            with sp.Fori(0, NT // GR) as g:
                sp.dma_start(yn[:, DS(g * GR, GR), :], yn_d.rearrange("(p t) f -> p t f", t=NT)[:, DS(g * GR, GR), :]
                             ).then_inc(s_back, 16)
                sp.dma_start(x_sb[:, DS(g * GR, GR), :], xb_d.rearrange("(p t) f -> p t f", t=NT)[:, DS(g * GR, GR), :]
                             ).then_inc(s_back, 16)
            with sp.Fori(0, NT // GR) as g:
                sp.wait_ge(s_fin, g + 1)
                sp.dma_start(out.rearrange("(p t) f -> p t f", t=NT)[:, DS(g * GR, GR), :],
                             yn[:, DS(g * GR, GR), :]).then_inc(s_out, 16)
            sp.wait_ge(s_out, 16 * (NT // GR))

        @block.vector
        def _(dve):
            V = nc.vector
            chain = [0]

            def link(ins):
                chain[0] += 1
                ins.then_inc(s_chain, 1)
                dve.wait_ge(s_chain, chain[0])

            def after(ins):
                chain[0] += 1
                ins.then_inc(s_chain, 1)

            def join():
                dve.wait_ge(s_chain, chain[0])

            V.memset(keys[0][:, :].bitcast(i32), SENTINEL).then_inc(s_chain, 1)
            chain[0] += 1
            dve.wait_ge(s_const, 11)
            for lv in range(LEVELS + 1):
                link(V.tensor_scalar(bit[:, :], rown[:, :], lv, 1, ALU.logical_shift_right, ALU.bitwise_and))
                link(V.tensor_scalar(sign[:, lv:lv + 1], bit[:, :], -2.0, 1.0, ALU.mult, ALU.add))
            link(V.tensor_tensor(toggle[:, 1:], sign[:, 0:LEVELS], sign[:, 1:], ALU.mult))

            def split(whole, quotient, rest, t1):
                link(V.tensor_scalar(t1, whole, 1, None, ALU.logical_shift_right))
                link(V.tensor_scalar(quotient, t1, 1311, None, ALU.mult))
                link(V.tensor_scalar(quotient, quotient, 15, None, ALU.logical_shift_right))
                link(V.scalar_tensor_tensor(rest, quotient, -NT, whole, ALU.mult, ALU.add))

            dve.wait_ge(s_dst, 16)
            split(dsts, ta, tb, tf)
            dve.wait_ge(s_src, 16)
            split(srcs, tc, td, tf)
            link(V.tensor_scalar(te, td, 3, None, ALU.bitwise_and))
            link(V.scalar_tensor_tensor(tc, te, NP, tc, ALU.mult, ALU.add))
            link(V.tensor_scalar(td, td, 2, None, ALU.logical_shift_right))
            link(V.scalar_tensor_tensor(td, td, NT, tb, ALU.mult, ALU.add))
            link(V.scalar_tensor_tensor(tc, tc, 128, ta, ALU.mult, ALU.add))
            after(V.tensor_scalar(ta, td, 5, None, ALU.logical_shift_right))
            after(V.tensor_scalar(tb, td, 31, None, ALU.bitwise_and))
            link(V.tensor_scalar(td, td, BASE, None, ALU.add))
            after(V.tensor_copy(hi16[:, :], ta))
            after(V.tensor_copy(lo16[:, :], tb))
            link(V.scalar_tensor_tensor(keys[0][0:NP, 0:EC].bitcast(i32), td, 16, tc,
                                        ALU.logical_shift_left, ALU.bitwise_or))
            link(V.tensor_scalar(keys[0][:, :], keys[0][:, :], sign[:, 0:1], None, ALU.mult))

            def digits_hot(q):
                if q >= 2:
                    dve.wait_ge(s_hist, q - 1)
                for v in range(HH):
                    V.tensor_scalar(hot_hi[q % 2][:, :, v, :], hi16[:, q * HP:(q + 1) * HP].rearrange("p (g j) -> p g j", j=HJ),
                                    float(v), None, ALU.is_equal)
                for v in range(HL):
                    last = V.tensor_scalar(hot_lo[q % 2][:, v, :], lo16[:, q * HP:(q + 1) * HP], float(v), None, ALU.is_equal)
                last.then_inc(s_hot, 1)

            def moments(s_stat, s_root, s_moment, scale):
                with dve.Fori(0, NT - 9, 10) as t:
                    for u in range(10):
                        V.bn_stats(stats[:, DS(t + u, 1), :].rearrange("p a s -> p (a s)"),
                                   x_sb[:, DS(t + u, 1), :].rearrange("p a f -> p (a f)")).then_inc(s_stat, 1)
                dve.wait_ge(s_stat, NT)
                link(V.tensor_tensor(mean[:, :], stats[:, :, 1], stats[:, :, 4], ALU.add))
                link(V.tensor_tensor(var[:, :], stats[:, :, 1], stats[:, :, 4], ALU.subtract))
                link(V.tensor_tensor(var[:, :], var[:, :], var[:, :], ALU.mult))
                link(V.tensor_tensor(shift[:, :], stats[:, :, 2], stats[:, :, 5], ALU.add))
                link(V.scalar_tensor_tensor(var[:, :], var[:, :], F / 4, shift[:, :], ALU.mult, ALU.add))
                V.tensor_scalar(mean[:, :], mean[:, :], -0.5 * scale, None, ALU.mult).then_inc(s_moment, 1)

            def factors(s_stat, s_root, scale):
                dve.wait_ge(s_root, 1)
                link(V.reciprocal(rstd[:, :], var[:, :]))
                link(V.tensor_tensor(shift[:, :], mean[:, :], rstd[:, :], ALU.mult))
                V.tensor_scalar(rstd[:, :], rstd[:, :], scale, None, ALU.mult).then_inc(s_stat, 1)

            def offsets():
                dve.wait_ge(s_hist, PIECES)
                after(V.tensor_reduce(same[:, :], cube[:, :, :].rearrange("p v j -> p j v"), AX.X, ALU.add))
                link(V.tensor_reduce(fold[:, :], cube[:, :, :], AX.X, ALU.add))
                link(V.tensor_tensor(crossed[:, :, :], psH.rearrange("p (j l) -> p j l", j=HJ),
                                     same[:, :].rearrange("p (j a) -> p j a", a=1).to_broadcast([HJ * HH, HJ, HL]), ALU.mult))
                link(V.tensor_reduce(diag[:, :], crossed[:, :, :].rearrange("p j l -> p l j"), AX.X, ALU.add))
                V.tensor_copy(bit[0:1, :], rown[0:1, :]).then_inc(s_diag, 1)
                dve.wait_ge(s_folded, 1)
                link(V.tensor_copy(cnt[:, :], psC))
                after(V.tensor_reduce(most[:, :], cnt[:, :], AX.X, ALU.max))
                link(V.tensor_tensor_scan(incl[:, :], cnt[:, :], cnt[:, :], 0.0, ALU.add, ALU.bypass))
                V.tensor_copy(bit[0:1, :], rown[0:1, :]).then_inc(s_cnt, 1)
                dve.wait_ge(s_base, 1)
                link(V.tensor_tensor(offf[:, :], incl[:, :], cnt[:, :], ALU.subtract))
                V.tensor_scalar(offi[:, :], offf[:, :], psO, None, ALU.add).then_inc(s_offi, 1)
                link(V.tensor_reduce(rnd[:, 0:1], psM, AX.X, ALU.max))
                link(V.tensor_scalar(rnd[:, 1:2], rnd[:, 0:1], WIN - 1, None, ALU.add))
                link(V.tensor_scalar(rnd[:, 2:3], rnd[:, 1:2], 7, None, ALU.logical_shift_right))
                link(V.tensor_scalar(rnd[:, 3:4], rnd[:, 2:3], 683, None, ALU.mult))
                V.tensor_scalar(rnd[:, 4:5], rnd[:, 3:4], 11, None, ALU.logical_shift_right).then_inc(s_rounds, 1)

            digits_hot(0)
            digits_hot(1)

            state = [0]

            def exchange(source, sz, k, both, other=None):
                join()
                target = keys[1 - state[0]]
                if both:
                    i, o = (a.rearrange("p (m d q w k) -> p m d q w k", d=2, q=sz // (2 * k), w=2, k=k)
                            for a in (source, target[:, :]))
                    for d in range(2):
                        a, b = i[:, :, d, :, 0, :], i[:, :, d, :, 1, :]
                        after(V.tensor_tensor(o[:, :, d, :, 0, :], a, b, ALU.max if d else ALU.min))
                        after(V.tensor_tensor(o[:, :, d, :, 1, :], a, b, ALU.min if d else ALU.max))
                else:
                    i, o = (a.rearrange("p (q w k) -> p q w k", w=2, k=k) for a in (source, target[:, :]))
                    a, b = i[:, :, 0, :], i[:, :, 1, :]
                    if other is not None:
                        b = other.rearrange("p (q k) -> p q k", k=k)
                    after(V.tensor_tensor(o[:, :, 0, :], a, b, ALU.min))
                    after(V.tensor_tensor(o[:, :, 1, :], a, b, ALU.max))
                state[0] = 1 - state[0]

            def now():
                return keys[state[0]][:, :]

            sz = 2
            while sz <= C:
                k = sz // 2
                while k:
                    exchange(now(), sz, k, sz < C)
                    k //= 2
                if sz == 16:
                    digits_hot(2)
                elif sz == 32:
                    dve.wait_ge(s_x, 16)
                    moments(s_ln, s_std, s_var, UP)
                elif sz == 64:
                    digits_hot(3)
                    factors(s_ln, s_std, UP)
                elif sz == 256:
                    offsets()
                sz *= 2
            for lv in range(1, LEVELS + 1):
                join()
                V.tensor_copy(bit[0:1, :], rown[0:1, :]).then_inc(s_rows, 1)
                kept.append(state[0])
                dve.wait_ge(s_T, 4 * lv)
                dve.wait_ge(s_Tup, 4 * lv)
                source = psT
                k = 2 ** (lv - 1)
                while k:
                    exchange(source, 2 * k, k, False, upper if source is psT else None)
                    source = now()
                    k //= 2
                join()
                V.tensor_copy(bit[0:1, :], rown[0:1, :]).then_inc(s_Tdone, 1)
                kept2.append(state[0])
                dve.wait_ge(s_R, 4 * lv)
                dve.wait_ge(s_Rup, 2 * lv)
                source = psR
                k = C // 2
                while k:
                    exchange(source, 2 * k, k, False, upper if source is psR else None)
                    source = now()
                    k //= 2
            join()
            a, b = keys[state[0]], keys[1 - state[0]]
            link(V.tensor_scalar(b[:, :].bitcast(i32), a[:, :].bitcast(i32), 7, None, ALU.logical_shift_right))
            V.tensor_copy(listed[:, :, 0], b[:, :].bitcast(i32)).then_inc(s_listed, 1)
            link(V.tensor_scalar(a[:, :].bitcast(i32), a[:, :].bitcast(i32), 127, None, ALU.bitwise_and))
            V.tensor_copy(listed[:, :, 1], a[:, :].bitcast(i32)).then_inc(s_listed, 1)
            dve.wait_ge(s_lnE, NT)
            link(V.memset(xnT[:, :, N:], 0.0))

            dve.wait_ge(s_offrow, 16)
            V.tensor_scalar(offrow[:, :], offrow[:, :], LAST_START, None, ALU.min).then_inc(s_offnew, 1)
            dve.wait_ge(s_rounds, 1)
            rounds = dve.value_load(rnd[0:1, 4:5], min_val=1, max_val=521)

            dve.sem_inc(s_winfree, GU)
            dve.wait_ge(s_list, 16)
            dve.wait_ge(s_sq, 4 * X + 3)
            with dve.Fori(0, rounds) as r:
                with dve.Fori(0, NS) as S:
                    with dve.Fori(0, NT // GU) as G:
                        b0 = (S * (NT // GU) + G) * GU
                        n0 = r * NB + b0
                        for u in range(GU):
                            dve.wait_ge(s_win[u], (r * (NB // GU) + S * (NT // GU) + G) * 16 + 16)
                            V.tensor_tensor(rel[:, u % 2, :], win[:, u, :, 0],
                                            firsts[:, DS(b0 + u, 1)].to_broadcast([128, K]), ALU.subtract).then_inc(s_rel, 1)
                            dve.wait_ge(s_built, n0 + u + 1)
                            for k in range(K):
                                V.tensor_scalar(ohd[:, u % OR, k, :], places[:, 0:128], win[:, u, k, 1:2], None, ALU.is_equal)
                            dve.wait_ge(s_rel, n0 + u + 1)
                            for k in range(K):
                                last = V.tensor_scalar(ohs[:, u % OR, k, :], places[:, :], rel[:, u % 2, k:k + 1], None, ALU.is_equal)
                            last.then_inc(s_oh, 1)
                            V.tensor_copy(bit[0:1, :], rown[0:1, :]).then_inc(s_winfree, 1)
                    dve.wait_ge(s_main, r * NB + S * NT + NT + AR)
                    V.scalar_tensor_tensor(xnT[:, :, DS(S * BN, BN)], ps[:, 2:4, 0:BN], 1.0 / UP,
                                           xnT[:, :, DS(S * BN, BN)], ALU.mult, ALU.add).then_inc(s_agg, 1)
                dve.wait_ge(s_round, r + 1)
                V.tensor_scalar(offrow[:, :], offrow[:, :], WIN, LAST_START, ALU.add, ALU.min).then_inc(s_offnew, 1)

            dve.wait_ge(s_w1T, 1)
            for a in range(HID // 128):
                last = V.tensor_copy(w1T[:, a, :], ps[:, 4 + a // 2, (a % 2) * 256:(a % 2) * 256 + 256])
            last.then_inc(s_w1Te, 1)
            dve.wait_ge(s_wf, 1)
            V.tensor_copy(wf[:, :, :], ps[:, 6, :].rearrange("p (a f) -> p a f", a=FH))
            V.tensor_tensor(brow[:, :], ps[0:1, 7, 0:F], b2r[:, :], ALU.add).then_inc(s_wfe, 1)
            with dve.Fori(0, NT - 1, 2) as t:
                for u in range(2):
                    dve.wait_ge(s_lin, t + u + 1)
                    V.tensor_tensor(x_sb[:, DS(t + u, 1), :].rearrange("p a f -> p (a f)"), ps[0:NP, u, 0:F],
                                    x_sb[:, DS(t + u, 1), :].rearrange("p a f -> p (a f)"), ALU.add).then_inc(s_x1, 1)

            dve.wait_ge(s_x1, NT)
            moments(s_ln2, s_std2, s_var2, 1.0)
            factors(s_ln2, s_std2, 1.0)

            def evacuate(t, u, first=False):
                dve.wait_ge(s_ynT, t + 1)
                if not first:
                    dve.wait_ge(s_lg, t - 1)
                V.tensor_copy(ynT[:, u, :, :], ps[:, u, 0:FH * NP].rearrange("p (a n) -> p a n", a=FH)).then_inc(s_ynE, 1)

            for t in range(2):
                evacuate(t, t, True)
            with dve.Fori(2, NT - 1, 2) as t:
                for u in range(2):
                    evacuate(t + u, u)

            dve.wait_ge(s_lg, NT)
            dve.wait_ge(s_con2, 4)
            dve.wait_ge(s_gw, 32)

            def over_tiles(a, n):
                return a.rearrange("p (t e) -> p t e", t=1).to_broadcast([NP, n, X])

            def over_experts(a):
                return a.rearrange("p (t e) -> p t e", e=1).to_broadcast([NP, NT, X])

            after(V.tensor_tensor(logits[:, 0:32, :], ps[0:NP, 2, :].rearrange("p (t e) -> p t e", e=X), over_tiles(gb[:, :], 32), ALU.add))
            link(V.tensor_tensor(logits[:, 32:, :], ps[0:NP, 3, 0:(NT - 32) * X].rearrange("p (t e) -> p t e", e=X), over_tiles(gb[:, :], NT - 32), ALU.add))
            values = logits
            for k in range(2):
                one = chosen[:, :, k * NT:(k + 1) * NT].rearrange("p e t -> p t e")
                link(V.tensor_reduce(best[:, k, :], values, AX.X, ALU.max))
                link(V.tensor_tensor(one, values, over_experts(best[:, k, :]), ALU.is_equal))
                link(V.scalar_tensor_tensor(one, one, -64.0, over_tiles(eix64[:, :], NT), ALU.mult, ALU.add))
                link(V.tensor_reduce(which[:, k, :], one, AX.X, ALU.min))
                link(V.tensor_tensor(one, over_tiles(eix[:, :], NT), over_experts(which[:, k, :]), ALU.is_equal))
                if k == 0:
                    link(V.scalar_tensor_tensor(masked, one, -3.0e38, logits, ALU.mult, ALU.add))
                    values = masked
            V.tensor_tensor(share[:, 1, :], best[:, 1, :], best[:, 0, :], ALU.subtract).then_inc(s_gap, 1)
            V.tensor_copy(chosen16, chosen.rearrange("p e k -> p (e k)")).then_inc(s_chosen, 1)
            dve.wait_ge(s_exp, 1)
            link(V.tensor_scalar(share[:, 0, :], share[:, 1, :], 1.0, None, ALU.add))
            link(V.reciprocal(share[:, 0, :], share[:, 0, :]))
            link(V.tensor_tensor(share[:, 1, :], share[:, 1, :], share[:, 0, :], ALU.mult))

            dve.wait_ge(s_rank, 1)
            link(V.tensor_copy(total.rearrange("p e k -> p (e k)").rearrange("p (b n) -> p b n", b=4), ps[0:NP, 4:8, 0:400]))
            flat = (total.rearrange("p e k -> p (e k)"), upto.rearrange("p e k -> p (e k)"))
            link(V.tensor_tensor_scan(flat[1], flat[0], flat[0], 0.0, ALU.add, ALU.bypass))
            link(V.tensor_tensor(total, upto, total, ALU.subtract))
            link(V.tensor_tensor(padded[:, :], upto[:, :, KT - 1], total[:, :, 0], ALU.subtract))
            link(V.tensor_scalar(nexp[:, :], padded[:, :], 127.0, None, ALU.add))
            link(V.tensor_scalar(nexp[:, :], nexp[:, :], 7, 7, ALU.logical_shift_right, ALU.logical_shift_left))
            link(V.tensor_copy(padded[:, :], nexp[:, :]))
            link(V.tensor_tensor_scan(padend[:, :], padded[:, :], padded[:, :], 0.0, ALU.add, ALU.bypass))
            link(V.tensor_tensor(adjust[:, :], padend[:, :], padded[:, :], ALU.subtract))
            link(V.tensor_tensor(adjust[:, :], adjust[:, :], total[:, :, 0], ALU.subtract))
            link(V.tensor_tensor(place.rearrange("p e k -> p (e k)").rearrange("p (b n) -> p b n", b=4), ps[0:NP, 0:4, 0:400],
                                 total.rearrange("p e k -> p (e k)").rearrange("p (b n) -> p b n", b=4), ALU.add))
            link(V.tensor_tensor(place, place, adjust[:, :].rearrange("p (e k) -> p e k", k=1).to_broadcast([NP, X, KT]), ALU.add))
            link(V.tensor_tensor(place, place, chosen, ALU.mult))
            link(V.tensor_reduce(posf[:, :], place.rearrange("p e k -> p k e"), AX.X, ALU.add))
            V.tensor_copy(posi[:, :], posf[:, :]).then_inc(s_pos, 1)
            link(V.memset(ones128, 1.0))
            dve.wait_ge(s_sq, 4 * X + 3)
            after(V.tensor_reduce(bound[:, 0:2], squares[:, 0:4 * X].rearrange("p (a n) -> p a n", a=2), AX.X, ALU.add))
            link(V.tensor_copy(bound[:, 2:3], squares[:, 4 * X:]))
            V.tensor_copy(bit[0:1, :], rown[0:1, :]).then_inc(s_bound, 1)
            dve.wait_ge(s_erowi, 1)
            link(V.tensor_tensor(reach, started, padend[0:1, :].rearrange("p (j e) -> p j e", j=1).to_broadcast([1, NCH, X]), ALU.is_ge))
            link(V.tensor_reduce(erowf[:, :], reach, AX.X, ALU.add))
            V.tensor_scalar(erow[:, :], erowf[:, :], X - 1, None, ALU.min).then_inc(s_erow, 1)

            dve.wait_ge(s_root, 1)
            link(V.scalar_tensor_tensor(bound[:, 2:3], bound[:, 0:1], 16.5, bound[:, 2:3], ALU.mult, ALU.add))
            link(V.tensor_scalar(bound[:, 0:3], bound[:, 0:3], 1e-20, None, ALU.max))
            link(V.tensor_scalar(expo[:, 0:3], bound[:, 0:3].bitcast(i32), 0x7F800000, None, ALU.bitwise_and))
            link(V.tensor_scalar(up2[:, 0:3].bitcast(i32), expo[:, 0:3], -1.0, 268.0 * 2 ** 23, ALU.mult, ALU.add))
            link(V.tensor_scalar(down2[:, 0:3].bitcast(i32), up2[:, 0:3].bitcast(i32), -1.0, 254.0 * 2 ** 23, ALU.mult, ALU.add))
            link(V.scalar_tensor_tensor(back[:, 0:1], up2[:, 2:3], 1.0 / UP, down2[:, 0:1], ALU.mult, ALU.mult))
            link(V.tensor_tensor(back[:, 1:2], down2[:, 2:3], down2[:, 1:2], ALU.mult))
            dve.wait_ge(s_b1T, 1)
            V.tensor_scalar(b1T, ps[:, 7, 448:448 + X * HA], up2[:, 2:3], None, ALU.mult).then_inc(s_scales, 1)

            dve.sem_inc(s_wlo, 2)

            def low(e, u, pair):
                dve.wait_ge(s_stg[u], pair * 32 + 32)
                for m, (a, b) in enumerate(((0, FH * EH), (FH * EH, WN))):
                    dve.wait_ge(s_whi, 2 * e + m + 1)
                    last = V.scalar_tensor_tensor(wts[:, DS(e, 1), 1, a:b].rearrange("p e n -> p (e n)"), staged[u][:, a:b],
                                                  up2[:, m:m + 1], wts[:, DS(e, 1), 0, a:b].rearrange("p e n -> p (e n)"),
                                                  ALU.mult, ALU.subtract)
                last.then_inc(s_wlo, 1)

            with dve.Fori(0, X // 2) as g:
                for u in range(2):
                    low(g * 2 + u, u, g)

            dve.sem_inc(s_l1, 2 * HA)
            dve.sem_inc(s_eo, LR)
            dve.sem_inc(s_hl, 4)

            def rows_T(j, u):
                dve.wait_ge(s_ct, j + 1)
                dve.wait_ge(s_l1, (j + 1) * HA)
                V.tensor_scalar(xT[:, u, 0, :, :], ps[:, u, 0:F].rearrange("p (a n) -> p a n", a=FH), UP, None, ALU.mult).then_inc(s_xh, 1)
                dve.wait_ge(s_xh, j + 1)
                V.scalar_tensor_tensor(xT[:, u, 1, :, :], ps[:, u, 0:F].rearrange("p (a n) -> p a n", a=FH), UP,
                                       xT[:, u, 0, :, :], ALU.mult, ALU.subtract).then_inc(s_xl, 1)

            def hidden_low(j, u):
                for m in range(2):
                    part = slice(m * EH // 2, (m + 1) * EH // 2)
                    dve.wait_ge(s_hh, 2 * j + m + 1)
                    V.tensor_tensor(hT[:, u, 1, part], hs[:, u, part], hT[:, u, 0, part], ALU.subtract).then_inc(s_hl, 1)

            def result(j, u, pair):
                dve.wait_ge(s_ffn, j + 1 + 2)
                if pair is not None:
                    dve.wait_ge(s_store[u % 2], pair * 16)
                V.scalar_tensor_tensor(eo[:, u % 2, :], ps[:, 4 + u % 2, 0:F], back[:, 1:2], wb2[:, u, :],
                                       ALU.mult, ALU.add).then_inc(s_eo, 1)

            rows_T(0, 0)
            rows_T(1, 1)
            hidden_low(0, 0)
            for j in range(LR):
                rows_T(j + 2, j % 2)
                hidden_low(j + 1, (j + 1) % 2)
                result(j, j, j // 2 if j >= 2 else None)
            with dve.Fori(1, (NCH - 2) // LR) as g:
                for u in range(LR):
                    rows_T(g * LR + u + 2, u % 2)
                    hidden_low(g * LR + u + 1, (u + 1) % 2)
                    result(g * LR + u, u, g * (LR // 2) + u // 2)
            for j in range((NCH - 2) // LR * LR, NCH):
                if j + 2 < NCH:
                    rows_T(j + 2, j % 2)
                if j + 1 < NCH:
                    hidden_low(j + 1, (j + 1) % 2)
                result(j, j % LR, j // 2)

            dve.wait_ge(s_gam, 32)
            def rows(t):
                return yn[:, DS(t, 1), :].rearrange("p a f -> p (a f)")

            def mix(g):
                dve.wait_ge(s_back, 32 * (NT // GR))
                cols = DS(g * GR, GR)
                for u in range(GR):
                    dve.wait_ge(s_got[u], g * 32 + 32)
                    V.scalar_tensor_tensor(rows(g * GR + u), got[:, u, 0, :], share[:, 0, DS(g * GR + u, 1)], rows(g * GR + u),
                                           ALU.mult, ALU.add).then_inc(s_y, 1)
                for u in range(GR):
                    dve.wait_ge(s_y, g * 2 * GR + u + 1)
                    V.scalar_tensor_tensor(rows(g * GR + u), got[:, u, 1, :], share[:, 1, DS(g * GR + u, 1)], rows(g * GR + u),
                                           ALU.mult, ALU.add).then_inc(s_y, 1)
                dve.wait_ge(s_y, g * 2 * GR + 2 * GR)
                dve.sem_inc(s_started, 1)
                for u in range(GR):
                    V.bn_stats(stats[:, u, :], rows(g * GR + u)).then_inc(s_used, 1)
                dve.wait_ge(s_used, g * GR + GR)
                V.tensor_tensor(mean[:, cols], stats[:, 0:GR, 1], stats[:, 0:GR, 4], ALU.add).then_inc(s_v3, 1)
                V.tensor_tensor(var[:, cols], stats[:, 0:GR, 1], stats[:, 0:GR, 4], ALU.subtract).then_inc(s_v3, 1)
                V.tensor_tensor(shift[:, cols], stats[:, 0:GR, 2], stats[:, 0:GR, 5], ALU.add).then_inc(s_v3, 1)
                dve.wait_ge(s_v3, g * 7 + 2)
                V.tensor_tensor(var[:, cols], var[:, cols], var[:, cols], ALU.mult).then_inc(s_v3, 1)
                dve.wait_ge(s_v3, g * 7 + 4)
                V.scalar_tensor_tensor(var[:, cols], var[:, cols], F / 4, shift[:, cols], ALU.mult, ALU.add).then_inc(s_v3, 1)
                dve.wait_ge(s_std3, g + 1)
                V.reciprocal(rstd[:, cols], var[:, cols]).then_inc(s_v3, 1)
                dve.wait_ge(s_v3, g * 7 + 6)
                V.scalar_tensor_tensor(shift[:, cols], mean[:, cols], -0.5, rstd[:, cols], ALU.mult, ALU.mult).then_inc(s_v3, 1)

            def finish(g):
                dve.wait_ge(s_norm, g * GR + GR)
                five = yn[:, DS(g * GR, GR), :]
                V.tensor_tensor(five, five, gam[:, :].rearrange("p (t f) -> p t f", t=1).to_broadcast([NP, GR, F]),
                                ALU.mult).then_inc(s_sh3, 1)
                dve.wait_ge(s_sh3, g + 1)
                V.tensor_tensor(five, five, x_sb[:, DS(g * GR, GR), :], ALU.add).then_inc(s_fin, 1)

            mix(0)
            with dve.Fori(1, NT // GR) as g:
                mix(g)
                finish(g - 1)
            finish(NT // GR - 1)

        @block.scalar
        def _(act):
            A = nc.scalar
            act.sem_inc(s_sq, 2)
            act.wait_ge(s_var, 1)
            act.wait_ge(s_const, 11)
            A.activation(var[:, :], var[:, :], ACT.Sqrt, bias=eps[0:NP, :], scale=1.0 / F).then_inc(s_std, 1)
            act.wait_ge(s_ln, NT + 1)
            act.wait_ge(s_hist, PIECES)

            def normalise(t, u, first=False):
                if not first:
                    act.wait_ge(s_lnT, t - 1)
                    act.wait_ge(s_lo, t - 1)
                A.activation(xs[:, u, :], x_sb[:, DS(t, 1), :].rearrange("p a f -> p (a f)"), ACT.Identity,
                             bias=shift[:, DS(t, 1)], scale=rstd[:, DS(t, 1)]).then_inc(s_xs, 1)
                act.wait_ge(s_xs, t + 1)
                A.activation(xh[:, DS(t, 1), :].rearrange("p a f -> p (a f)"), xs[:, u, :], ACT.Copy).then_inc(s_hi, 1)
                act.wait_ge(s_lnT, t + 1)
                A.activation(xnT[:, :, DS(t * NP, NP)], ps[:, u, 0:FH * NP].rearrange("p (a n) -> p a n", a=FH),
                             ACT.Copy, scale=1.0 / UP).then_inc(s_lnE, 1)

            for t in range(2):
                normalise(t, t, True)
            with act.Fori(2, NT - 1, 2) as t:
                for u in range(2):
                    normalise(t + u, u)
            for lv in range(1, LEVELS + 1):
                act.wait_ge(s_rows, lv)
                a, b = keys[kept[lv - 1]], keys[1 - kept[lv - 1]]
                for q in range(4):
                    nc.scalar.activation(b[:, q * 512:(q + 1) * 512], a[:, q * 512:(q + 1) * 512], ACT.Copy,
                                         scale=toggle[:, lv:lv + 1]).then_inc(s_signed, 1)
                k = 2 ** (lv - 1)
                for q in range(4):
                    act.wait_ge(s_T, 4 * (lv - 1) + q + 1)
                    nc.scalar.activation(upper[:, q * 256:(q + 1) * 256].rearrange("p (a k) -> p a k", k=k),
                                         ps[:, q, :].rearrange("p (a w k) -> p a w k", w=2, k=k)[:, :, 1, :],
                                         ACT.Copy).then_inc(s_Tup, 1)
                for q in range(2):
                    act.wait_ge(s_R, 4 * (lv - 1) + q + 3)
                    nc.scalar.activation(upper[:, q * 512:(q + 1) * 512], ps[:, 6 + q, :], ACT.Copy).then_inc(s_Rup, 1)
                first, last, base = [(0, 4, 0), (4, 8, 0), (8, 12, 0), (12, 16, 0), (0, 6, X), (6, 11, X), (11, 16, X)][lv - 1]
                with act.Fori(first, last) as e:
                    for a in range(2):
                        act.wait_ge(s_sqld[a], 16 * (e + base) + 16)
                        A.activation(sqs[a], sqs[a], ACT.Square, accum_out=squares[:, DS(2 * (e + base) + a, 1)]).then_inc(s_sq, 1)
            act.wait_ge(s_sqld[0], 16 * (2 * X + 1))
            A.activation(sqs[0][:, 0:X * HA], sqs[0][:, 0:X * HA], ACT.Square, accum_out=squares[:, 4 * X:]).then_inc(s_sq, 1)

            act.wait_ge(s_rounds, 1)
            rounds = act.value_load(rnd[0:1, 4:5], min_val=1, max_val=521)
            act.sem_inc(s_at, AR)
            with act.Fori(0, rounds) as r:
                with act.Fori(0, NB // GU) as g:
                    n0 = (r * (NB // GU) + g) * GU
                    for u in range(GU):
                        act.wait_ge(s_built, n0 + u + 1 + OR)
                        act.wait_ge(s_main, n0 + u + 1)
                        A.activation(atn[:, u % AR, :], ps[0:NP, u % AR, 0:BN], ACT.Copy).then_inc(s_at, 1)
            act.wait_ge(s_agg, rounds * NS + 1)

            def stage(t, u, first=False):
                if not first:
                    act.wait_ge(s_lin, t - 1)
                A.activation(hst[:, u, :, :], xnT[:, :, DS(t * NP, NP)], ACT.Copy).then_inc(s_hst, 1)

            for t in range(2):
                stage(t, t, True)
            with act.Fori(2, NT - 1, 2) as t:
                for u in range(2):
                    stage(t + u, u)

            act.wait_ge(s_var2, 1)
            A.activation(var[:, :], var[:, :], ACT.Sqrt, bias=eps[0:NP, :], scale=1.0 / F).then_inc(s_std2, 1)
            act.wait_ge(s_ln2, NT + 1)
            with act.Fori(0, NT) as t:
                A.activation(yn[:, DS(t, 1), :].rearrange("p a f -> p (a f)"), x_sb[:, DS(t, 1), :].rearrange("p a f -> p (a f)"),
                             ACT.Identity, bias=shift[:, DS(t, 1)], scale=rstd[:, DS(t, 1)]).then_inc(s_yn, 1)
            act.wait_ge(s_gap, 1)
            A.activation(share[:, 1, :], share[:, 1, :], ACT.Exp).then_inc(s_exp, 1)
            act.wait_ge(s_sum, 1)
            A.activation(bound[:, 0:3], ps[:, 1, 0:3], ACT.Sqrt).then_inc(s_root, 1)
            act.wait_ge(s_scales, 1)

            def high(e, u, pair):
                act.wait_ge(s_stg[u], pair * 32 + 32)
                for m, (a, b) in enumerate(((0, FH * EH), (FH * EH, WN))):
                    A.activation(wts[:, DS(e, 1), 0, a:b].rearrange("p e n -> p (e n)"), staged[u][:, a:b], ACT.Copy,
                                 scale=up2[:, m:m + 1]).then_inc(s_whi, 1)

            with act.Fori(0, X // 2) as g:
                for u in range(2):
                    high(g * 2 + u, u, g)

            def hidden(j, u):
                e = act.value_load(erow[0:1, DS(j, 1)], min_val=0, max_val=X - 1)
                act.wait_ge(s_ffn, j + 1)
                for m in range(2):
                    act.wait_ge(s_l1, j * HA + 2 * m + 2 + 2 * HA)
                    act.wait_ge(s_hl, 2 * j + m + 1)
                    for a in range(2 * m, 2 * m + 2):
                        A.activation(hs[:, u, a * 128:(a + 1) * 128], ps[:, 2 + 4 * u + m, (a % 2) * 128:(a % 2 + 1) * 128],
                                     ACT.Relu, bias=b1T[:, DS(e * HA + a, 1)], scale=back[:, 0:1]).then_inc(s_hs, 1)
                    part = slice(m * EH // 2, (m + 1) * EH // 2)
                    act.wait_ge(s_hs, 4 * j + 2 * m + 2)
                    A.activation(hT[:, u, 0, part], hs[:, u, part], ACT.Copy).then_inc(s_hh, 1)

            with act.Fori(0, NCH - 2, 2) as j:
                for u in range(2):
                    hidden(j + u, u)
            hidden(NCH - 1, 0)

            with act.Fori(0, NT // GR) as g:
                act.wait_ge(s_v3, g * 7 + 5)
                A.activation(var[:, DS(g * GR, GR)], var[:, DS(g * GR, GR)], ACT.Sqrt, bias=eps[0:NP, :], scale=1.0 / F).then_inc(s_std3, 1)
                act.wait_ge(s_v3, g * 7 + 7)
                for u in range(GR):
                    A.activation(yn[:, DS(g * GR + u, 1), :].rearrange("p a f -> p (a f)"), yn[:, DS(g * GR + u, 1), :].rearrange("p a f -> p (a f)"),
                                 ACT.Identity, bias=shift[:, DS(g * GR + u, 1)], scale=rstd[:, DS(g * GR + u, 1)]).then_inc(s_norm, 1)

        @block.tensor
        def _(pe):
            T = nc.tensor
            HG = 10

            def count(q, g, start, stop):
                return T.matmul(psH.rearrange("p (j l) -> p j l", j=HJ),
                                hot_hi[q % 2][:, DS(g, 1), :, :].rearrange("p g v j -> p (g v j)"),
                                hot_lo[q % 2][:, :, DS(g * HJ, HJ)].rearrange("p v j -> p j v"), start=start, stop=stop)

            steps = HP // HJ
            for q in range(PIECES):
                pe.wait_ge(s_hot, q + 1)
                head = HG if q == 0 else 0
                for j in range(head):
                    count(q, j, j == 0, False)
                with pe.Fori(head, steps - 2 * HG + 1, HG) as j0:
                    for j in range(HG):
                        count(q, j0 + j, False, False)
                for j in range(steps - HG, steps):
                    last = count(q, j, False, q == PIECES - 1 and j == steps - 1)
                last.then_inc(s_hist, 1)
            pe.wait_ge(s_const, 11)
            pe.wait_ge(s_diag, 1)
            T.matmul(psC, fold[:, :], diag[:, :], start=True, stop=True).then_inc(s_folded, 1)
            pe.wait_ge(s_cnt, 1)
            T.matmul(psO, before[0:HH, 0:HH], incl[:, HL - 1:HL], start=True, stop=True)
            T.transpose(psM, most[:, :], ident[0:HH, 0:HH]).then_inc(s_base, 1)

            def turn(t, u, first=False):
                pe.wait_ge(s_xs, t + 1)
                if not first:
                    pe.wait_ge(s_lnE, t - 1)
                for a in range(FH):
                    last = T.transpose(ps[:, u, a * NP:(a + 1) * NP], xs[:, u, a * 128:(a + 1) * 128], ident[0:NP, 0:NP])
                last.then_inc(s_lnT, 1)

            for t in range(2):
                turn(t, t, True)
            with pe.Fori(2, NT - 1, 2) as t:
                for u in range(2):
                    turn(t + u, u)
            pe.wait_ge(s_lnE, NT)
            for lv in range(1, LEVELS + 1):
                b = keys[1 - kept[lv - 1]]
                for q in range(16):
                    if q % 4 == 0:
                        pe.wait_ge(s_signed, 4 * (lv - 1) + q // 4 + 1)
                    t = T.transpose(psT[:, q * 128:(q + 1) * 128], b[:, q * 128:(q + 1) * 128], ident[:, :])
                    if q % 4 == 3:
                        t.then_inc(s_T, 1)
                b = keys[kept2[lv - 1]]
                pe.wait_ge(s_Tdone, lv)
                for q in range(16):
                    t = T.transpose(psR[:, q * 128:(q + 1) * 128], b[:, q * 128:(q + 1) * 128], ident[:, :])
                    if q % 4 == 3:
                        t.then_inc(s_R, 1)
            pe.wait_ge(s_Tdone, LEVELS)


            pe.wait_ge(s_lo, NT)
            pe.wait_ge(s_listed, 2)
            pe.wait_ge(s_rounds, 1)
            rounds = pe.value_load(rnd[0:1, 4:5], min_val=1, max_val=521)
            pe.sem_inc(s_built, OR)
            pe.sem_inc(s_main, AR)
            pe.sem_inc(s_agg, 1)

            def build(n, u):
                pe.wait_ge(s_oh, n + 1)
                pe.wait_ge(s_at, n + 1)
                for k in range(K):
                    last = T.matmul(ps[0:NP, u % AR, 0:BN], ohd[:, u % OR, k, 0:NP], ohs[:, u % OR, k, :],
                                    start=k == 0, stop=k == K - 1)
                last.then_inc(s_built, 1)

            def add(n, D, u, start, stop):
                pe.wait_ge(s_at, n + 1 + AR)
                for a in range(FH):
                    for h, half in enumerate((xh, xl)):
                        last = T.matmul(ps[:, 2 + a, 0:BN],
                                        half[:, DS(D, 1), a * 128:(a + 1) * 128].rearrange("p a f -> p (a f)"),
                                        atn[:, u % AR, :], start=start and h == 0, stop=stop and h == 1)
                last.then_inc(s_main, 1)

            with pe.Fori(0, rounds) as r:
                with pe.Fori(0, NS) as S:
                    n = r * NB + S * NT
                    build(n, 0)
                    for u in range(1, GU):
                        build(n + u, u)
                        if u == 1:
                            pe.wait_ge(s_agg, r * NS + S + 1)
                        add(n + u - 1, u - 1, u - 1, u == 1, False)
                    with pe.Fori(GU, NT - GU + 1, GU) as D:
                        for u in range(GU):
                            build(n + D + u, u)
                            add(n + D + (u - 1), D + (u - 1), (u - 1) % GU, False, False)
                    add(n + NT - 1, NT - 1, (NT - 1) % GU, False, True)

            pe.wait_ge(s_w, 64)
            for a in range(HID // 128):
                for f in range(FH):
                    last = T.transpose(ps[:, 4 + a // 2, (a % 2) * 256 + f * 128:(a % 2) * 256 + (f + 1) * 128],
                                       w1s[:, f, a * 128:(a + 1) * 128], ident[:, :])
            last.then_inc(s_w1T, 1)
            pe.wait_ge(s_w1Te, 1)
            for f in range(FH):
                for a in range(HID // 128):
                    T.matmul(ps[:, 6, f * F:(f + 1) * F], w1T[:, a, f * 128:(f + 1) * 128], w2s[:, a, :],
                             start=a == 0, stop=a == HID // 128 - 1)
            for a in range(HID // 128):
                last = T.matmul(ps[0:1, 7, 0:F], b1c[:, a:a + 1], w2s[:, a, :], start=a == 0, stop=a == HID // 128 - 1)
            last.then_inc(s_wf, 1)
            pe.wait_ge(s_wfe, 1)
            pe.wait_ge(s_agg, rounds * NS + 1)

            def linear(t, u, first=False):
                pe.wait_ge(s_hst, t + 1)
                if not first:
                    pe.wait_ge(s_x1, t - 1)
                for a in range(FH):
                    T.matmul(ps[0:NP, u, 0:F], hst[:, u, a, :], wf[:, a, :], start=a == 0, stop=False)
                T.matmul(ps[0:NP, u, 0:F], ones[0:1, 0:NP], brow[:, :], start=False, stop=True).then_inc(s_lin, 1)

            for t in range(2):
                linear(t, t, True)
            with pe.Fori(2, NT - 1, 2) as t:
                for u in range(2):
                    linear(t + u, u)

            def gate_T(t, u):
                pe.wait_ge(s_yn, t + 1)
                for a in range(FH):
                    last = T.transpose(ps[:, u, a * NP:(a + 1) * NP],
                                       yn[:, DS(t, 1), a * 128:(a + 1) * 128].rearrange("p a f -> p (a f)"), ident[0:NP, 0:NP])
                last.then_inc(s_ynT, 1)

            def gate(t, u):
                pe.wait_ge(s_ynE, t + 1)
                for a in range(FH):
                    last = T.matmul(ps[0:NP, 2 + t // 32, (t % 32) * X:(t % 32 + 1) * X], ynT[:, u, a, :], gw[:, a, :],
                                    start=a == 0, stop=a == FH - 1)
                last.then_inc(s_lg, 1)

            pe.wait_ge(s_x1, NT)
            pe.wait_ge(s_gw, 32)
            gate_T(0, 0)
            for t in range(1, NT):
                gate_T(t, t % 2)
                gate(t - 1, (t - 1) % 2)
            gate(NT - 1, (NT - 1) % 2)

            pe.wait_ge(s_con2, 4)
            pe.wait_ge(s_chosen, 1)
            for b in range(4):
                T.matmul(ps[0:NP, b, 0:400], before16[:, :], chosen16[:, b * 400:(b + 1) * 400], start=True, stop=True)
                last = T.matmul(ps[0:NP, 4 + b, 0:400], ones16[:, :], chosen16[:, b * 400:(b + 1) * 400], start=True, stop=True)
            last.then_inc(s_rank, 1)
            pe.wait_ge(s_b1r, 16)
            pe.wait_ge(s_pos, 1)
            pe.wait_ge(s_bound, 1)
            T.matmul(ps[:, 1, 0:3], ones128, bound[:, 0:3], start=True, stop=True).then_inc(s_sum, 1)
            T.transpose(ps[:, 7, 448:448 + X * HA], b1r, ident[0:X * HA, 0:X * HA]).then_inc(s_b1T, 1)

            pe.wait_ge(s_erow, 1)
            pe.wait_ge(s_wlo, X + 2)
            pe.sem_inc(s_ffn, 2)

            def chunk_T(u, turn):
                pe.wait_ge(s_xld[u], turn * 32 + 32)
                for a in range(FH):
                    last = T.transpose(ps[:, u % 2, a * 128:(a + 1) * 128], xr[:, u, a * 128:(a + 1) * 128], ident[:, :])
                last.then_inc(s_ct, 1)

            PARTS = ((0, 0), (0, 1), (1, 0))

            def up(j, u):
                e = pe.value_load(erow[0:1, DS(j, 1)], min_val=0, max_val=X - 1)
                pe.wait_ge(s_xl, j + 1)
                for m in range(HA):
                    steps = [(a, w, x) for a in range(FH) for w, x in PARTS]
                    for n, (a, w, x) in enumerate(steps):
                        last = T.matmul(ps[:, 2 + 4 * u + m // 2, (m % 2) * 128:(m % 2 + 1) * 128],
                                        wts[:, DS(e, 1), w, a * EH + m * 128:a * EH + (m + 1) * 128].rearrange("p e n -> p (e n)"),
                                        xT[:, u, x, a, :], start=n == 0, stop=n == len(steps) - 1)
                    last.then_inc(s_l1, 1)

            def down(j, u):
                e = pe.value_load(erow[0:1, DS(j, 1)], min_val=0, max_val=X - 1)
                pe.wait_ge(s_eo, j + 1 + LR - 2)
                for m in range(HA):
                    if m % 2 == 0:
                        pe.wait_ge(s_hl, 2 * j + m // 2 + 1 + 4)
                    for w, h in PARTS:
                        last = T.matmul(ps[:, 4 + u, 0:F], hT[:, u, h, m * 128:(m + 1) * 128],
                                        wts[:, DS(e, 1), w, FH * EH + m * F:FH * EH + (m + 1) * F].rearrange("p e n -> p (e n)"),
                                        start=m == 0 and w == h == 0, stop=m == HA - 1 and w == 1)
                last.then_inc(s_ffn, 1)

            chunk_T(0, 0)
            chunk_T(1, 0)
            up(0, 0)
            with pe.Fori(0, (NCH - 2) // LR) as g:
                for u in range(LR):
                    chunk_T((u + 2) % LR, g + (u + 2) // LR)
                    up(g * LR + u + 1, (u + 1) % 2)
                    down(g * LR + u, u % 2)
            for j in range((NCH - 2) // LR * LR, NCH):
                if j + 2 < NCH:
                    chunk_T((j + 2) % LR, (j + 2) // LR)
                if j + 1 < NCH:
                    up(j + 1, (j + 1) % 2)
                down(j, j % 2)


_INS = ['x', 'src', 'dst', 'L0_gnn_W1', 'L0_gnn_b1', 'L0_gnn_W2', 'L0_gnn_b2', 'L0_ffn_gate_w', 'L0_ffn_gate_b',
        'L0_ffn_w1', 'L0_ffn_b1', 'L0_ffn_w2', 'L0_ffn_b2', 'L0_ffn_gamma', 'L0_ffn_beta']
_OUTS = [((6250, 256), 'float32')]


def kernel(**inputs):
    import numpy as _np
    import concourse.bacc as _bacc
    from concourse import mybir as _mybir
    from concourse.bass_utils import run_bass_kernel_spmd as _run
    nc = _bacc.Bacc("TRN2", target_bir_lowering=False, num_devices=1)
    arrays, args, outs = {}, [], []
    for name in _INS:
        a = _np.ascontiguousarray(inputs[name])
        arrays[f"in_{name}_dram"] = a
        args.append(nc.dram_tensor(f"in_{name}_dram", a.shape, _mybir.dt.from_np(a.dtype), kind="ExternalInput").ap())
    for i, (shape, dtype) in enumerate(_OUTS):
        dt = _mybir.dt.from_np(_np.dtype(dtype))
        outs.append(nc.dram_tensor(f"out_{i}_dram", shape, dt, kind="ExternalOutput").ap())
    list_d = nc.dram_tensor("list_d", (262144, 2), _mybir.dt.float32, kind="Internal").ap()
    off_d = nc.dram_tensor("off_d", (672,), _mybir.dt.int32, kind="Internal").ap()
    slots_d = nc.dram_tensor("slots_d", (113 * 128, 256), _mybir.dt.float32, kind="Internal").ap()
    eo_d = nc.dram_tensor("eo_d", (113 * 128, 256), _mybir.dt.float32, kind="Internal").ap()
    xb_d = nc.dram_tensor("xb_d", (6250, 256), _mybir.dt.float32, kind="Internal").ap()
    yn_d = nc.dram_tensor("yn_d", (6250, 256), _mybir.dt.float32, kind="Internal").ap()
    prog(nc, *args, outs[0], list_d, off_d, slots_d, eo_d, xb_d, yn_d)
    r = _run(nc, [arrays], core_ids=[0])
    return r.results[0]["out_0_dram"]
```

```python
import concourse.bass as bass
from concourse import mybir
from contextlib import ExitStack


def prog(nc, x, src, dst, W1, b1, W2, b2, gate_w, gate_b, ew1, eb1, ew2, eb2, gamma, beta, out, list_d, off_d, slots_d, eo_d, xb_d, yn_d):
    fp32, fp16, i32 = mybir.dt.float32, mybir.dt.float16, mybir.dt.int32
    ALU, ACT, AX = mybir.AluOpType, mybir.ActivationFunctionType, mybir.AxisListType
    DS = bass.ds

    N, F = x.shape
    E = src.shape[0]
    HID = W1.shape[1]
    NP, NT = 125, 50
    BN = 314
    NS = -(-N // BN)
    NB = NS * NT
    EC = E // NP
    C = 2048
    LEVELS = 7
    BASE = 128
    SENTINEL = (NB + 50 + BASE) << 16
    K = 2
    WIN = 128 * K
    LAST_START = 128 * C - WIN
    HH, HL = 32, 32
    HP = 400
    PIECES = EC // HP
    UP = 2.0 ** 11
    GU = 10
    OR = 5
    AR = 2
    HJ = 4
    EPS = 1e-5
    X, EH = ew1.shape[0], ew1.shape[2]
    KT = 2 * NT
    NCH = (KT * NP + X * 127) // 128
    HA = EH // 128
    GR = 5
    FH = F // 128
    EARLY = 30
    LR = 4
    CU = 16

    kept, kept2 = [], []

    ctx = ExitStack()
    with ctx:
        def sb(name, shape, dt):
            return ctx.enter_context(nc.sbuf_tensor(name, shape, dt))

        def sem(name):
            return ctx.enter_context(nc.semaphore(name))

        XN, XS = 13056, NT * F
        arena = sb("arena", [128, XN + 2 * XS], fp32)
        xnT = arena[:, 0:FH * NS * BN].rearrange("p (a n) -> p a n", a=FH)
        x_sb = arena[0:NP, XN:XN + XS].rearrange("p (t f) -> p t f", t=NT)
        halves = arena[:, XN + XS:].bitcast(fp16).rearrange("p (a n) -> p a n", a=2)
        xh = halves[0:NP, 0, :].rearrange("p (t f) -> p t f", t=NT)
        xl = halves[0:NP, 1, :].rearrange("p (t f) -> p t f", t=NT)
        scratch = halves[0:NP, :, :].rearrange("p a n -> p (a n)").bitcast(i32)
        edges = [scratch[:, i * EC:(i + 1) * EC] for i in range(8)]
        srcs, dsts, ta, tb, tc, td, te, tf = edges
        hots = [arena[0:NP, at:at + (HH + HL) * HP // 2].bitcast(fp16) for at in (0, XN + XS)]
        hot_hi = [h[:, 0:HH * HP].rearrange("p (g v j) -> p g v j", v=HH, j=HJ) for h in hots]
        hot_lo = [h[:, HH * HP:].rearrange("p (v j) -> p v j", j=HP) for h in hots]
        keys = [sb(f"keys{i}", [128, C], fp32) for i in range(2)]
        listed = sb("listed", [128, C, 2], fp32)
        digits = listed[0:NP, :, :].rearrange("p c w -> p (c w)").bitcast(fp16)
        hi16, lo16 = digits[:, 0:EC], digits[:, EC:2 * EC]
        upper = listed[:, 0:C // 4, :].rearrange("p c w -> p (c w)")
        ident = sb("ident", [128, 128], fp32)
        rown = sb("rown", [128, 1], i32)
        bit = sb("bit", [128, 1], i32)
        sign = sb("sign", [128, LEVELS + 1], fp32)
        toggle = sb("toggle", [128, LEVELS + 1], fp32)
        before = sb("before", [128, 128], fp32)
        cube = sb("cube", [HJ * HH, HH, HJ], fp32)
        same = sb("same", [HJ * HH, HJ], fp32)
        fold = sb("fold", [HJ * HH, HH], fp32)
        crossed = sb("crossed", [HJ * HH, HJ, HL], fp32)
        diag = sb("diag", [HJ * HH, HL], fp32)
        stats = sb("stats", [NP, NT, 6], fp32)
        mean = sb("mean", [NP, NT], fp32)
        var = sb("var", [NP, NT], fp32)
        rstd = sb("rstd", [NP, NT], fp32)
        shift = sb("shift", [NP, NT], fp32)
        eps = sb("eps", [128, 1], fp32)
        squares = sb("squares", [128, 4 * X + 1], fp32)
        bound = sb("bound", [128, 4], fp32)
        expo = sb("expo", [128, 4], i32)
        up2 = sb("up2", [128, 4], fp32)
        down2 = sb("down2", [128, 4], fp32)
        back = sb("back", [128, 2], fp32)
        rows = sb("rows", [128, 2, F], fp32)
        xs = rows[0:NP, :, :]
        hst = rows[:, :, 0:FH * NP].rearrange("p u (a n) -> p u a n", a=FH)
        ohs = (listed[:, :, :].rearrange("p c w -> p (c w)").bitcast(fp16)[:, 0:OR * K * BN]
               .rearrange("p (o k n) -> p o k n", o=OR, k=K))
        small = sb("small", [128, 832], fp32)
        ohd = small[:, 0:OR * K * 64].bitcast(fp16).rearrange("p (o k n) -> p o k n", o=OR, k=K)
        zeros = small[:, 0:F]
        biasb = small[0:NP, 0:F]
        sqs = [small[:, 0:HID], listed[:, C // 2:C // 2 + HID // 2, :].rearrange("p c w -> p (c w)")]
        atn = sb("atn", [NP, AR, BN], fp16)
        win = sb("win", [128, GU, K, 2], fp32)
        firsts = listed[:, :, :].rearrange("p c w -> p (c w)")[:, C:C + NB]
        places = sb("places", [128, BN], fp16)
        wf = sb("wf", [128, FH, F], fp32)
        w1s = keys[0][:, 0:FH * HID].rearrange("p (a n) -> p a n", a=FH)
        w2s = keys[1][:, 0:FH * HID].rearrange("p (a n) -> p a n", a=HID // 128)
        w1T = keys[0][:, FH * HID:2 * FH * HID].rearrange("p (a n) -> p a n", a=HID // 128)
        b1c = sb("b1c", [128, HID // 128], fp32)
        b2r = sb("b2r", [1, F], fp32)
        ones = sb("ones", [1, 128], fp32)
        cnt = sb("cnt", [HH, HL], fp32)
        incl = sb("incl", [HH, HL], fp32)
        offf = sb("offf", [HH, HL], fp32)
        offi = sb("offi", [HH, HL], i32)
        most = sb("most", [HH, 1], fp32)
        rnd = sb("rnd", [1, 8], i32)
        offrow = sb("offrow", [1, HH * HL], i32)

        yn = halves[0:NP, :, :].rearrange("p a n -> p (a n)").bitcast(fp32).rearrange("p (t f) -> p t f", t=NT)
        area = arena[:, 0:XN]
        at = [0]

        def carve(n, rows=128):
            at[0] += n
            return area[0:rows, at[0] - n:at[0]]

        wb2 = carve(LR * F).rearrange("p (u n) -> p u n", u=LR)
        xr = carve(LR * F).rearrange("p (u n) -> p u n", u=LR)
        xT = carve(2 * F).bitcast(fp16).rearrange("p (u h a n) -> p u h a n", u=2, h=2, a=FH)
        hs = carve(2 * EH).rearrange("p (u n) -> p u n", u=2)
        hT = carve(2 * EH).bitcast(fp16).rearrange("p (u h n) -> p u h n", u=2, h=2)
        eo = carve(2 * F).rearrange("p (u n) -> p u n", u=2)
        logits = area[0:NP, 0:NT * X].rearrange("p (t e) -> p t e", e=X)
        masked = area[0:NP, 800:800 + NT * X].rearrange("p (t e) -> p t e", e=X)
        chosen16 = area[0:NP, 1600:1600 + KT * X // 2].bitcast(fp16)
        ones128 = area[:, 2400:2528]
        WN = FH * EH + HA * F
        wts = arena[:, XN + 2 * XS - X * WN:].bitcast(fp16).rearrange("p (e h n) -> p e h n", e=X, h=2)
        staged = [k[:, 0:WN] for k in keys]
        b1T = carve(X * HA)
        assert at[0] + 128 + 2 * F <= XN + 2 * XS - X * WN
        b1r = carve(128, X * HA)
        chosen = keys[0][0:NP, 0:KT * X].rearrange("p (e k) -> p e k", e=X)
        total = keys[1][0:NP, 0:KT * X].rearrange("p (e k) -> p e k", e=X)
        lst = listed[0:NP, :, :].rearrange("p c w -> p (c w)")
        upto = lst[:, 0:KT * X].rearrange("p (e k) -> p e k", e=X)
        place = lst[:, 2048:2048 + KT * X].rearrange("p (e k) -> p e k", e=X)
        gw = sb("gw", [128, FH, X], fp32)
        gb = sb("gb", [NP, X], fp32)
        eix = sb("eix", [NP, X], fp32)
        eix64 = sb("eix64", [NP, X], fp32)
        used = [0]

        def take(*shape, dt=fp32):
            n = shape[0] if len(shape) == 1 else shape[0] * shape[1]
            used[0] += n
            flat = small[0:NP, used[0] - n:used[0]]
            flat = flat if dt is fp32 else flat.bitcast(dt)
            return flat if len(shape) == 1 else flat.rearrange("p (a b) -> p a b", a=shape[0])

        before16 = sb("before16", [NP, NP], fp16)
        ones16 = sb("ones16", [NP, NP], fp16)
        best = take(2, NT)
        which = take(2, NT)
        share = take(2, NT)
        nexp = take(X, dt=i32)
        padded = take(X)
        padend = take(X)
        adjust = take(X)
        posf = take(KT)
        posi = take(KT, dt=i32)
        erow = take(NCH, dt=i32)[0:1, :]
        erowf = take(NCH)[0:1, :]
        gam = carve(F, NP)
        bet = carve(F, NP)
        GB = (0, 1, 4, 5, 6)
        ynT = [hst[:, 0, :, :], hst[:, 1, :, :]] + [
            area[:, 4368 + i * FH * NP:4368 + (i + 1) * FH * NP].rearrange("p (a n) -> p a n", a=FH) for i in range(3)]
        reach = listed[0:1, :, :].rearrange("p c w -> p (c w)")[:, 0:NCH * X].rearrange("p (j e) -> p j e", e=X)
        got = [lst[:, i * 2 * F:(i + 1) * 2 * F].rearrange("p (k n) -> p k n", k=2) for i in range(8)]
        got += [keys[0][0:NP, i * 2 * F:(i + 1) * 2 * F].rearrange("p (k n) -> p k n", k=2) for i in range(2)]
        started = area[0:1, 2560:2560 + NCH * X].rearrange("p (j e) -> p j e", e=X)

        ps = ctx.enter_context(nc.psum_tensor("ps", [128, 8, 512], fp32))
        psT = ps[:, 0:4, :].rearrange("p a n -> p (a n)")
        psR = ps[:, 4:8, :].rearrange("p a n -> p (a n)")
        psH = ps[0:HJ * HH, 7, 0:HJ * HL]
        psC = ps[0:HH, 4, 0:HL]
        psO = ps[0:HH, 6, 0:1]
        psM = ps[0:1, 5, 0:HH]

        s_src, s_dst = sem("s_src"), sem("s_dst")
        s_const = sem("s_const")
        s_chain = sem("s_chain")
        s_hot = sem("s_hot")
        s_hist = sem("s_hist")
        s_cnt, s_base, s_rounds = sem("s_cnt"), sem("s_base"), sem("s_rounds")
        s_offi, s_offd, s_offrow = sem("s_offi"), sem("s_offd"), sem("s_offrow")
        s_rows, s_signed, s_T, s_Tdone, s_R = sem("s_rows"), sem("s_signed"), sem("s_T"), sem("s_Tdone"), sem("s_R")
        s_Tup, s_Rup = sem("s_Tup"), sem("s_Rup")
        s_listed, s_list, s_out = sem("s_listed"), sem("s_list"), sem("s_out")
        s_x, s_diag, s_folded = sem("s_x"), sem("s_diag"), sem("s_folded")
        s_var, s_std, s_ln = sem("s_var"), sem("s_std"), sem("s_ln")
        s_xs, s_hi, s_lo, s_lnT, s_lnE = sem("s_xs"), sem("s_hi"), sem("s_lo"), sem("s_lnT"), sem("s_lnE")
        s_win = [sem(f"s_win{u}") for u in range(GU)]
        s_bias, s_pre, s_firsts, s_oh, s_built, s_at, s_main, s_agg = (
            sem(n) for n in ("s_bias", "s_pre", "s_firsts", "s_oh", "s_built", "s_at", "s_main", "s_agg"))
        s_started = sem("s_started")
        s_round, s_offnew = sem("s_round"), sem("s_offnew")
        s_w, s_w1T, s_w1Te, s_wf, s_wfe = sem("s_w"), sem("s_w1T"), sem("s_w1Te"), sem("s_wf"), sem("s_wfe")
        s_hst, s_lin, s_x1 = sem("s_hst"), sem("s_lin"), sem("s_x1")
        s_zero, s_z, s_gw, s_gam, s_con2 = sem("s_zero"), sem("s_z"), sem("s_gw"), sem("s_gam"), sem("s_con2")
        s_var2, s_std2, s_ln2, s_yn, s_ynT, s_ynE, s_lg = (
            sem(n) for n in ("s_var2", "s_std2", "s_ln2", "s_yn", "s_ynT", "s_ynE", "s_lg"))
        s_gap, s_exp, s_chosen, s_rank, s_pos = (
            sem(n) for n in ("s_gap", "s_exp", "s_chosen", "s_rank", "s_pos"))
        s_scat = {e: sem(f"s_scat{e}") for e in range(9, X)}
        s_erowi = sem("s_erowi")
        s_b1r, s_b1T, s_erow = sem("s_b1r"), sem("s_b1T"), sem("s_erow")
        s_xld = [sem(f"s_xld{u}") for u in range(LR)]
        s_wb = [sem(f"s_wb{u}") for u in range(LR)]
        s_ct, s_xh, s_xl, s_l1, s_hs, s_hh, s_hl, s_ffn, s_eo = (
            sem(n) for n in ("s_ct", "s_xh", "s_xl", "s_l1", "s_hs", "s_hh", "s_hl", "s_ffn", "s_eo"))
        s_sqld = [sem(f"s_sqld{u}") for u in range(2)]
        s_sq, s_sum, s_bound, s_root, s_scales = (sem(n) for n in ("s_sq", "s_sum", "s_bound", "s_root", "s_scales"))
        s_stg = [sem(f"s_stg{u}") for u in range(2)]
        s_whi, s_wlo, s_parked = sem("s_whi"), sem("s_wlo"), sem("s_parked")
        s_back = [sem(f"s_back{u}") for u in range(2)]
        s_store = [sem(f"s_store{u}") for u in range(2)]
        s_got = [sem(f"s_got{u}") for u in range(2 * GR)]
        s_used, s_y, s_v3, s_std3, s_sh3, s_norm, s_fin, s_xb = (
            sem(n) for n in ("s_used", "s_y", "s_v3", "s_std3", "s_sh3", "s_norm", "s_fin", "s_xb"))
        block = ctx.enter_context(nc.Block())

        def over(t):
            return (XN + XS + (t + 1) * F - 1 - (XN + 2 * XS - X * WN)) // WN

        def later(lv):
            return range(EARLY + 4 * (lv - 1), min(EARLY + 4 * lv, NT))

        def experts(j, count, engine):
            _, values = nc.values_load_multi_w_load_instructions(
                erow[0:1, DS(j, count)], engines=[engine], min_val=0, max_val=X - 1)
            return values

        @block.gpsimd
        def _(pool):
            nc.gpsimd.memset(ident[:, :], 0.0).then_inc(s_const, 1)
            nc.gpsimd.memset(zeros[:, :], 0.0).then_inc(s_z, 1)
            nc.gpsimd.memset(before[:, :], 1.0).then_inc(s_const, 1)
            pool.wait_ge(s_const, 2)
            nc.gpsimd.affine_select(out=ident[:, :], in_=ident[:, :], compare_op=ALU.not_equal, fill=1.0,
                                    base=0, pattern=[[-1, 128]], channel_multiplier=1).then_inc(s_const, 1)
            nc.gpsimd.affine_select(out=before[:, :], in_=before[:, :], compare_op=ALU.is_gt, fill=0.0,
                                    base=0, pattern=[[1, 128]], channel_multiplier=-1).then_inc(s_const, 1)
            nc.gpsimd.iota(rown[:, :], pattern=[[0, 1]], base=0, channel_multiplier=1).then_inc(s_const, 1)
            nc.gpsimd.memset(cube[:, :, :], 0.0).then_inc(s_const, 1)
            nc.gpsimd.memset(eps[:, :], EPS).then_inc(s_const, 1)
            nc.gpsimd.memset(ones[:, :], 1.0).then_inc(s_const, 1)
            pool.wait_ge(s_const, 8)
            nc.gpsimd.affine_select(out=cube[:, :, :], in_=cube[:, :, :], compare_op=ALU.not_equal, fill=1.0,
                                    base=0, pattern=[[-HJ, HH], [-1, HJ]], channel_multiplier=1).then_inc(s_const, 1)
            nc.gpsimd.iota(places[:, :], pattern=[[1, BN]], base=0, channel_multiplier=0,
                           allow_small_or_imprecise_dtypes=True).then_inc(s_const, 1)

            def low_half(t, u):
                pool.wait_ge(s_hi, t + 1)
                nc.gpsimd.tensor_tensor(xl[:, DS(t, 1), :].rearrange("p a f -> p (a f)"), xs[:, u, :],
                                        xh[:, DS(t, 1), :].rearrange("p a f -> p (a f)"), ALU.subtract).then_inc(s_lo, 1)

            with pool.Fori(0, NT - 1, 2) as t:
                for u in range(2):
                    low_half(t + u, u)

            pool.wait_ge(s_list, 32)
            nc.gpsimd.iota(firsts, pattern=[[512, NB]], base=512 * BASE, channel_multiplier=0,
                           allow_small_or_imprecise_dtypes=True).then_inc(s_firsts, 1)

            nc.gpsimd.iota(eix[:, :], pattern=[[1, X]], base=0, channel_multiplier=0,
                           allow_small_or_imprecise_dtypes=True).then_inc(s_con2, 1)
            nc.gpsimd.iota(eix64[:, :], pattern=[[1, X]], base=64, channel_multiplier=0,
                           allow_small_or_imprecise_dtypes=True).then_inc(s_con2, 1)
            nc.gpsimd.tensor_copy(before16[:, :], before[0:NP, 0:NP]).then_inc(s_con2, 1)
            nc.gpsimd.memset(ones16[:, :], 1.0).then_inc(s_con2, 1)

            pool.wait_ge(s_bias, 1)
            with pool.Fori(0, NT) as t:
                nc.gpsimd.tensor_tensor(x_sb[:, DS(t, 1), :].rearrange("p a f -> p (a f)"),
                                        x_sb[:, DS(t, 1), :].rearrange("p a f -> p (a f)"), biasb, ALU.add
                                        ).then_inc(s_pre, 1)

            pool.wait_ge(s_hst, NT)
            nc.gpsimd.iota(started, pattern=[[128, NCH], [0, X]], base=0, channel_multiplier=0,
                           allow_small_or_imprecise_dtypes=True).then_inc(s_erowi, 1)

            pool.wait_ge(s_gam, 32)
            pool.wait_ge(s_yn, NT)
            with pool.Fori(0, NT) as t:
                nc.gpsimd.tensor_tensor(x_sb[:, DS(t, 1), :].rearrange("p a f -> p (a f)"),
                                        x_sb[:, DS(t, 1), :].rearrange("p a f -> p (a f)"), bet[:, :], ALU.add
                                        ).then_inc(s_xb, 1)

            pool.wait_ge(s_pos, 1)
            pool.wait_ge(s_zero, 16)
            for t in range(NT):
                for k in range(2):
                    c = k * NT + t
                    nc.gpsimd.indirect_dma_start(
                        out=slots_d, out_offset=bass.IndirectOffsetOnAxis(ap=posi[:, c:c + 1], axis=0),
                        in_=yn[:, t, :], in_offset=None).then_inc(s_scat[over(t)], 16)

            def store(j, u):
                pool.wait_ge(s_eo, j + 1 + LR)
                pool.dma_start(eo_d[DS(j * 128, 128), :], eo[:, u, :]).then_inc(s_store[u], 16)

            with pool.Fori(0, NCH - 2, 2) as j:
                for u in range(2):
                    store(j + u, u)
            store(NCH - 1, 0)
            pool.wait_ge(s_store[0], 16 * (NCH // 2 + 1))
            pool.wait_ge(s_store[1], 16 * (NCH // 2))
            for t in range(NT):
                if t >= 2 * GR:
                    pool.wait_ge(s_used, t - 2 * GR + 1)
                for k in range(2):
                    nc.gpsimd.indirect_dma_start(
                        out=got[t % (2 * GR)][:, k, :], out_offset=None, in_=eo_d,
                        in_offset=bass.IndirectOffsetOnAxis(ap=posi[:, k * NT + t:k * NT + t + 1], axis=0)
                        ).then_inc(s_got[t % (2 * GR)], 16)

        @block.sync
        def _(sp):
            sp.dma_start(dsts, dst.rearrange("(p j) -> p j", p=NP)).then_inc(s_dst, 16)
            sp.dma_start(srcs, src.rearrange("(p j) -> p j", p=NP)).then_inc(s_src, 16)
            sp.dma_start(x_sb[:, :, :], x.rearrange("(p t) f -> p t f", t=NT)).then_inc(s_x, 16)
            sp.dma_start(gw[:, :, :], gate_w.rearrange("(a p) e -> p a e", p=128)).then_inc(s_gw, 16)
            sp.dma_start(gb[:, :], gate_b.rearrange("(a n) -> a n", a=1).to_broadcast([NP, X])).then_inc(s_gw, 16)
            sp.wait_ge(s_z, 1)
            sp.dma_start(slots_d.rearrange("(j p) f -> p j f", p=128),
                         zeros[:, :].rearrange("p (a f) -> p a f", a=1).to_broadcast([128, NCH, F])).then_inc(s_zero, 16)
            sp.wait_ge(s_offi, 1)
            sp.dma_start(off_d.rearrange("(h l) -> h l", h=HH), offi[:, :]).then_inc(s_offd, 16)
            sp.wait_ge(s_offd, 16)
            sp.dma_start(offrow[:, :], off_d.rearrange("(a n) -> a n", a=1)).then_inc(s_offrow, 16)
            sp.wait_ge(s_offrow, 16)

            def weigh(w, e, lo):
                for a in range(2):
                    sp.wait_ge(s_sq, 2 * (lo + e) + a + 1)
                    sp.dma_start(sqs[a], w[DS(e, 1), a * w.shape[1] // 2:(a + 1) * w.shape[1] // 2, :].rearrange(
                        "e (p c) n -> p (e c n)", p=128)).then_inc(s_sqld[a], 16)

            sp.wait_ge(s_zero, 16)
            sp.wait_ge(s_hist, PIECES)
            with sp.Fori(0, X) as e:
                weigh(ew1, e, 0)
            with sp.Fori(0, X) as e:
                weigh(ew2, e, X)
            sp.wait_ge(s_sq, 4 * X + 1)
            sp.dma_start(sqs[0][:, 0:X * HA], eb1.rearrange("e (c n) -> (e c) n", c=128 // X)
                         ).then_inc(s_sqld[0], 16)
            for h in range(2):
                cols = slice(h * C // 2, (h + 1) * C // 2)
                sp.wait_ge(s_listed, 2 * h + 2)
                sp.dma_start(list_d.rearrange("(p c) w -> p c w", p=128)[:, cols, :], listed[:, cols, :]).then_inc(s_list, 16)
            sp.wait_ge(s_rounds, 1)
            rounds = sp.value_load(rnd[0:1, 4:5], min_val=1, max_val=E // WIN + 1)
            with sp.Fori(0, rounds) as r:
                sp.wait_ge(s_offnew, r + 1)
                sp.sem_inc(s_started, 1)
                with sp.Fori(0, NB // GU // 2) as g:
                    _, starts = nc.values_load_multi_w_load_instructions(
                        offrow[0:1, DS(g * 2 * GU, 2 * GU)], engines=[mybir.EngineType.SP], min_val=0, max_val=LAST_START)
                    sp.wait_ge(s_list, 32)
                    for v in range(2 * GU):
                        if v % 2 == 0:
                            sp.wait_ge(s_oh, r * NB + g * 2 * GU + v + 2)
                        sp.dma_start(win[:, v % GU, :, :].rearrange("p k w -> p (k w)"),
                                     list_d[DS(starts[v], WIN), :].rearrange("(p k) w -> p (k w)", p=128)
                                     ).then_inc(s_win[v % GU], 16)
                sp.drain().then_inc(s_round, 1)
            sp.wait_ge(s_hst, NT)
            sp.dma_start(gam[:, :], gamma.rearrange("(a n) -> a n", a=1).to_broadcast([NP, F])).then_inc(s_gam, 16)
            sp.dma_start(bet[:, :], beta.rearrange("(a n) -> a n", a=1).to_broadcast([NP, F])).then_inc(s_gam, 16)
            sp.dma_start(b1r, eb1.rearrange("e (a n) -> (e a) n", a=HA)).then_inc(s_b1r, 16)
            sp.wait_ge(s_yn, NT)
            sp.dma_start(yn_d.rearrange("(p t) f -> p t f", t=NT), yn).then_inc(s_parked, 16)
            sp.wait_ge(s_xb, NT)
            sp.dma_start(xb_d.rearrange("(p t) f -> p t f", t=NT), x_sb).then_inc(s_parked, 16)
            sp.wait_ge(s_erow, 1)
            sp.wait_ge(s_scales, 1)
            sp.wait_ge(s_yn, NT)

            def stage_weights(e, u):
                sp.wait_ge(s_wlo, e + 1)
                sp.dma_start(staged[u][:, 0:FH * EH].rearrange("p (a n) -> p a n", a=FH),
                             ew1[DS(e, 1), :, :].rearrange("e (a p) n -> p (e a) n", p=128)).then_inc(s_stg[u], 16)
                sp.dma_start(staged[u][:, FH * EH:].rearrange("p (a n) -> p a n", a=HA),
                             ew2[DS(e, 1), :, :].rearrange("e (a p) n -> p (e a) n", p=128)).then_inc(s_stg[u], 16)

            stage_weights(0, 0)
            stage_weights(1, 1)
            sp.wait_ge(s_parked, 32)
            with sp.Fori(2, 8 - 1, 2) as e:
                for u in range(2):
                    stage_weights(e + u, u)
            for e in range(8, X):
                tiles = sum(over(t) == e for t in range(NT))
                if tiles:
                    sp.wait_ge(s_scat[e], 16 * 2 * tiles)
                stage_weights(e, e % 2)

            def load(j, u):
                sp.wait_ge(s_ct, j + 1)
                sp.dma_start(xr[:, u, :], slots_d[DS(j * 128, 128), :]).then_inc(s_xld[u], 16)

            with sp.Fori(0, NCH - LR, LR) as j:
                for u in range(LR):
                    load(j + u, u)
            load(NCH - 1, 0)
            sp.wait_ge(s_ffn, NCH + 2)

            def reload(g, h):
                cols = DS(g * GR, GR)
                sp.dma_start(yn[:, cols, :], yn_d.rearrange("(p t) f -> p t f", t=NT)[:, cols, :]).then_inc(s_back[h], 16)
                sp.dma_start(x_sb[:, cols, :], xb_d.rearrange("(p t) f -> p t f", t=NT)[:, cols, :]).then_inc(s_back[h], 16)

            def put(g):
                sp.wait_ge(s_fin, g + 1)
                cols = DS(g * GR, GR)
                sp.dma_start(out.rearrange("(p t) f -> p t f", t=NT)[:, cols, :], yn[:, cols, :]).then_inc(s_out, 16)

            reload(0, 0)
            reload(1, 1)
            with sp.Fori(1, NT // GR // 2) as g:
                for h in range(2):
                    sp.wait_ge(s_used, (g * 2 + (h - 1)) * GR)
                    reload(g * 2 + h, h)
                    put(g * 2 + (h - 2))
            put(NT // GR - 2)
            put(NT // GR - 1)
            sp.wait_ge(s_out, 16 * (NT // GR))

        @block.vector
        def _(dve):
            V = nc.vector
            chain = [0]

            def link(ins):
                chain[0] += 1
                ins.then_inc(s_chain, 1)
                dve.wait_ge(s_chain, chain[0])

            def after(ins):
                chain[0] += 1
                ins.then_inc(s_chain, 1)

            def mark():
                return V.tensor_copy(bit[0:1, :], rown[0:1, :])

            def join():
                dve.wait_ge(s_chain, chain[0])

            V.memset(keys[0][:, :].bitcast(i32), SENTINEL).then_inc(s_chain, 1)
            chain[0] += 1
            dve.wait_ge(s_const, 10)
            for lv in range(LEVELS + 1):
                link(V.tensor_scalar(bit[:, :], rown[:, :], lv, 1, ALU.logical_shift_right, ALU.bitwise_and))
                link(V.tensor_scalar(sign[:, lv:lv + 1], bit[:, :], -2.0, 1.0, ALU.mult, ALU.add))
            link(V.tensor_tensor(toggle[:, 1:], sign[:, 0:LEVELS], sign[:, 1:], ALU.mult))

            def split(whole, quotient, rest, t1):
                link(V.tensor_scalar(t1, whole, 1, None, ALU.logical_shift_right))
                link(V.tensor_scalar(quotient, t1, 1311, None, ALU.mult))
                link(V.tensor_scalar(quotient, quotient, 15, None, ALU.logical_shift_right))
                link(V.scalar_tensor_tensor(rest, quotient, -NT, whole, ALU.mult, ALU.add))

            dve.wait_ge(s_dst, 16)
            split(dsts, ta, tb, tf)
            dve.wait_ge(s_src, 16)
            split(srcs, tc, td, tf)
            link(V.scalar_tensor_tensor(tc, td, NP, tc, ALU.mult, ALU.add))
            link(V.tensor_scalar(te, tc, 1, None, ALU.logical_shift_right))
            link(V.tensor_scalar(td, te, 1670, None, ALU.mult))
            link(V.tensor_scalar(td, td, 18, None, ALU.logical_shift_right))
            link(V.scalar_tensor_tensor(tc, td, -BN, tc, ALU.mult, ALU.add))
            link(V.scalar_tensor_tensor(td, td, NT, tb, ALU.mult, ALU.add))
            link(V.scalar_tensor_tensor(tc, tc, 128, ta, ALU.mult, ALU.add))
            after(V.tensor_scalar(ta, td, 5, None, ALU.logical_shift_right))
            after(V.tensor_scalar(tb, td, 31, None, ALU.bitwise_and))
            link(V.tensor_scalar(td, td, BASE, None, ALU.add))
            after(V.tensor_copy(hi16[:, :], ta))
            after(V.tensor_copy(lo16[:, :], tb))
            link(V.scalar_tensor_tensor(keys[0][0:NP, 0:EC].bitcast(i32), td, 16, tc,
                                        ALU.logical_shift_left, ALU.bitwise_or))
            link(V.tensor_scalar(keys[0][:, :], keys[0][:, :], sign[:, 0:1], None, ALU.mult))

            def digits_hot(q):
                if q >= 2:
                    dve.wait_ge(s_hist, q - 1)
                for v in range(HH):
                    V.tensor_scalar(hot_hi[q % 2][:, :, v, :], hi16[:, q * HP:(q + 1) * HP].rearrange("p (g j) -> p g j", j=HJ),
                                    float(v), None, ALU.is_equal)
                for v in range(HL):
                    last = V.tensor_scalar(hot_lo[q % 2][:, v, :], lo16[:, q * HP:(q + 1) * HP], float(v), None, ALU.is_equal)
                last.then_inc(s_hot, 1)

            def statistics(t, s_stat):
                V.bn_stats(stats[:, DS(t, 1), :].rearrange("p a s -> p (a s)"),
                           x_sb[:, DS(t, 1), :].rearrange("p a f -> p (a f)")).then_inc(s_stat, 1)

            def moments(s_stat, s_moment, scale):
                dve.wait_ge(s_stat, NT)
                link(V.tensor_tensor(mean[:, :], stats[:, :, 1], stats[:, :, 4], ALU.add))
                link(V.tensor_tensor(var[:, :], stats[:, :, 1], stats[:, :, 4], ALU.subtract))
                link(V.tensor_tensor(var[:, :], var[:, :], var[:, :], ALU.mult))
                link(V.tensor_tensor(shift[:, :], stats[:, :, 2], stats[:, :, 5], ALU.add))
                link(V.scalar_tensor_tensor(var[:, :], var[:, :], F / 4, shift[:, :], ALU.mult, ALU.add))
                V.tensor_scalar(mean[:, :], mean[:, :], -0.5 * scale, None, ALU.mult).then_inc(s_moment, 1)

            def factors(s_stat, s_root, scale):
                dve.wait_ge(s_root, 1)
                link(V.reciprocal(rstd[:, :], var[:, :]))
                link(V.tensor_tensor(shift[:, :], mean[:, :], rstd[:, :], ALU.mult))
                V.tensor_scalar(rstd[:, :], rstd[:, :], scale, None, ALU.mult).then_inc(s_stat, 1)

            def offsets():
                dve.wait_ge(s_hist, PIECES)
                after(V.tensor_reduce(same[:, :], cube[:, :, :].rearrange("p v j -> p j v"), AX.X, ALU.add))
                link(V.tensor_reduce(fold[:, :], cube[:, :, :], AX.X, ALU.add))
                link(V.tensor_tensor(crossed[:, :, :], psH.rearrange("p (j l) -> p j l", j=HJ),
                                     same[:, :].rearrange("p (j a) -> p j a", a=1).to_broadcast([HJ * HH, HJ, HL]), ALU.mult))
                link(V.tensor_reduce(diag[:, :], crossed[:, :, :].rearrange("p j l -> p l j"), AX.X, ALU.add))
                mark().then_inc(s_diag, 1)
                dve.wait_ge(s_folded, 1)
                link(V.tensor_copy(cnt[:, :], psC))
                after(V.tensor_reduce(most[:, :], cnt[:, :], AX.X, ALU.max))
                link(V.tensor_tensor_scan(incl[:, :], cnt[:, :], cnt[:, :], 0.0, ALU.add, ALU.bypass))
                mark().then_inc(s_cnt, 1)
                dve.wait_ge(s_base, 1)
                link(V.tensor_tensor(offf[:, :], incl[:, :], cnt[:, :], ALU.subtract))
                V.tensor_scalar(offi[:, :], offf[:, :], psO, None, ALU.add).then_inc(s_offi, 1)
                link(V.tensor_reduce(rnd[:, 0:1], psM, AX.X, ALU.max))
                link(V.tensor_scalar(rnd[:, 1:2], rnd[:, 0:1], WIN - 1, None, ALU.add))
                V.tensor_scalar(rnd[:, 4:5], rnd[:, 1:2], 8, None, ALU.logical_shift_right).then_inc(s_rounds, 1)

            digits_hot(0)
            digits_hot(1)

            state = [0]

            def exchange(source, sz, k, both, other=None):
                join()
                target = keys[1 - state[0]]
                if both:
                    i, o = (a.rearrange("p (m d q w k) -> p m d q w k", d=2, q=sz // (2 * k), w=2, k=k)
                            for a in (source, target[:, :]))
                    for d in range(2):
                        a, b = i[:, :, d, :, 0, :], i[:, :, d, :, 1, :]
                        after(V.tensor_tensor(o[:, :, d, :, 0, :], a, b, ALU.max if d else ALU.min))
                        after(V.tensor_tensor(o[:, :, d, :, 1, :], a, b, ALU.min if d else ALU.max))
                else:
                    i, o = (a.rearrange("p (q w k) -> p q w k", w=2, k=k) for a in (source, target[:, :]))
                    a, b = i[:, :, 0, :], i[:, :, 1, :]
                    if other is not None:
                        b = other.rearrange("p (q k) -> p q k", k=k)
                    after(V.tensor_tensor(o[:, :, 0, :], a, b, ALU.min))
                    after(V.tensor_tensor(o[:, :, 1, :], a, b, ALU.max))
                state[0] = 1 - state[0]

            def now():
                return keys[state[0]][:, :]

            def halves_exchange(k, s_done, source=None, other=None, ready=None, finished=None):
                H = C // 2
                begin = state[0]
                for h in range(2):
                    if ready:
                        ready(h)
                    at, dist = begin, k
                    while dist:
                        join()
                        ps_in = dist == k and source is not None
                        i = (source if ps_in else keys[at])[:, h * H:(h + 1) * H].rearrange("p (q w k) -> p q w k", w=2, k=dist)
                        o = keys[1 - at][:, h * H:(h + 1) * H].rearrange("p (q w k) -> p q w k", w=2, k=dist)
                        a, b = i[:, :, 0, :], i[:, :, 1, :]
                        if ps_in:
                            b = other[:, h * H // 2:(h + 1) * H // 2].rearrange("p (q k) -> p q k", k=dist)
                        after(V.tensor_tensor(o[:, :, 0, :], a, b, ALU.min))
                        after(V.tensor_tensor(o[:, :, 1, :], a, b, ALU.max))
                        at, dist = 1 - at, dist // 2
                    join()
                    if finished:
                        finished(h, keys[at], keys[1 - at])
                    else:
                        mark().then_inc(s_done, 1)
                state[0] = at

            def list_half(h, a, b):
                cols = slice(h * C // 2, (h + 1) * C // 2)
                dve.wait_ge(s_sq, 4 * X + 3)
                link(V.tensor_scalar(b[:, cols].bitcast(i32), a[:, cols].bitcast(i32), 7, None, ALU.logical_shift_right))
                V.tensor_copy(listed[:, cols, 0], b[:, cols].bitcast(i32)).then_inc(s_listed, 1)
                link(V.tensor_scalar(a[:, cols].bitcast(i32), a[:, cols].bitcast(i32), 127, None, ALU.bitwise_and))
                V.tensor_copy(listed[:, cols, 1], a[:, cols].bitcast(i32)).then_inc(s_listed, 1)

            sz = 2
            while sz < C:
                k = sz // 2
                while k:
                    exchange(now(), sz, k, True)
                    k //= 2
                if sz == 16:
                    digits_hot(2)
                elif sz == 32:
                    dve.wait_ge(s_x, 16)
                    with dve.Fori(0, NT - 9, 10) as t:
                        for u in range(10):
                            statistics(t + u, s_ln)
                    moments(s_ln, s_var, UP)
                elif sz == 64:
                    digits_hot(3)
                    factors(s_ln, s_std, UP)
                elif sz == 256:
                    offsets()
                sz *= 2
            exchange(now(), C, C // 2, False)
            halves_exchange(C // 4, s_rows)
            for lv in range(1, LEVELS + 1):
                kept.append(state[0])
                if lv == 2:
                    dve.wait_ge(s_offrow, 16)
                    V.tensor_scalar(offrow[:, :], offrow[:, :], LAST_START, None, ALU.min).then_inc(s_offnew, 1)

                def turned(h):
                    dve.wait_ge(s_T, 4 * (lv - 1) + 2 * h + 2)
                    dve.wait_ge(s_Tup, 4 * (lv - 1) + 2 * h + 2)

                halves_exchange(2 ** (lv - 1), s_Tdone, psT, upper, turned)
                kept2.append(state[0])
                dve.wait_ge(s_R, 4 * lv)
                dve.wait_ge(s_Rup, 2 * lv)
                exchange(psR, C, C // 2, False, upper)
                halves_exchange(C // 4, s_rows, finished=list_half if lv == LEVELS else None)
            dve.wait_ge(s_lnE, NT)
            link(V.memset(xnT[:, :, N:], 0.0))

            dve.wait_ge(s_rounds, 1)
            rounds = dve.value_load(rnd[0:1, 4:5], min_val=1, max_val=E // WIN + 1)

            dve.sem_inc(s_oh, GU)
            dve.wait_ge(s_list, 32)
            dve.wait_ge(s_firsts, 1)

            def onehots(r, S, G):
                g = S * (NT // GU) + G
                for u in range(GU):
                    dve.wait_ge(s_win[u], (r * (NB // GU) + g) * 16 + 16)
                    dve.wait_ge(s_built, r * NB + g * GU + u + 1)
                    for k in range(K):
                        V.tensor_scalar(ohd[:, u % OR, k, :], places[:, 0:128], win[:, u, k, 1:2], None, ALU.is_equal)
                    for k in range(K):
                        last = V.tensor_scalar(ohs[:, u % OR, k, :], places[:, :], firsts[:, DS(g * GU + u, 1)],
                                               win[:, u, k, 0:1], ALU.add, ALU.is_equal)
                    last.then_inc(s_oh, 1)

            def block_sums(r, S, bank):
                dve.wait_ge(s_main, r * NB + S * NT + NT + AR)
                V.scalar_tensor_tensor(xnT[:, :, DS(S * BN, BN)], ps[:, bank:bank + 2, 0:BN], 1.0 / UP,
                                       xnT[:, :, DS(S * BN, BN)], ALU.mult, ALU.add).then_inc(s_agg, 1)

            def block_after(r, S, bank):
                onehots(r, S, 0)
                block_sums(r, S - 1, bank)
                with dve.Fori(1, NT // GU) as G:
                    onehots(r, S, G)

            with dve.Fori(0, rounds) as r:
                with dve.Fori(0, NT // GU) as G:
                    onehots(r, 0, G)
                with dve.Fori(1, NS - 2, 2) as S:
                    block_after(r, S, 2)
                    block_after(r, S + 1, 4)
                block_after(r, NS - 1, 2)
                block_sums(r, NS - 1, 4)
                dve.wait_ge(s_round, r + 1)
                V.tensor_scalar(offrow[:, :], offrow[:, :], WIN, LAST_START, ALU.add, ALU.min).then_inc(s_offnew, 1)

            dve.wait_ge(s_w1T, 1)
            for a in range(HID // 128):
                last = V.tensor_copy(w1T[:, a, :], ps[:, 4 + a // 2, (a % 2) * 256:(a % 2) * 256 + 256])
            last.then_inc(s_w1Te, 1)
            dve.wait_ge(s_wf, 1)
            V.tensor_copy(wf[:, :, :], ps[:, 6, :].rearrange("p (a f) -> p a f", a=FH)).then_inc(s_wfe, 1)
            V.tensor_copy(biasb, ps[0:NP, 7, 0:F]).then_inc(s_bias, 1)

            def residual(t, u, first=False):
                dve.wait_ge(s_lin, t + 1)
                dve.wait_ge(s_pre, t + 1)
                if not first:
                    dve.wait_ge(s_x1, t)
                V.tensor_tensor(x_sb[:, DS(t, 1), :].rearrange("p a f -> p (a f)"), ps[0:NP, u, 0:F],
                                x_sb[:, DS(t, 1), :].rearrange("p a f -> p (a f)"), ALU.add).then_inc(s_x1, 1)
                if not first:
                    statistics(t - 1, s_ln2)

            residual(0, 0, True)
            residual(1, 1)
            with dve.Fori(2, NT - 1, 2) as t:
                for u in range(2):
                    residual(t + u, u)
            dve.wait_ge(s_x1, NT)
            statistics(NT - 1, s_ln2)
            moments(s_ln2, s_var2, 1.0)
            factors(s_ln2, s_std2, 1.0)

            def evacuate(t, u, first=False):
                dve.wait_ge(s_ynT, t + 1)
                if not first:
                    dve.wait_ge(s_lg, t - len(GB) + 1)
                V.tensor_copy(ynT[u], ps[:, GB[u], 0:FH * NP].rearrange("p (a n) -> p a n", a=FH)).then_inc(s_ynE, 1)

            for t in range(len(GB)):
                evacuate(t, t, True)
            with dve.Fori(len(GB), NT - len(GB) + 1, len(GB)) as t:
                for u in range(len(GB)):
                    evacuate(t + u, u)

            dve.wait_ge(s_lg, NT)
            dve.wait_ge(s_con2, 4)
            dve.wait_ge(s_gw, 32)

            def over_tiles(a, n):
                return a.rearrange("p (t e) -> p t e", t=1).to_broadcast([NP, n, X])

            def over_experts(a):
                return a.rearrange("p (t e) -> p t e", e=1).to_broadcast([NP, NT, X])

            after(V.tensor_tensor(logits[:, 0:32, :], ps[0:NP, 2, :].rearrange("p (t e) -> p t e", e=X), over_tiles(gb[:, :], 32), ALU.add))
            link(V.tensor_tensor(logits[:, 32:, :], ps[0:NP, 3, 0:(NT - 32) * X].rearrange("p (t e) -> p t e", e=X), over_tiles(gb[:, :], NT - 32), ALU.add))
            values = logits
            for k in range(2):
                one = chosen[:, :, k * NT:(k + 1) * NT].rearrange("p e t -> p t e")
                link(V.tensor_reduce(best[:, k, :], values, AX.X, ALU.max))
                link(V.tensor_tensor(one, values, over_experts(best[:, k, :]), ALU.is_equal))
                link(V.scalar_tensor_tensor(one, one, -64.0, over_tiles(eix64[:, :], NT), ALU.mult, ALU.add))
                link(V.tensor_reduce(which[:, k, :], one, AX.X, ALU.min))
                link(V.tensor_tensor(one, over_tiles(eix[:, :], NT), over_experts(which[:, k, :]), ALU.is_equal))
                if k == 0:
                    link(V.scalar_tensor_tensor(masked, one, -3.0e38, logits, ALU.mult, ALU.add))
                    values = masked
            V.tensor_tensor(share[:, 1, :], best[:, 1, :], best[:, 0, :], ALU.subtract).then_inc(s_gap, 1)
            V.tensor_copy(chosen16, chosen.rearrange("p e k -> p (e k)")).then_inc(s_chosen, 1)
            dve.wait_ge(s_exp, 1)
            link(V.tensor_scalar(share[:, 0, :], share[:, 1, :], 1.0, None, ALU.add))
            link(V.reciprocal(share[:, 0, :], share[:, 0, :]))
            link(V.tensor_tensor(share[:, 1, :], share[:, 1, :], share[:, 0, :], ALU.mult))

            dve.wait_ge(s_rank, 1)
            link(V.tensor_copy(total.rearrange("p e k -> p (e k)").rearrange("p (b n) -> p b n", b=4), ps[0:NP, 4:8, 0:400]))
            flat = (total.rearrange("p e k -> p (e k)"), upto.rearrange("p e k -> p (e k)"))
            link(V.tensor_tensor_scan(flat[1], flat[0], flat[0], 0.0, ALU.add, ALU.bypass))
            link(V.tensor_tensor(total, upto, total, ALU.subtract))
            link(V.tensor_tensor(padded[:, :], upto[:, :, KT - 1], total[:, :, 0], ALU.subtract))
            link(V.tensor_scalar(nexp[:, :], padded[:, :], 127.0, None, ALU.add))
            link(V.tensor_scalar(nexp[:, :], nexp[:, :], 7, 7, ALU.logical_shift_right, ALU.logical_shift_left))
            link(V.tensor_copy(padded[:, :], nexp[:, :]))
            link(V.tensor_tensor_scan(padend[:, :], padded[:, :], padded[:, :], 0.0, ALU.add, ALU.bypass))
            link(V.tensor_tensor(adjust[:, :], padend[:, :], padded[:, :], ALU.subtract))
            link(V.tensor_tensor(adjust[:, :], adjust[:, :], total[:, :, 0], ALU.subtract))
            link(V.tensor_tensor(place.rearrange("p e k -> p (e k)").rearrange("p (b n) -> p b n", b=4), ps[0:NP, 0:4, 0:400],
                                 total.rearrange("p e k -> p (e k)").rearrange("p (b n) -> p b n", b=4), ALU.add))
            link(V.tensor_tensor(place, place, adjust[:, :].rearrange("p (e k) -> p e k", k=1).to_broadcast([NP, X, KT]), ALU.add))
            link(V.tensor_tensor(place, place, chosen, ALU.mult))
            link(V.tensor_reduce(posf[:, :], place.rearrange("p e k -> p k e"), AX.X, ALU.add))
            V.tensor_copy(posi[:, :], posf[:, :]).then_inc(s_pos, 1)
            link(V.memset(ones128, 1.0))
            dve.wait_ge(s_sq, 4 * X + 3)
            after(V.tensor_reduce(bound[:, 0:2], squares[:, 0:4 * X].rearrange("p (a n) -> p a n", a=2), AX.X, ALU.add))
            link(V.tensor_copy(bound[:, 2:3], squares[:, 4 * X:]))
            mark().then_inc(s_bound, 1)
            dve.wait_ge(s_erowi, 1)
            link(V.tensor_tensor(reach, started, padend[0:1, :].rearrange("p (j e) -> p j e", j=1).to_broadcast([1, NCH, X]), ALU.is_ge))
            link(V.tensor_reduce(erowf[:, :], reach, AX.X, ALU.add))
            V.tensor_scalar(erow[:, :], erowf[:, :], X - 1, None, ALU.min).then_inc(s_erow, 1)

            dve.wait_ge(s_root, 1)
            link(V.scalar_tensor_tensor(bound[:, 2:3], bound[:, 0:1], 16.5, bound[:, 2:3], ALU.mult, ALU.add))
            link(V.tensor_scalar(bound[:, 0:3], bound[:, 0:3], 1e-20, None, ALU.max))
            link(V.tensor_scalar(expo[:, 0:3], bound[:, 0:3].bitcast(i32), 0x7F800000, None, ALU.bitwise_and))
            link(V.tensor_scalar(up2[:, 0:3].bitcast(i32), expo[:, 0:3], -1.0, 268.0 * 2 ** 23, ALU.mult, ALU.add))
            link(V.tensor_scalar(down2[:, 0:3].bitcast(i32), up2[:, 0:3].bitcast(i32), -1.0, 254.0 * 2 ** 23, ALU.mult, ALU.add))
            link(V.scalar_tensor_tensor(back[:, 0:1], up2[:, 2:3], 1.0 / UP, down2[:, 0:1], ALU.mult, ALU.mult))
            link(V.tensor_tensor(back[:, 1:2], down2[:, 2:3], down2[:, 1:2], ALU.mult))
            dve.wait_ge(s_b1T, 1)
            V.tensor_scalar(b1T, ps[:, 7, 448:448 + X * HA], up2[:, 2:3], None, ALU.mult).then_inc(s_scales, 1)

            dve.sem_inc(s_wlo, 2)

            def low(e, u, pair):
                dve.wait_ge(s_stg[u], pair * 32 + 32)
                for m, (a, b) in enumerate(((0, FH * EH), (FH * EH, WN))):
                    dve.wait_ge(s_whi, 2 * e + m + 1)
                    last = V.scalar_tensor_tensor(wts[:, DS(e, 1), 1, a:b].rearrange("p e n -> p (e n)"), staged[u][:, a:b],
                                                  up2[:, m:m + 1], wts[:, DS(e, 1), 0, a:b].rearrange("p e n -> p (e n)"),
                                                  ALU.mult, ALU.subtract)
                last.then_inc(s_wlo, 1)

            with dve.Fori(0, X // 2) as g:
                for u in range(2):
                    low(g * 2 + u, u, g)

            dve.sem_inc(s_l1, 2 * HA)
            dve.sem_inc(s_eo, LR)
            dve.sem_inc(s_hl, 4)

            def rows_T(j, u):
                dve.wait_ge(s_ct, j + 1 + LR)
                dve.wait_ge(s_l1, (j + 1) * HA)
                V.tensor_scalar(xT[:, u, 0, :, :], ps[:, u, 0:F].rearrange("p (a n) -> p a n", a=FH), UP, None, ALU.mult).then_inc(s_xh, 1)
                dve.wait_ge(s_xh, j + 1)
                V.scalar_tensor_tensor(xT[:, u, 1, :, :], ps[:, u, 0:F].rearrange("p (a n) -> p a n", a=FH), UP,
                                       xT[:, u, 0, :, :], ALU.mult, ALU.subtract).then_inc(s_xl, 1)

            def hidden_low(j, u):
                for m in range(2):
                    part = slice(m * EH // 2, (m + 1) * EH // 2)
                    dve.wait_ge(s_hh, 2 * j + m + 1)
                    V.tensor_tensor(hT[:, u, 1, part], hs[:, u, part], hT[:, u, 0, part], ALU.subtract).then_inc(s_hl, 1)

            def result(j, u, turn, used):
                dve.wait_ge(s_ffn, j + 1 + 2)
                dve.wait_ge(s_wb[u], turn * 16 + 16)
                if used is not None:
                    dve.wait_ge(s_store[u % 2], used * 16)
                V.scalar_tensor_tensor(eo[:, u % 2, :], ps[:, 4 + u % 2, 0:F], back[:, 1:2], wb2[:, u, :],
                                       ALU.mult, ALU.add).then_inc(s_eo, 1)

            rows_T(0, 0)
            rows_T(1, 1)
            hidden_low(0, 0)
            for j in range(LR):
                rows_T(j + 2, j % 2)
                hidden_low(j + 1, (j + 1) % 2)
                result(j, j, 0, j // 2 if j >= 2 else None)
            with dve.Fori(1, (NCH - 2) // LR) as g:
                for u in range(LR):
                    rows_T(g * LR + u + 2, u % 2)
                    hidden_low(g * LR + u + 1, (u + 1) % 2)
                    result(g * LR + u, u, g, g * (LR // 2) + u // 2)
            for j in range((NCH - 2) // LR * LR, NCH):
                if j + 2 < NCH:
                    rows_T(j + 2, j % 2)
                if j + 1 < NCH:
                    hidden_low(j + 1, (j + 1) % 2)
                result(j, j % LR, j // LR, j // 2)

            dve.wait_ge(s_gam, 32)
            def rows(t):
                return yn[:, DS(t, 1), :].rearrange("p a f -> p (a f)")

            def mix(g, h, turn):
                cols = DS(g * GR, GR)
                dve.wait_ge(s_back[h], turn * 32 + 32)
                for u in range(GR):
                    dve.wait_ge(s_got[h * GR + u], turn * 32 + 32)
                    V.scalar_tensor_tensor(rows(g * GR + u), got[h * GR + u][:, 0, :], share[:, 0, DS(g * GR + u, 1)],
                                           rows(g * GR + u), ALU.mult, ALU.add).then_inc(s_y, 1)
                for u in range(GR):
                    dve.wait_ge(s_y, g * 2 * GR + u + 1)
                    V.scalar_tensor_tensor(rows(g * GR + u), got[h * GR + u][:, 1, :], share[:, 1, DS(g * GR + u, 1)],
                                           rows(g * GR + u), ALU.mult, ALU.add).then_inc(s_y, 1)
                dve.wait_ge(s_y, g * 2 * GR + 2 * GR)
                dve.sem_inc(s_started, 1)
                for u in range(GR):
                    V.bn_stats(stats[:, u, :], rows(g * GR + u)).then_inc(s_used, 1)
                dve.wait_ge(s_used, g * GR + GR)
                V.tensor_tensor(mean[:, cols], stats[:, 0:GR, 1], stats[:, 0:GR, 4], ALU.add).then_inc(s_v3, 1)
                V.tensor_tensor(var[:, cols], stats[:, 0:GR, 1], stats[:, 0:GR, 4], ALU.subtract).then_inc(s_v3, 1)
                V.tensor_tensor(shift[:, cols], stats[:, 0:GR, 2], stats[:, 0:GR, 5], ALU.add).then_inc(s_v3, 1)
                dve.wait_ge(s_v3, g * 7 + 2)
                V.tensor_tensor(var[:, cols], var[:, cols], var[:, cols], ALU.mult).then_inc(s_v3, 1)
                dve.wait_ge(s_v3, g * 7 + 4)
                V.scalar_tensor_tensor(var[:, cols], var[:, cols], F / 4, shift[:, cols], ALU.mult, ALU.add).then_inc(s_v3, 1)
                dve.wait_ge(s_std3, g + 1)
                V.reciprocal(rstd[:, cols], var[:, cols]).then_inc(s_v3, 1)
                dve.wait_ge(s_v3, g * 7 + 6)
                V.scalar_tensor_tensor(shift[:, cols], mean[:, cols], -0.5, rstd[:, cols], ALU.mult, ALU.mult).then_inc(s_v3, 1)

            def finish(g):
                dve.wait_ge(s_norm, g * GR + GR)
                five = yn[:, DS(g * GR, GR), :]
                V.tensor_tensor(five, five, gam[:, :].rearrange("p (t f) -> p t f", t=1).to_broadcast([NP, GR, F]),
                                ALU.mult).then_inc(s_sh3, 1)
                dve.wait_ge(s_sh3, g + 1)
                V.tensor_tensor(five, five, x_sb[:, DS(g * GR, GR), :], ALU.add).then_inc(s_fin, 1)

            mix(0, 0, 0)
            mix(1, 1, 0)
            finish(0)
            with dve.Fori(1, NT // GR // 2) as g:
                for h in range(2):
                    mix(g * 2 + h, h, g)
                    finish(g * 2 + (h - 1))
            finish(NT // GR - 1)

        @block.scalar
        def _(act):
            A = nc.scalar
            act.sem_inc(s_sq, 2)
            act.wait_ge(s_var, 1)
            act.wait_ge(s_const, 10)
            A.activation(var[:, :], var[:, :], ACT.Sqrt, bias=eps[0:NP, :], scale=1.0 / F).then_inc(s_std, 1)
            act.wait_ge(s_ln, NT + 1)
            act.wait_ge(s_hist, PIECES)

            def normalise(t, u, first=False):
                if not first:
                    act.wait_ge(s_lnT, t - 1)
                    act.wait_ge(s_lo, t - 1)
                A.activation(xs[:, u, :], x_sb[:, DS(t, 1), :].rearrange("p a f -> p (a f)"), ACT.Identity,
                             bias=shift[:, DS(t, 1)], scale=rstd[:, DS(t, 1)]).then_inc(s_xs, 1)
                act.wait_ge(s_xs, t + 1)
                A.activation(xh[:, DS(t, 1), :].rearrange("p a f -> p (a f)"), xs[:, u, :], ACT.Copy).then_inc(s_hi, 1)
                act.wait_ge(s_lnT, t + 1)
                A.activation(xnT[:, :, DS(t * NP, NP)], ps[:, u, 0:FH * NP].rearrange("p (a n) -> p a n", a=FH),
                             ACT.Copy, scale=1.0 / UP).then_inc(s_lnE, 1)

            for t in range(2):
                normalise(t, t, True)
            with act.Fori(2, EARLY - 1, 2) as t:
                for u in range(2):
                    normalise(t + u, u)
            for lv in range(1, LEVELS + 1):
                a, b = keys[kept[lv - 1]], keys[1 - kept[lv - 1]]
                k = 2 ** (lv - 1)
                for h in range(2):
                    act.wait_ge(s_rows, 2 * (lv - 1) + h + 1)
                    for q in range(2 * h, 2 * h + 2):
                        nc.scalar.activation(b[:, q * 512:(q + 1) * 512], a[:, q * 512:(q + 1) * 512], ACT.Copy,
                                             scale=toggle[:, lv:lv + 1]).then_inc(s_signed, 1)
                    for q in range(2 * h, 2 * h + 2):
                        act.wait_ge(s_T, 4 * (lv - 1) + q + 1)
                        nc.scalar.activation(upper[:, q * 256:(q + 1) * 256].rearrange("p (a k) -> p a k", k=k),
                                             ps[:, q, :].rearrange("p (a w k) -> p a w k", w=2, k=k)[:, :, 1, :],
                                             ACT.Copy).then_inc(s_Tup, 1)
                for q in range(2):
                    act.wait_ge(s_R, 4 * (lv - 1) + q + 3)
                    nc.scalar.activation(upper[:, q * 512:(q + 1) * 512], ps[:, 6 + q, :], ACT.Copy).then_inc(s_Rup, 1)
                for t in later(lv):
                    normalise(t, t % 2)
                first, last, base = [(0, 4, 0), (4, 8, 0), (8, 12, 0), (12, 16, 0), (0, 6, X), (6, 11, X), (11, 16, X)][lv - 1]
                with act.Fori(first, last) as e:
                    for a in range(2):
                        act.wait_ge(s_sqld[a], 16 * (e + base) + 16)
                        A.activation(sqs[a], sqs[a], ACT.Square, accum_out=squares[:, DS(2 * (e + base) + a, 1)]).then_inc(s_sq, 1)
            act.wait_ge(s_sqld[0], 16 * (2 * X + 1))
            A.activation(sqs[0][:, 0:X * HA], sqs[0][:, 0:X * HA], ACT.Square, accum_out=squares[:, 4 * X:]).then_inc(s_sq, 1)

            act.wait_ge(s_rounds, 1)
            rounds = act.value_load(rnd[0:1, 4:5], min_val=1, max_val=E // WIN + 1)
            act.wait_ge(s_list, 32)
            act.dma_start(w1s, W1.rearrange("(a p) n -> p a n", p=128)).then_inc(s_w, 16)
            act.dma_start(w2s, W2.rearrange("(a p) n -> p a n", p=128)).then_inc(s_w, 16)
            with nc.allow_non_contiguous_dma(reason="512 numbers, once"):
                act.dma_start(b1c[:, :], b1.rearrange("(a p) -> p a", p=128)).then_inc(s_w, 16)
            act.dma_start(b2r[:, :], b2.rearrange("(a n) -> a n", a=1)).then_inc(s_w, 16)
            act.sem_inc(s_at, AR)
            with act.Fori(0, rounds) as r:
                with act.Fori(0, NB // GU) as g:
                    n0 = (r * (NB // GU) + g) * GU
                    for u in range(GU):
                        act.wait_ge(s_built, n0 + u + 1 + OR)
                        act.wait_ge(s_main, n0 + u + 1)
                        A.activation(atn[:, u % AR, :], ps[0:NP, u % AR, 0:BN], ACT.Copy).then_inc(s_at, 1)
            act.wait_ge(s_agg, rounds * NS + 2)

            def stage(t, u, first=False):
                if not first:
                    act.wait_ge(s_lin, t - 1)
                A.activation(hst[:, u, :, :], xnT[:, :, DS(t * NP, NP)], ACT.Copy).then_inc(s_hst, 1)

            for t in range(2):
                stage(t, t, True)
            with act.Fori(2, NT - 1, 2) as t:
                for u in range(2):
                    stage(t + u, u)

            act.wait_ge(s_var2, 1)
            A.activation(var[:, :], var[:, :], ACT.Sqrt, bias=eps[0:NP, :], scale=1.0 / F).then_inc(s_std2, 1)
            act.wait_ge(s_ln2, NT + 1)
            with act.Fori(0, NT) as t:
                A.activation(yn[:, DS(t, 1), :].rearrange("p a f -> p (a f)"), x_sb[:, DS(t, 1), :].rearrange("p a f -> p (a f)"),
                             ACT.Identity, bias=shift[:, DS(t, 1)], scale=rstd[:, DS(t, 1)]).then_inc(s_yn, 1)
            act.wait_ge(s_gap, 1)
            A.activation(share[:, 1, :], share[:, 1, :], ACT.Exp).then_inc(s_exp, 1)
            act.wait_ge(s_sum, 1)
            A.activation(bound[:, 0:3], ps[:, 1, 0:3], ACT.Sqrt).then_inc(s_root, 1)
            act.wait_ge(s_scales, 1)

            def high(e, u, pair):
                act.wait_ge(s_stg[u], pair * 32 + 32)
                for m, (a, b) in enumerate(((0, FH * EH), (FH * EH, WN))):
                    A.activation(wts[:, DS(e, 1), 0, a:b].rearrange("p e n -> p (e n)"), staged[u][:, a:b], ACT.Copy,
                                 scale=up2[:, m:m + 1]).then_inc(s_whi, 1)

            with act.Fori(0, X // 2) as g:
                for u in range(2):
                    high(g * 2 + u, u, g)

            def hidden(j, u, e):
                act.wait_ge(s_eo, j + 1)
                act.dma_start(wb2[:, u % LR, :], eb2[DS(e, 1), :].to_broadcast([128, F])).then_inc(s_wb[u % LR], 16)
                act.wait_ge(s_ffn, j + 1)
                for m in range(2):
                    act.wait_ge(s_l1, j * HA + 2 * m + 2 + 2 * HA)
                    act.wait_ge(s_hl, 2 * j + m + 1)
                    for a in range(2 * m, 2 * m + 2):
                        A.activation(hs[:, u % 2, a * 128:(a + 1) * 128], ps[:, 2 + 4 * (u % 2) + m, (a % 2) * 128:(a % 2 + 1) * 128],
                                     ACT.Relu, bias=b1T[:, DS(e * HA + a, 1)], scale=back[:, 0:1]).then_inc(s_hs, 1)
                    part = slice(m * EH // 2, (m + 1) * EH // 2)
                    act.wait_ge(s_hs, 4 * j + 2 * m + 2)
                    A.activation(hT[:, u % 2, 0, part], hs[:, u % 2, part], ACT.Copy).then_inc(s_hh, 1)

            with act.Fori(0, NCH - CU, CU) as j:
                es = experts(j, CU, mybir.EngineType.Activation)
                for u in range(CU):
                    hidden(j + u, u, es[u])
            hidden(NCH - 1, 0, experts(NCH - 1, 1, mybir.EngineType.Activation)[0])

            with act.Fori(0, NT // GR) as g:
                act.wait_ge(s_v3, g * 7 + 5)
                A.activation(var[:, DS(g * GR, GR)], var[:, DS(g * GR, GR)], ACT.Sqrt, bias=eps[0:NP, :], scale=1.0 / F).then_inc(s_std3, 1)
                act.wait_ge(s_v3, g * 7 + 7)
                for u in range(GR):
                    A.activation(yn[:, DS(g * GR + u, 1), :].rearrange("p a f -> p (a f)"), yn[:, DS(g * GR + u, 1), :].rearrange("p a f -> p (a f)"),
                                 ACT.Identity, bias=shift[:, DS(g * GR + u, 1)], scale=rstd[:, DS(g * GR + u, 1)]).then_inc(s_norm, 1)

        @block.tensor
        def _(pe):
            T = nc.tensor
            HG = 10

            def count(q, g, start, stop):
                return T.matmul(psH.rearrange("p (j l) -> p j l", j=HJ),
                                hot_hi[q % 2][:, DS(g, 1), :, :].rearrange("p g v j -> p (g v j)"),
                                hot_lo[q % 2][:, :, DS(g * HJ, HJ)].rearrange("p v j -> p j v"), start=start, stop=stop)

            steps = HP // HJ
            for q in range(PIECES):
                pe.wait_ge(s_hot, q + 1)
                head = HG if q == 0 else 0
                for j in range(head):
                    count(q, j, j == 0, False)
                with pe.Fori(head, steps - 2 * HG + 1, HG) as j0:
                    for j in range(HG):
                        count(q, j0 + j, False, False)
                for j in range(steps - HG, steps):
                    last = count(q, j, False, q == PIECES - 1 and j == steps - 1)
                last.then_inc(s_hist, 1)
            pe.wait_ge(s_const, 10)
            pe.wait_ge(s_diag, 1)
            T.matmul(psC, fold[:, :], diag[:, :], start=True, stop=True).then_inc(s_folded, 1)
            pe.wait_ge(s_cnt, 1)
            T.matmul(psO, before[0:HH, 0:HH], incl[:, HL - 1:HL], start=True, stop=True)
            T.transpose(psM, most[:, :], ident[0:HH, 0:HH]).then_inc(s_base, 1)

            def turn(t, u, first=False):
                pe.wait_ge(s_xs, t + 1)
                if not first:
                    pe.wait_ge(s_lnE, t - 1)
                for a in range(FH):
                    last = T.transpose(ps[:, u, a * NP:(a + 1) * NP], xs[:, u, a * 128:(a + 1) * 128], ident[0:NP, 0:NP])
                last.then_inc(s_lnT, 1)

            for t in range(2):
                turn(t, t, True)
            with pe.Fori(2, EARLY - 1, 2) as t:
                for u in range(2):
                    turn(t + u, u)
            for lv in range(1, LEVELS + 1):
                b = keys[1 - kept[lv - 1]]
                pe.wait_ge(s_lnE, EARLY + sum(len(later(i)) for i in range(1, lv)))
                for q in range(16):
                    if q % 4 == 0:
                        pe.wait_ge(s_signed, 4 * (lv - 1) + q // 4 + 1)
                    t = T.transpose(psT[:, q * 128:(q + 1) * 128], b[:, q * 128:(q + 1) * 128], ident[:, :])
                    if q % 4 == 3:
                        t.then_inc(s_T, 1)
                b = keys[kept2[lv - 1]]
                for q in range(16):
                    if q % 8 == 0:
                        pe.wait_ge(s_Tdone, 2 * (lv - 1) + q // 8 + 1)
                    t = T.transpose(psR[:, q * 128:(q + 1) * 128], b[:, q * 128:(q + 1) * 128], ident[:, :])
                    if q % 4 == 3:
                        t.then_inc(s_R, 1)
                for t in later(lv):
                    turn(t, t % 2)
            pe.wait_ge(s_Tdone, 2 * LEVELS)


            pe.wait_ge(s_lo, NT)
            pe.wait_ge(s_listed, 4)
            pe.wait_ge(s_rounds, 1)
            rounds = pe.value_load(rnd[0:1, 4:5], min_val=1, max_val=E // WIN + 1)
            pe.sem_inc(s_built, OR)
            pe.sem_inc(s_main, AR)
            pe.sem_inc(s_agg, 2)

            def build(n, u):
                pe.wait_ge(s_oh, n + 1 + GU)
                pe.wait_ge(s_at, n + 1)
                for k in range(K):
                    last = T.matmul(ps[0:NP, u % AR, 0:BN], ohd[:, u % OR, k, 0:NP], ohs[:, u % OR, k, :],
                                    start=k == 0, stop=k == K - 1)
                last.then_inc(s_built, 1)

            def add(n, D, u, bank, start, stop):
                pe.wait_ge(s_at, n + 1 + AR)
                for a in range(FH):
                    for h, half in enumerate((xh, xl)):
                        last = T.matmul(ps[:, bank + a, 0:BN],
                                        half[:, DS(D, 1), a * 128:(a + 1) * 128].rearrange("p a f -> p (a f)"),
                                        atn[:, u % AR, :], start=start and h == 0, stop=stop and h == 1)
                last.then_inc(s_main, 1)

            with pe.Fori(0, rounds) as r:
                with pe.Fori(0, NS - 1, 2) as S:
                    for h in range(2):
                        bank = 2 + 2 * h
                        n = r * NB + (S + h) * NT
                        build(n, 0)
                        for u in range(1, GU):
                            build(n + u, u)
                            if u == 1:
                                pe.wait_ge(s_agg, r * NS + S + h + 1)
                            add(n + u - 1, u - 1, u - 1, bank, u == 1, False)
                        with pe.Fori(GU, NT - GU + 1, GU) as D:
                            for u in range(GU):
                                build(n + D + u, u)
                                add(n + D + (u - 1), D + (u - 1), (u - 1) % GU, bank, False, False)
                        add(n + NT - 1, NT - 1, (NT - 1) % GU, bank, False, True)

            pe.wait_ge(s_agg, rounds * NS + 2)
            pe.wait_ge(s_w, 64)
            for a in range(HID // 128):
                for f in range(FH):
                    last = T.transpose(ps[:, 4 + a // 2, (a % 2) * 256 + f * 128:(a % 2) * 256 + (f + 1) * 128],
                                       w1s[:, f, a * 128:(a + 1) * 128], ident[:, :])
            last.then_inc(s_w1T, 1)
            pe.wait_ge(s_w1Te, 1)
            for f in range(FH):
                for a in range(HID // 128):
                    T.matmul(ps[:, 6, f * F:(f + 1) * F], w1T[:, a, f * 128:(f + 1) * 128], w2s[:, a, :],
                             start=a == 0, stop=a == HID // 128 - 1)
            for a in range(HID // 128):
                T.matmul(ps[0:NP, 7, 0:F], b1c[:, a:a + 1].to_broadcast([128, NP]), w2s[:, a, :], start=a == 0, stop=False)
            last = T.matmul(ps[0:NP, 7, 0:F], ones[0:1, 0:NP], b2r[:, :], start=False, stop=True)
            last.then_inc(s_wf, 1)
            pe.wait_ge(s_wfe, 1)

            def linear(t, u, first=False):
                pe.wait_ge(s_hst, t + 1)
                if not first:
                    pe.wait_ge(s_x1, t - 1)
                for a in range(FH):
                    last = T.matmul(ps[0:NP, u, 0:F], hst[:, u, a, :], wf[:, a, :], start=a == 0, stop=a == FH - 1)
                last.then_inc(s_lin, 1)

            for t in range(2):
                linear(t, t, True)
            with pe.Fori(2, NT - 1, 2) as t:
                for u in range(2):
                    linear(t + u, u)

            def gate_T(t, u):
                pe.wait_ge(s_yn, t + 1)
                for a in range(FH):
                    last = T.transpose(ps[:, GB[u], a * NP:(a + 1) * NP],
                                       yn[:, DS(t, 1), a * 128:(a + 1) * 128].rearrange("p a f -> p (a f)"), ident[0:NP, 0:NP])
                last.then_inc(s_ynT, 1)

            def gate(t, u):
                pe.wait_ge(s_ynE, t + 1)
                for a in range(FH):
                    last = T.matmul(ps[0:NP, 2 + t // 32, (t % 32) * X:(t % 32 + 1) * X], ynT[u][:, a, :], gw[:, a, :],
                                    start=a == 0, stop=a == FH - 1)
                last.then_inc(s_lg, 1)

            pe.wait_ge(s_x1, NT)
            pe.wait_ge(s_gw, 32)
            for t in range(NT + 3):
                if t < NT:
                    gate_T(t, t % len(GB))
                if t >= 3:
                    gate(t - 3, (t - 3) % len(GB))

            pe.wait_ge(s_con2, 4)
            pe.wait_ge(s_chosen, 1)
            for b in range(4):
                T.matmul(ps[0:NP, b, 0:400], before16[:, :], chosen16[:, b * 400:(b + 1) * 400], start=True, stop=True)
                last = T.matmul(ps[0:NP, 4 + b, 0:400], ones16[:, :], chosen16[:, b * 400:(b + 1) * 400], start=True, stop=True)
            last.then_inc(s_rank, 1)
            pe.wait_ge(s_b1r, 16)
            pe.wait_ge(s_pos, 1)
            pe.wait_ge(s_bound, 1)
            T.matmul(ps[:, 1, 0:3], ones128, bound[:, 0:3], start=True, stop=True).then_inc(s_sum, 1)
            T.transpose(ps[:, 7, 448:448 + X * HA], b1r, ident[0:X * HA, 0:X * HA]).then_inc(s_b1T, 1)

            pe.wait_ge(s_erow, 1)
            pe.wait_ge(s_wlo, X + 2)
            pe.sem_inc(s_ffn, 2)
            pe.sem_inc(s_ct, LR)

            def chunk_T(u, turn):
                pe.wait_ge(s_xld[u], turn * 16 + 16)
                for a in range(FH):
                    last = T.transpose(ps[:, u % 2, a * 128:(a + 1) * 128], xr[:, u, a * 128:(a + 1) * 128], ident[:, :])
                last.then_inc(s_ct, 1)

            PARTS = ((0, 0), (0, 1), (1, 0))

            def up(j, u, e):
                pe.wait_ge(s_xl, j + 1)
                for m in range(HA):
                    steps = [(a, w, x) for a in range(FH) for w, x in PARTS]
                    for n, (a, w, x) in enumerate(steps):
                        last = T.matmul(ps[:, 2 + 4 * u + m // 2, (m % 2) * 128:(m % 2 + 1) * 128],
                                        wts[:, DS(e, 1), w, a * EH + m * 128:a * EH + (m + 1) * 128].rearrange("p e n -> p (e n)"),
                                        xT[:, u, x, a, :], start=n == 0, stop=n == len(steps) - 1)
                    last.then_inc(s_l1, 1)

            def down(j, u, e):
                pe.wait_ge(s_eo, j + 1 + LR - 2)
                for m in range(HA):
                    if m % 2 == 0:
                        pe.wait_ge(s_hl, 2 * j + m // 2 + 1 + 4)
                    for w, h in PARTS:
                        last = T.matmul(ps[:, 4 + u, 0:F], hT[:, u, h, m * 128:(m + 1) * 128],
                                        wts[:, DS(e, 1), w, FH * EH + m * F:FH * EH + (m + 1) * F].rearrange("p e n -> p (e n)"),
                                        start=m == 0 and w == h == 0, stop=m == HA - 1 and w == 1)
                last.then_inc(s_ffn, 1)

            chunk_T(0, 0)
            chunk_T(1, 0)
            up(0, 0, experts(0, 1, mybir.EngineType.PE)[0])
            with pe.Fori(0, (NCH - 2) // CU) as g:
                es = experts(g * CU, CU + 1, mybir.EngineType.PE)
                for u in range(CU):
                    chunk_T((u + 2) % LR, g * (CU // LR) + (u + 2) // LR)
                    up(g * CU + u + 1, (u + 1) % 2, es[u + 1])
                    down(g * CU + u, u % 2, es[u])
            rest = (NCH - 2) // CU * CU
            es = experts(rest, NCH - rest, mybir.EngineType.PE)
            for j in range(rest, NCH):
                if j + 2 < NCH:
                    chunk_T((j + 2) % LR, (j + 2) // LR)
                if j + 1 < NCH:
                    up(j + 1, (j + 1) % 2, es[j + 1 - rest])
                down(j, j % 2, es[j - rest])


_INS = ['x', 'src', 'dst', 'L0_gnn_W1', 'L0_gnn_b1', 'L0_gnn_W2', 'L0_gnn_b2', 'L0_ffn_gate_w', 'L0_ffn_gate_b',
        'L0_ffn_w1', 'L0_ffn_b1', 'L0_ffn_w2', 'L0_ffn_b2', 'L0_ffn_gamma', 'L0_ffn_beta']
_OUTS = [((6250, 256), 'float32')]


def kernel(**inputs):
    import numpy as _np
    import concourse.bacc as _bacc
    from concourse import mybir as _mybir
    from concourse.bass_utils import run_bass_kernel_spmd as _run
    nc = _bacc.Bacc("TRN2", target_bir_lowering=False, num_devices=1)
    arrays, args, outs = {}, [], []
    for name in _INS:
        a = _np.ascontiguousarray(inputs[name])
        arrays[f"in_{name}_dram"] = a
        args.append(nc.dram_tensor(f"in_{name}_dram", a.shape, _mybir.dt.from_np(a.dtype), kind="ExternalInput").ap())
    for i, (shape, dtype) in enumerate(_OUTS):
        dt = _mybir.dt.from_np(_np.dtype(dtype))
        outs.append(nc.dram_tensor(f"out_{i}_dram", shape, dt, kind="ExternalOutput").ap())
    list_d = nc.dram_tensor("list_d", (262144, 2), _mybir.dt.float32, kind="Internal").ap()
    off_d = nc.dram_tensor("off_d", (1024,), _mybir.dt.int32, kind="Internal").ap()
    slots_d = nc.dram_tensor("slots_d", (113 * 128, 256), _mybir.dt.float32, kind="Internal").ap()
    eo_d = nc.dram_tensor("eo_d", (113 * 128, 256), _mybir.dt.float32, kind="Internal").ap()
    xb_d = nc.dram_tensor("xb_d", (6250, 256), _mybir.dt.float32, kind="Internal").ap()
    yn_d = nc.dram_tensor("yn_d", (6250, 256), _mybir.dt.float32, kind="Internal").ap()
    prog(nc, *args, outs[0], list_d, off_d, slots_d, eo_d, xb_d, yn_d)
    r = _run(nc, [arrays], core_ids=[0])
    return r.results[0]["out_0_dram"]
```
